# Optimizing a Trainium2 kernel written in Bass

```python
import numpy as np
import jax
import jax.numpy as jnp

def _softmax(x, axis=-1):
    return jax.nn.softmax(x, axis=axis)

def _gelu(x):
    return jax.nn.gelu(x, approximate=True)

def _silu(x):
    return jax.nn.silu(x)

def _sigmoid(x):
    return jax.nn.sigmoid(x)

def _layernorm(x, axis=-1, eps=1e-05):
    m = jnp.mean(x, axis=axis, keepdims=True)
    v = jnp.var(x, axis=axis, keepdims=True)
    return (x - m) / jnp.sqrt(v + eps)

def _scatter_add(tgt, idx, src, axis=0):
    return tgt.at[idx].add(src)

def _segment_sum(src, seg, n):
    return jax.ops.segment_sum(src, seg, n)
kernel_name = 'mk_seq_preln_d1_jaxref_r2_7b48f2'

def setup_inputs(seed: int=0):
    np.random.seed(seed)
    _w = jnp.asarray

    def _L0_attn_setup():
        import jax, jax.numpy as jnp
        import numpy as np
        D_MODEL = 512
        D_STATE = 128
        key = jax.random.key(seed)
        ks = jax.random.split(key, 16)
        dm, ds = (D_MODEL, D_STATE)

        def lin(kw, kb, out_f, in_f):
            bound = 1.0 / np.sqrt(in_f)
            W = jax.random.uniform(kw, (out_f, in_f), jnp.float32, -bound, bound)
            b = jax.random.uniform(kb, (out_f,), jnp.float32, -bound, bound)
            return (W, b)
        x = jax.random.normal(ks[0], (8, 1024, dm), jnp.float32)
        A = jax.random.normal(ks[1], (ds, ds), jnp.float32) * 0.05
        B_w, B_b = lin(ks[2], ks[3], ds, dm)
        C_w, C_b = lin(ks[4], ks[5], dm, ds)
        D_w, D_b = lin(ks[6], ks[7], dm, dm)
        s_w1, s_b1 = lin(ks[8], ks[9], dm // 2, dm)
        s_w2, s_b2 = lin(ks[10], ks[11], ds, dm // 2)
        g_w, g_b = lin(ks[12], ks[13], dm, dm)
        return {'x': x, 'A': A, 'B_w': B_w, 'B_b': B_b, 'C_w': C_w, 'C_b': C_b, 'D_w': D_w, 'D_b': D_b, 's_w1': s_w1, 's_b1': s_b1, 's_w2': s_w2, 's_b2': s_b2, 'g_w': g_w, 'g_b': g_b}
    _L0_attn_in = _L0_attn_setup()

    def _L0_ffn_setup():
        import jax, jax.numpy as jnp
        import numpy as np
        B, S, H, E = (2, 4096, 512, 8)
        SCALE = 0.5
        key = jax.random.key(seed)
        k1, k2 = jax.random.split(key)
        x = jax.random.normal(k1, (B, S, H), dtype=jnp.float32)
        gate_w = jax.random.normal(k2, (E, H), dtype=jnp.float32) * 0.02
        coeff = SCALE * (1.0 + 0.05 * jnp.arange(E, dtype=jnp.float32))
        expert_w = coeff[:, None, None] * jnp.eye(H, dtype=jnp.float32)
        return {'x': x, 'gate_w': gate_w, 'expert_w': expert_w}
    _L0_ffn_in = _L0_ffn_setup()
    _d = {'L0_attn_x': _L0_attn_in['x'], 'L0_attn_A': _L0_attn_in['A'], 'L0_attn_B_w': _L0_attn_in['B_w'], 'L0_attn_B_b': _L0_attn_in['B_b'], 'L0_attn_C_w': _L0_attn_in['C_w'], 'L0_attn_C_b': _L0_attn_in['C_b'], 'L0_attn_D_w': _L0_attn_in['D_w'], 'L0_attn_D_b': _L0_attn_in['D_b'], 'L0_attn_s_w1': _L0_attn_in['s_w1'], 'L0_attn_s_b1': _L0_attn_in['s_b1'], 'L0_attn_s_w2': _L0_attn_in['s_w2'], 'L0_attn_s_b2': _L0_attn_in['s_b2'], 'L0_attn_g_w': _L0_attn_in['g_w'], 'L0_attn_g_b': _L0_attn_in['g_b'], 'L0_ffn_gate_w': _L0_ffn_in['gate_w'], 'L0_ffn_expert_w': _L0_ffn_in['expert_w']}
    _x0 = _d['L0_attn_x']
    _d['L0_attn_x'] = jax.random.normal(jax.random.fold_in(jax.random.key(seed), 1), (2, 4096, 512), dtype=_x0.dtype)
    del _x0
    return _d

def reference(L0_attn_x, L0_attn_A, L0_attn_B_w, L0_attn_B_b, L0_attn_C_w, L0_attn_C_b, L0_attn_D_w, L0_attn_D_b, L0_attn_s_w1, L0_attn_s_b1, L0_attn_s_w2, L0_attn_s_b2, L0_attn_g_w, L0_attn_g_b, L0_ffn_gate_w, L0_ffn_expert_w):

    def _L0_attn_ref(x, A, B_w, B_b, C_w, C_b, D_w, D_b, s_w1, s_b1, s_w2, s_b2, g_w, g_b):
        import jax, jax.numpy as jnp
        import numpy as np
        D_MODEL = 512
        D_STATE = 128
        s = jax.nn.sigmoid(jax.nn.silu(jnp.einsum('btd,hd->bth', x, s_w1) + s_b1) @ s_w2.T + s_b2)
        Bt = jnp.einsum('btd,sd->bts', x, B_w) + B_b
        u = Bt * s
        h0 = jnp.zeros((x.shape[0], A.shape[0]), x.dtype)

        def step(h, u_t):
            h = h @ A.T + u_t
            return (h, h)
        _, hs = jax.lax.scan(step, h0, jnp.swapaxes(u, 0, 1))
        hs = jnp.swapaxes(hs, 0, 1)
        y = jnp.einsum('bts,ds->btd', hs, C_w) + C_b + jnp.einsum('btd,ed->bte', x, D_w) + D_b
        gate = jax.nn.sigmoid(jnp.einsum('btd,ed->bte', x, g_w) + g_b)
        return y * gate

    def _L0_ffn_ref(x, gate_w, expert_w):
        import jax, jax.numpy as jnp
        import numpy as np
        B, S, H, E = (2, 4096, 512, 8)
        SCALE = 0.5
        scores = jnp.einsum('bsh,eh->bse', x, gate_w)
        chosen = jnp.argmax(scores, axis=-1)
        onehot = jax.nn.one_hot(chosen, gate_w.shape[0], dtype=x.dtype)
        expert_out = jnp.einsum('bsh,efh->bsef', x, expert_w)
        return x + jnp.einsum('bsef,bse->bsf', expert_out, onehot)
    x = L0_attn_x
    x = x + _L0_attn_ref(_layernorm(x, axis=-1), L0_attn_A, L0_attn_B_w, L0_attn_B_b, L0_attn_C_w, L0_attn_C_b, L0_attn_D_w, L0_attn_D_b, L0_attn_s_w1, L0_attn_s_b1, L0_attn_s_w2, L0_attn_s_b2, L0_attn_g_w, L0_attn_g_b)
    x = x + _L0_ffn_ref(_layernorm(x, axis=-1), L0_ffn_gate_w, L0_ffn_expert_w)
    return x

_drawn_inputs = setup_inputs


def setup_inputs(seed=0):
    import zlib

    import numpy as np

    out = dict(_drawn_inputs(seed))
    spreads = {}
    factors = {'L0_attn_B_b': 8.0,
     'L0_attn_D_b': 4.368,
     'L0_attn_s_w1': 6.165,
     'L0_attn_s_b1': 46.174,
     'L0_attn_s_w2': 6.0,
     'L0_attn_s_b2': 64.0,
     'L0_attn_g_b': 8.0}
    for name, (base, spread) in spreads.items():
        noise = np.random.default_rng([zlib.crc32(name.encode()), seed]).standard_normal(out[name].shape)
        drawn = base * np.exp(spread * noise) if base else spread * noise
        out[name] = jnp.asarray(drawn.astype(out[name].dtype))
    for name, factor in factors.items():
        out[name] = (out[name] * factor).astype(out[name].dtype)
    return out
```

```python
import concourse.bass as bass
from concourse import mybir
from contextlib import ExitStack


def preln_ssm_moe_kernel(nc, x, A, B_w, B_b, C_w, C_b, D_w, D_b, s_w1, s_b1, s_w2, s_b2, g_w, g_b,
                         gate_w, expert_w, out):
    f32, f32r, bf16, i32 = mybir.dt.float32, mybir.dt.float32r, mybir.dt.bfloat16, mybir.dt.int32
    ALU, ACT, AX = mybir.AluOpType, mybir.ActivationFunctionType, mybir.AxisListType

    P = 128
    NB, S, D = x.shape
    NS = A.shape[0]
    DH = s_w1.shape[0]
    E = expert_w.shape[0]
    KD, KH = D // P, DH // P
    EPS = 1e-5
    TB = 512
    SB = TB // NB
    NT = TB // P
    NBLK = NB * S // TB
    LASTB = NBLK - 1
    J = 4
    CH = SB // J
    CW = CH * NB
    EC = (CH + 1) * NB
    KIN = J.bit_length() - 1
    LEVELS = [2 ** i for i in range(CH.bit_length())]
    NSTEP = 1 + KIN + len(LEVELS)
    POWERS = list(range(1, J + 1)) + [J * o for o in LEVELS[1:]]
    RW = D + 4
    MEAN, RSTD, TID = D, D + 1, D + 2
    REG = NB * S + P
    DUMMY = E * REG
    SLOTS = NB * S // P + E - 1
    OOB = NB * S
    RING = 3
    M = 4
    FULL = SLOTS // M
    SC_RANK, SC_COUNT = 2 * NT * E, 4 * NT * E

    x_t = [x[n].rearrange("(b t p) d -> b p t d", t=SB // P, p=P) for n in range(NB)]
    out_rows = out.rearrange("n s d -> (n s) d")
    routed = nc.dram_tensor("routed_rows", (DUMMY + P, RW), f32, kind="Internal").ap()

    def wait(eng, sem, value):
        if not isinstance(value, int) or value > 0:
            eng.wait_ge(sem, value)

    with ExitStack() as keep:
        def psum(name):
            return keep.enter_context(nc.psum_tensor(name, [P, 512], f32))

        def sem(name):
            return keep.enter_context(nc.semaphore(name))

        def kb(name, shape, dt=f32):
            return keep.enter_context(nc.sbuf_tensor(name, shape, dt))

        Y = [psum(f"y{i}") for i in range(NT)]
        G, TP, SA, SC = psum("gates"), psum("turned"), psum("scan"), psum("scores")
        XT_BANKS = [SA, TP, G, SC]

        raw = kb("raw_weights", [P, RING, KD, D])
        ident = kb("ident", [P, P])
        tri, ones = kb("strictly_before", [P, P], bf16), kb("ones", [P, P], bf16)
        run = kb("list_ends", [P, E])
        e_iota = kb("expert_iota", [P, NT, E])
        pad_idx = kb("pad_idx", [P, E], i32)
        padrow = kb("padrow", [P, RW])
        part_id = kb("partition_id_f", [P, 1])
        gate = kb("gate", [P, NT, D])
        xrow = [kb(f"x1_rows{q}", [P, NT, RW]) for q in range(2)]
        xn2 = kb("x1_norm", [P, NT, D])
        x2T = [(kb(f"x1T_hi{q}", [P, KD, P], f32r), kb(f"x1T_lo{q}", [P, KD, P], f32r)) for q in range(2)]
        gateT = kb("gateT", [P, KD, 2, E], f32r)
        ends = kb("chunk_ends", [P, EC])
        endp = kb("chunk_ends_hi", [P, EC], f32r), kb("chunk_ends_lo", [P, EC], f32r)
        st1, st2 = kb("ln1_stats", [P, NT, 6]), kb("ln2_stats", [P, NT, 6])
        mv1, mv2 = kb("ln1_mean_var", [P, NT, 2]), kb("ln2_mean_var", [P, NT, 2])
        ve1, ve2 = kb("ln1_var_eps", [P, NT]), kb("ln2_var_eps", [P, NT])
        rs1, mhalf = kb("ln1_rstd", [P, NT]), kb("minus_half", [P, NT])
        scores = kb("score_sums", [P, NT, E])
        top, best, bounded = kb("top_score", [P, NT]), kb("best", [P, NT]), kb("best_bounded", [P, NT])
        hit, cand = kb("is_top", [P, NT, E]), kb("candidate", [P, NT, E])
        onehot = kb("onehot", [P, NT, E], bf16)
        pos, picked = kb("list_position", [P, NT, E]), kb("picked_position", [P, NT, E])
        dest_f = kb("dest_f", [P, NT])
        dest = [kb(f"dest{q}", [P, NT], i32) for q in range(2)]
        ids = [kb(f"ids{m}", [P, 1], i32) for m in range(M)]
        count, tiles_f, cum, gap = kb("list_count", [1, E]), kb("list_tiles", [1, E]), kb("tiles_upto", [1, E]), kb("list_gap", [1, E])
        tiles_i, tiles_s, zeros = kb("list_tiles_i", [1, E], i32), kb("list_tiles_s", [1, E], i32), kb("zeros_row", [1, E])
        slot_iota = kb("slot_iota", [1, SLOTS])
        past, past_gap = kb("slot_past", [1, SLOTS, E]), kb("slot_past_gap", [1, SLOTS, E])
        slot_e, slot_r, slot_r2 = kb("slot_expert_f", [1, SLOTS]), kb("slot_row_f", [1, SLOTS]), kb("slot_row_sum", [1, SLOTS])
        slot_expert, slot_row = kb("slot_expert", [1, SLOTS], i32), kb("slot_row", [1, SLOTS], i32)
        rows = [xrow[0][:, m, :] for m in range(M)]
        rnorm = [xn2[:, m, :] for m in range(M)]
        res = [gate[:, m, :] for m in range(M)]

        with ExitStack() as main:
            def sb(name, shape, dt=f32):
                return main.enter_context(nc.sbuf_tensor(name, shape, dt))

            def pair(name, shape):
                return sb(name + "_hi", shape, f32r), sb(name + "_lo", shape, f32r)

            DwT, GwT = pair("DwT", [P, KD, D]), pair("GwT", [P, KD, D])
            s1T, s2T = pair("s1T", [P, KD, DH]), pair("s2T", [P, KH, NS])
            BwT, CwT = pair("BwT", [P, KD, NS]), pair("CwT", [P, D])
            AT = pair("A_powers", [P, len(POWERS), NS])
            bias_rows = [sb("y_bias_rows", [P, D], f32r), sb("g_bias_rows", [P, D], f32r)]
            bias_pick = sb("bias_pick", [P, P], f32r)
            b1, b2, bB = sb("s_b1_col", [P, KH]), sb("s_b2_col", [P, 1]), sb("B_b_col", [P, 1])
            xin, xn = sb("x_in", [P, NT, D]), sb("x_norm", [P, NT, D])
            xT = pair("xT", [P, KD, TB])
            silu = sb("silu", [P, KH, TB])
            sT = pair("siluT", [P, KH, TB])
            sel = sb("select", [P, TB])
            z = sb("z", [P, J, CH, NB])
            zp = pair("z", [P, J * CW])
            hT = pair("hT", [P, TB])
        with ExitStack() as later:
            We = [later.enter_context(nc.sbuf_tensor("expert" + h, [P, E, KD, D], f32r)) for h in ("_hi", "_lo")]
        z2 = z[:].rearrange("p j c n -> p (j c n)")
        powT, powP = xn2[:].rearrange("p t d -> p (t d)"), gate[:].rearrange("p t d -> p (t d)")
        bias_y, bias_g, bias_c = xn[:, 0, :], xn[:, 1, :], xn[:, 2, :]
        bias_hi = [sT[0][:, 0, :], sT[0][:, 1, :]]
        raw_C, raw_A, raw_gate = silu[:, 0, :], silu[:, 1, 0:NS], z2[0:E, :]

        S_ = {}
        for name in ("bias_loaded cols_loaded aux_loaded xin_loaded consts_made consts2_made pad_made ident_made "
                     "bias_sum bias_hi bias_split bias_done w_turned w_hi w_lo pow_psum pow_copied pow_hi pow_lo "
                     "stats1 mv1_ready ve1_ready rstd1_ready xn_ready xT_psum xT_hi xT_lo "
                     "s1_psum s1_sig silu_ready silu_hi silu_lo bt_psum s2_psum sel_ready "
                     "scan_psum scan_sum scan_hi scan_lo down_psum h_sum h_hi h_lo carry_ready "
                     "g_psum gate_ready y_psum yg_ready x1_ready "
                     "stats2 mv2_ready ve2_ready rstd2_ready mean_copied xn2_ready x2T_psum x2T_hi x2T_lo "
                     "scores_psum scores_ready top_ready hit_ready cand_ready best_ready bounded_ready onehot_ready "
                     "rank_psum pos_ready picked_ready run_ready destf_ready dest_ready ids_ready pad_idx_ready pad_sent "
                     "expert_turned expert_hi expert_lo table_step slot_iota_made expert_table row_table "
                     "slot_norm slot_turned slot_hi slot_lo slot_psum slot_base slot_ids slot_result").split():
            S_[name] = sem(name)
        raw_loaded = [sem(f"raw_loaded{r}") for r in range(RING)]
        xres_loaded = [sem("xres_loaded_even"), sem("xres_loaded_odd")]
        rows_sent = [sem("rows_sent_even"), sem("rows_sent_odd")]
        row_loaded = [sem(f"row_loaded{m}") for m in range(M)]
        out_sent = [sem(f"out_sent{m}") for m in range(M)]

        def counted_waits(eng, *waits):
            waits = [(sem, v if isinstance(v, int) else eng.to_reg(v)) for sem, v in waits]
            eng.wait_ge(S_["ident_made"], 1)
            for sem, v in waits:
                wait(eng, sem, v)

        def by_block(bank):
            return bank[:].rearrange("p (k t) -> p k t", k=KD)

        def token_order(t):
            return t[:].rearrange("p (n c j) -> p j c n", n=NB, j=J)

        JOBS = []
        for k in range(KD):
            JOBS.append((0, [(raw[:, 0, f, k * P:(k + 1) * P], f * P, P) for f in range(KH)], DH,
                         [h[:, k, :] for h in s1T]))
        JOBS.append((0, [(raw[:, 0, 2, k * P:(k + 1) * P], k * NS, P) for k in range(KD)], KD * NS,
                     [h[:].rearrange("p k n -> p (k n)") for h in BwT]))
        JOBS.append((0, [(raw[:, 0, 3, k * P:(k + 1) * P], k * NS, P) for k in range(KH)], KH * NS,
                     [h[:].rearrange("p k n -> p (k n)") for h in s2T]))
        for r, w in ((1, DwT), (2, GwT)):
            for k in range(KD):
                JOBS.append((r, [(raw[:, r, f, k * P:(k + 1) * P], f * P, P) for f in range(KD)], D,
                             [h[:, k, :] for h in w]))
        JOBS.append((None, [(raw_C[:, f * P:(f + 1) * P], f * P, P) for f in range(KD)], D, [h[:] for h in CwT]))
        JOBS.append((None, [(raw_gate[:, k * P:(k + 1) * P], k * E, E) for k in range(KD)], KD * E,
                     [gateT[:, :, h, :] for h in range(2)]))
        RAW_NEED = [48, 16, 16]
        PREP_BANKS = Y + [G, TP, SA]

        def job_view(j):
            _, _, n, dst = JOBS[j]
            bank = PREP_BANKS[j % len(PREP_BANKS)][:, 0:n]
            return bank.rearrange("p (k e) -> p k e", e=E) if len(dst[0].shape) == 3 else bank

        PK = [1] + [2 ** i for i in range(1, POWERS[-1].bit_length() - 1)]

        def tslot(k):
            i = POWERS.index(k)
            return powT[:, i * NS:(i + 1) * NS]

        def pslot(k):
            i = PK.index(k)
            return raw_A if k == 1 else powP[:, i * NS:(i + 1) * NS]

        ROUNDS = [[("T", 1, 0, 0)], [("T", 2, 1, 1), ("P", 2, 1, 1)],
                  [("T", 3, 1, 2), ("T", 4, 2, 2), ("P", 4, 2, 2)]]
        for k in PK[2:]:
            ROUNDS.append([("T", 2 * k, k, k)] + ([("P", 2 * k, k, k)] if 2 * k in PK else []))

        PREP = []
        for n in range(max(len(JOBS), len(ROUNDS))):
            PREP += [("job", n)] * (n < len(JOBS)) + [("pow", n)] * (n < len(ROUNDS))

        EBANKS = [G, SA] + Y
        NE = E * KD
        E_STEPS = [8, 10, 12, 14, 18, 20, NE]

        block = keep.enter_context(nc.Block())

        @block.sync
        def _(sp):
            def load_x(b):
                wait(sp, S_["xn_ready"], NT * b)
                for n in range(NB):
                    sp.dma_start(xin[:, 2 * n:2 * n + 2, :], x_t[n][b] if isinstance(b, int)
                                 else x_t[n][bass.ds(b, 1)].rearrange("o p t d -> p (o t) d")
                                 ).then_inc(S_["xin_loaded"], 16)

            def load_residual(b, q, turn):
                wait(sp, rows_sent[q], 16 * NT * turn)
                for n in range(NB):
                    sp.dma_start(xrow[q][:, 2 * n:2 * n + 2, 0:D], x_t[n][b] if isinstance(b, int)
                                 else x_t[n][bass.ds(b, 1)].rearrange("o p t d -> p (o t) d")
                                 ).then_inc(xres_loaded[q], 16)

            def load_expert(e):
                sp.dma_start(raw[:, e % RING], expert_w[e].rearrange("(f p) d -> p f d", p=P)
                             ).then_inc(raw_loaded[e % RING], 16)

            sp.dma_start(raw[:, 0, 0:KH], s_w1.rearrange("(f p) d -> p f d", p=P)).then_inc(raw_loaded[0], 16)
            sp.dma_start(raw[:, 0, 2], B_w).then_inc(raw_loaded[0], 16)
            sp.dma_start(raw[:, 0, 3, 0:DH], s_w2).then_inc(raw_loaded[0], 16)
            load_x(0)
            sp.dma_start(raw[:, 1], D_w.rearrange("(f p) d -> p f d", p=P)).then_inc(raw_loaded[1], 16)
            sp.dma_start(raw[:, 2], g_w.rearrange("(f p) d -> p f d", p=P)).then_inc(raw_loaded[2], 16)
            load_residual(0, 0, 0)
            load_x(1)
            load_residual(1, 1, 0)
            load_x(2)
            sp.wait_ge(S_["w_turned"], len(JOBS))
            for e in range(RING):
                load_expert(e)
            with sp.Fori(1, NBLK // 2 - 1) as t:
                load_residual(t * 2, 0, t)
                load_x(t * 2 + 1)
                load_residual(t * 2 + 1, 1, t)
                load_x(t * 2 + 2)
            load_residual(LASTB - 1, 0, NBLK // 2 - 1)
            load_x(LASTB)
            load_residual(LASTB, 1, NBLK // 2 - 1)
            for e in range(RING, E):
                sp.wait_ge(S_["expert_turned"], KD * (e - RING + 1))
                load_expert(e)
            for q in range(2):
                sp.wait_ge(rows_sent[q], 16 * NT * NBLK // 2)
            sp.wait_ge(S_["pad_sent"], 16 * (E + 1))
            sp.wait_ge(S_["row_table"], 1)

            def load_slot(s, m):
                row = sp.value_load(slot_row[0:1, bass.ds(s, 1)], min_val=0, max_val=DUMMY)
                wait(sp, S_["slot_result"], s - M + 1)
                wait(sp, S_["slot_ids"], s - M + 1)
                sp.dma_start(rows[m], routed[bass.ds(row, P), :]).then_inc(row_loaded[m], 16)

            for m in range(M):
                load_slot(m, m)
            with sp.Fori(1, FULL) as u:
                for m in range(M):
                    load_slot(u * M + m, m)
            for s in range(FULL * M, SLOTS):
                load_slot(s, s % M)

        @block.gpsimd
        def _(pool):
            made = [nc.gpsimd.memset(ident[:], 0.0), nc.gpsimd.memset(tri[:], 1.0),
                    nc.gpsimd.memset(ones[:], 1.0), nc.gpsimd.memset(mhalf[:], -0.5),
                    nc.gpsimd.memset(bias_pick[:].bitcast(f32), 0.0), nc.gpsimd.memset(padrow[:], 0.0),
                    nc.gpsimd.memset(xrow[0][:, :, D:RW], 0.0), nc.gpsimd.memset(xrow[1][:, :, D:RW], 0.0),
                    nc.gpsimd.memset(ends[:, 0:NB], 0.0)]
            made += [nc.gpsimd.memset(h[:, 0:NB].bitcast(f32), 0.0) for h in endp]
            for ins in made:
                ins.then_inc(S_["consts_made"], 1)
            pool.wait_ge(S_["consts_made"], len(made))
            nc.gpsimd.affine_select(out=ident[:], in_=ident[:], compare_op=ALU.not_equal, fill=1.0, base=0,
                                    pattern=[[-1, P]], channel_multiplier=1).then_inc(S_["ident_made"], 1)
            nc.gpsimd.affine_select(out=tri[:], in_=tri[:], compare_op=ALU.is_gt, fill=0.0, base=0,
                                    pattern=[[1, P]], channel_multiplier=-1).then_inc(S_["consts2_made"], 1)
            nc.gpsimd.memset(bias_pick[0:2, :].bitcast(f32), 1.0).then_inc(S_["consts2_made"], 1)
            for tile, pattern, mult in ((run[:], [[REG, E]], 0), (e_iota[:], [[0, NT], [1, E]], 0),
                                        (part_id[:], [[0, 1]], 1), (slot_iota[:], [[1, SLOTS]], 0)):
                nc.gpsimd.iota(tile, pattern=pattern, base=0, channel_multiplier=mult,
                               allow_small_or_imprecise_dtypes=True).then_inc(S_["consts2_made"], 1)
            nc.gpsimd.memset(padrow[:].bitcast(i32)[:, TID:TID + 1], OOB).then_inc(S_["pad_made"], 1)
            for q in range(2):
                nc.gpsimd.iota(xrow[q][:].bitcast(i32)[:, :, TID].rearrange("p (n t) -> p n t", n=NB),
                               pattern=[[S, NB], [P, SB // P]], base=(q - 2) * SB,
                               channel_multiplier=1).then_inc(S_["ids_ready"], 1)
            pool.wait_ge(S_["pad_made"], 1)
            pool.dma_start(routed[DUMMY:DUMMY + P, :], padrow[:]).then_inc(S_["pad_sent"], 16)

            def rstd1(b):
                counted_waits(pool, (S_["mv1_ready"], b + 1))
                nc.gpsimd.tensor_scalar(ve1[:], mv1[:, :, 1], EPS, None, ALU.add).then_inc(S_["ve1_ready"], 1)
                pool.wait_ge(S_["ve1_ready"], b + 1)
                wait(pool, S_["xn_ready"], NT * b)
                nc.gpsimd.tensor_tensor(rs1[:], ve1[:], mhalf[:], ALU.pow).then_inc(S_["rstd1_ready"], 1)

            def residual(b, q, turn):
                pool.wait_ge(xres_loaded[q], 16 * NB * (turn + 1))
                for i in range(NT):
                    pool.wait_ge(S_["yg_ready"], NT * b + i + 1)
                    nc.gpsimd.tensor_tensor(xrow[q][:, i, 0:D], xrow[q][:, i, 0:D], gate[:, i, :],
                                            ALU.add).then_inc(S_["x1_ready"], 1)

            def rstd2(b, q):
                row_i = xrow[q][:].bitcast(i32)[:, :, TID]
                counted_waits(pool, (S_["mv2_ready"], b + 1))
                nc.gpsimd.tensor_scalar(ve2[:], mv2[:, :, 1], EPS, None, ALU.add).then_inc(S_["ve2_ready"], 1)
                nc.gpsimd.tensor_copy(xrow[q][:, :, MEAN], mv2[:, :, 0]).then_inc(S_["mean_copied"], 1)
                pool.wait_ge(S_["ve2_ready"], b + 1)
                nc.gpsimd.tensor_tensor(xrow[q][:, :, RSTD], ve2[:], mhalf[:], ALU.pow).then_inc(S_["rstd2_ready"], 1)
                counted_waits(pool, (S_["ids_ready"], b + 2))
                nc.gpsimd.tensor_scalar(row_i, row_i, float(2 * SB), None, ALU.add).then_inc(S_["ids_ready"], 1)

            def scatter(b, q):
                counted_waits(pool, (S_["dest_ready"], b + 1), (S_["rstd2_ready"], b + 1),
                              (S_["mean_copied"], b + 1), (S_["ids_ready"], b + 3))
                for i in range(NT):
                    nc.gpsimd.indirect_dma_start(
                        out=routed, out_offset=bass.IndirectOffsetOnAxis(ap=dest[q][:, i:i + 1], axis=0),
                        in_=xrow[q][:, i, :], in_offset=None).then_inc(rows_sent[q], 16)

            def body(b, q, turn):
                if not (isinstance(b, int) and b == 0):
                    before = turn - (1 - q)
                    residual(b - 1, 1 - q, before)
                    rstd2(b - 1, 1 - q)
                if not (isinstance(b, int) and b == LASTB):
                    rstd1(b + 1)
                if not (isinstance(b, int) and b == 0):
                    scatter(b - 1, 1 - q)

            rstd1(0)
            for b in range(3):
                body(b, b % 2, b // 2)
            with pool.Fori(1, NBLK // 2 - 1) as t:
                body(t * 2 + 1, 1, t)
                body(t * 2 + 2, 0, t + 1)
            body(LASTB, 1, NBLK // 2 - 1)
            residual(LASTB, 1, NBLK // 2 - 1)
            rstd2(LASTB, 1)
            scatter(LASTB, 1)
            pool.wait_ge(S_["pad_idx_ready"], 1)
            for e in range(E):
                nc.gpsimd.indirect_dma_start(
                    out=routed, out_offset=bass.IndirectOffsetOnAxis(ap=pad_idx[:, e:e + 1], axis=0),
                    in_=padrow[:], in_offset=None).then_inc(S_["pad_sent"], 16)

            def slot_base(s, m, turn):
                counted_waits(pool, (row_loaded[m], 16 * (turn + 1)), (out_sent[m], 16 * turn))
                nc.gpsimd.tensor_copy(ids[m][:], rows[m].bitcast(i32)[:, TID:TID + 1]).then_inc(S_["slot_ids"], 1)
                pool.wait_ge(S_["slot_norm"], s + 1)
                nc.gpsimd.tensor_tensor(rows[m][:, 0:D], rows[m][:, 0:D], rnorm[m], ALU.add
                                        ).then_inc(S_["slot_base"], 1)

            def slot_store(s, m):
                counted_waits(pool, (S_["slot_result"], s + 1), (S_["slot_ids"], s + 1))
                nc.gpsimd.indirect_dma_start(
                    out=out_rows, out_offset=bass.IndirectOffsetOnAxis(ap=ids[m][:, 0:1], axis=0),
                    in_=res[m], in_offset=None, bounds_check=OOB - 1, oob_is_err=False
                ).then_inc(out_sent[m], 16)

            def slot(s, m, turn):
                slot_base(s, m, turn)
                if not (isinstance(s, int) and s == 0):
                    slot_store(s - 1, (m - 1) % M)

            for m in range(M):
                slot(m, m, 0)
            with pool.Fori(1, FULL) as u:
                for m in range(M):
                    slot(u * M + m, m, u)
            for s in range(FULL * M, SLOTS):
                slot(s, s % M, FULL)
            slot_store(SLOTS - 1, (SLOTS - 1) % M)
            for m in range(M):
                pool.wait_ge(out_sent[m], 16 * len(range(m, SLOTS, M)))

        @block.scalar
        def _(act):
            act.dma_start(raw_A, A).then_inc(S_["aux_loaded"], 16)
            act.dma_start(bias_y, D_b.partition_broadcast(P)).then_inc(S_["bias_loaded"], 16)
            act.dma_start(bias_g, g_b.partition_broadcast(P)).then_inc(S_["bias_loaded"], 16)
            act.dma_start(bias_c, C_b.partition_broadcast(P)).then_inc(S_["bias_loaded"], 16)
            act.dma_start(raw_C.rearrange("p (f s) -> p f s", f=KD), C_w.rearrange("(f p) s -> p f s", p=P)
                          ).then_inc(S_["aux_loaded"], 16)
            act.dma_start(raw_gate, gate_w).then_inc(S_["aux_loaded"], 16)
            for m in range(KH):
                act.dma_start(b1[:, m:m + 1], s_b1[m * P:(m + 1) * P].unsqueeze(1)).then_inc(S_["cols_loaded"], 16)
            act.dma_start(b2[:], s_b2.unsqueeze(1)).then_inc(S_["cols_loaded"], 16)
            act.dma_start(bB[:], B_b.unsqueeze(1)).then_inc(S_["cols_loaded"], 16)
            copied = 0
            for what, n in PREP:
                if what == "pow":
                    act.wait_ge(S_["pow_psum"], n + 1)
                    for i, (side, k, _, _) in enumerate(ROUNDS[n]):
                        nc.scalar.activation(tslot(k) if side == "T" else pslot(k), SC[:, i * NS:(i + 1) * NS],
                                             ACT.Copy).then_inc(S_["pow_copied"], 1)
                    copied += len(ROUNDS[n])
                else:
                    act.wait_ge(S_["w_turned"], n + 1)
                    nc.scalar.activation(JOBS[n][3][0], job_view(n), ACT.Copy).then_inc(S_["w_hi"], 1)
            act.wait_ge(S_["pow_copied"], copied)
            nc.scalar.activation(AT[0][:].rearrange("p k s -> p (k s)"), powT[:, 0:len(POWERS) * NS],
                                 ACT.Copy).then_inc(S_["pow_hi"], 1)
            act.wait_ge(S_["cols_loaded"], 16 * (KH + 2))

            def tail_hi(b, i):
                act.wait_ge(S_["x2T_psum"], NT * b + i + 1)
                nc.scalar.activation(x2T[i % 2][0][:], by_block(TP), ACT.Copy).then_inc(S_["x2T_hi"], 1)

            def gates(b, i):
                act.wait_ge(S_["g_psum"], NT * b + i + 1)
                wait(act, S_["x1_ready"], NT * (b - 1) + i + 1)
                nc.scalar.activation(gate[:, i, :], G[:], ACT.Sigmoid).then_inc(S_["gate_ready"], 1)

            def body(b):
                tail = not (isinstance(b, int) and b == 0)
                for i in range(NT):
                    act.wait_ge(S_["xT_psum"], NT * b + i + 1)
                    nc.scalar.activation(xT[0][:, :, i * P:(i + 1) * P], by_block(XT_BANKS[i]), ACT.Copy
                                         ).then_inc(S_["xT_hi"], 1)
                for m in range(KH):
                    act.wait_ge(S_["s1_psum"], KH * b + m + 1)
                    wait(act, S_["silu_lo"], KH * (b - 1) + m + 1)
                    nc.scalar.activation(silu[:, m, :], (G, TP)[m][:], ACT.Sigmoid, bias=b1[:, m:m + 1]
                                         ).then_inc(S_["s1_sig"], 1)
                    act.wait_ge(S_["silu_ready"], KH * b + m + 1)
                    nc.scalar.activation(sT[0][:, m, :], silu[:, m, :], ACT.Copy).then_inc(S_["silu_hi"], 1)
                act.wait_ge(S_["s2_psum"], b + 1)
                nc.scalar.activation(sel[:], SC[:], ACT.Sigmoid, bias=b2[:]).then_inc(S_["sel_ready"], 1)
                gates(b, 0)
                if tail:
                    tail_hi(b - 1, 0)
                    tail_hi(b - 1, 1)
                gates(b, 1)
                if tail:
                    tail_hi(b - 1, 2)
                    tail_hi(b - 1, 3)
                gates(b, 2)
                act.wait_ge(S_["h_sum"], b + 1)
                nc.scalar.activation(token_order(hT[0]), z[:], ACT.Copy).then_inc(S_["h_hi"], 1)
                gates(b, 3)

            body(0)
            body(1)
            with act.Fori(2, NBLK) as b:
                body(b)

            def experts(first, end):
                for n in range(first, end):
                    act.wait_ge(S_["expert_turned"], n + 1)
                    nc.scalar.activation(We[0][:, n // KD, n % KD, :], EBANKS[n % 6][:], ACT.Copy
                                         ).then_inc(S_["expert_hi"], 1)

            experts(0, E_STEPS[0])
            for i in range(NT):
                tail_hi(LASTB, i)
                experts(E_STEPS[i], E_STEPS[i + 1])
            experts(E_STEPS[NT], NE)

            def slot_hi(s, q):
                act.wait_ge(S_["slot_turned"], s + 1)
                wait(act, S_["slot_psum"], s - 1)
                nc.scalar.activation(x2T[q][0][:], by_block((TP, SC)[q]), ACT.Copy).then_inc(S_["slot_hi"], 1)

            for s in range(M):
                slot_hi(s, s % 2)
            with act.Fori(1, FULL) as u:
                for m in range(M):
                    slot_hi(u * M + m, m % 2)
            for s in range(FULL * M, SLOTS):
                slot_hi(s, s % 2)

        @block.vector
        def _(dve):
            def ln1_stats(b, i):
                if i == 0:
                    dve.wait_ge(S_["xin_loaded"], 16 * NB * (b + 1))
                nc.vector.bn_stats(st1[:, i, :], xin[:, i, :]).then_inc(S_["stats1"], 1)

            def ln1_mv(b):
                counted_waits(dve, (S_["stats1"], NT * (b + 1)), (S_["rstd1_ready"], b))
                for i in range(NT):
                    ins = nc.vector.bn_aggr(mv1[:, i, :], st1[:, i, :])
                ins.then_inc(S_["mv1_ready"], 1)

            def normalise1(b):
                dve.wait_ge(S_["rstd1_ready"], b + 1)
                dve.wait_ge(S_["mv1_ready"], b + 1)
                wait(dve, S_["xT_psum"], NT * b)
                for i in range(NT):
                    nc.vector.tensor_scalar(xn[:, i, :], xin[:, i, :], mv1[:, i, 0:1], rs1[:, i:i + 1],
                                            ALU.subtract, ALU.mult).then_inc(S_["xn_ready"], 1)

            dve.wait_ge(S_["bias_loaded"], 48)
            nc.vector.tensor_tensor(bias_y, bias_y, bias_c, ALU.add).then_inc(S_["bias_sum"], 1)
            dve.wait_ge(S_["bias_sum"], 1)
            for hi, src in zip(bias_hi, (bias_y, bias_g)):
                nc.vector.tensor_copy(hi, src).then_inc(S_["bias_hi"], 1)
            dve.wait_ge(S_["bias_hi"], 2)
            for dst, hi, src in zip(bias_rows, bias_hi, (bias_y, bias_g)):
                nc.vector.tensor_tensor(dst[:], src, hi.bitcast(f32), ALU.subtract).then_inc(S_["bias_split"], 1)
            dve.wait_ge(S_["bias_split"], 2)
            for dst, hi in zip(bias_rows, bias_hi):
                nc.vector.tensor_copy(dst[0:1, :], hi[0:1, :].bitcast(f32)).then_inc(S_["bias_done"], 1)
            for i in range(NT):
                ln1_stats(0, i)
            ln1_mv(0)
            for j, (_, _, _, dst) in enumerate(JOBS):
                dve.wait_ge(S_["w_hi"], j + 1)
                nc.vector.tensor_tensor(dst[1], job_view(j), dst[0].bitcast(f32), ALU.subtract).then_inc(S_["w_lo"], 1)
                if j == len(JOBS) // 2:
                    normalise1(0)
            dve.wait_ge(S_["pow_hi"], 1)
            nc.vector.tensor_tensor(AT[1][:].rearrange("p k s -> p (k s)"), powT[:, 0:len(POWERS) * NS],
                                    AT[0][:].rearrange("p k s -> p (k s)").bitcast(f32),
                                    ALU.subtract).then_inc(S_["pow_lo"], 1)

            def split(hi, lo, src, n):
                dve.wait_ge(S_["scan_sum"], n)
                nc.vector.tensor_copy(hi, src).then_inc(S_["scan_hi"], 1)
                dve.wait_ge(S_["scan_hi"], n)
                nc.vector.tensor_tensor(lo, src, hi.bitcast(f32), ALU.subtract).then_inc(S_["scan_lo"], 1)

            def inside(b, k):
                n = NSTEP * b + 2 + k
                o = 2 ** k * CW
                dve.wait_ge(S_["scan_psum"], (NSTEP - 1) * b + k + 1)
                nc.vector.tensor_tensor(z2[:, o:], SA[:, o:], z2[:, o:], ALU.add).then_inc(S_["scan_sum"], 1)
                if k < KIN - 1:
                    split(zp[0][:, o:], zp[1][:, o:], z2[:, o:], n)
                else:
                    split(endp[0][:, NB:], endp[1][:, NB:], z2[:, (J - 1) * CW:], n)
                    nc.vector.tensor_copy(ends[:, NB:], z2[:, (J - 1) * CW:]).then_inc(S_["carry_ready"], 1)

            def over(b, l):
                n = NSTEP * b + 2 + KIN + l
                o = LEVELS[l] * NB
                dve.wait_ge(S_["scan_psum"], (NSTEP - 1) * b + KIN + l + 1)
                if l == 0:
                    dve.wait_ge(S_["carry_ready"], 3 * b + 1)
                nc.vector.tensor_tensor(ends[:, o:], SA[:, o:EC], ends[:, o:], ALU.add).then_inc(S_["scan_sum"], 1)
                split(endp[0][:, o:], endp[1][:, o:], ends[:, o:], n)

            def gated(b):
                for i in range(NT):
                    dve.wait_ge(S_["y_psum"], NT * b + i + 1)
                    dve.wait_ge(S_["gate_ready"], NT * b + i + 1)
                    nc.vector.tensor_tensor(gate[:, i, :], Y[i][:], gate[:, i, :], ALU.mult
                                            ).then_inc(S_["yg_ready"], 1)

            def ln2_stats(b, q, i):
                dve.wait_ge(S_["x1_ready"], NT * b + i + 1)
                nc.vector.bn_stats(st2[:, i, :], xrow[q][:, i, 0:D]).then_inc(S_["stats2"], 1)

            def ln2_mv(b):
                counted_waits(dve, (S_["stats2"], NT * (b + 1)), (S_["rstd2_ready"], b), (S_["mean_copied"], b))
                for i in range(NT):
                    ins = nc.vector.bn_aggr(mv2[:, i, :], st2[:, i, :])
                ins.then_inc(S_["mv2_ready"], 1)

            def normalise2(b, q):
                dve.wait_ge(S_["rstd2_ready"], b + 1)
                dve.wait_ge(S_["mean_copied"], b + 1)
                wait(dve, S_["x2T_psum"], NT * b)
                for i in range(NT):
                    nc.vector.tensor_scalar(xn2[:, i, :], xrow[q][:, i, 0:D], xrow[q][:, i, MEAN:MEAN + 1],
                                            xrow[q][:, i, RSTD:RSTD + 1], ALU.subtract, ALU.mult
                                            ).then_inc(S_["xn2_ready"], 1)

            def tail_lo(b, i):
                dve.wait_ge(S_["x2T_hi"], NT * b + i + 1)
                hi, lo = x2T[i % 2]
                nc.vector.tensor_tensor(lo[:], by_block(TP), hi[:].bitcast(f32), ALU.subtract).then_inc(S_["x2T_lo"], 1)

            def choose(b):
                dve.wait_ge(S_["scores_psum"], b + 1)
                nc.vector.tensor_reduce(scores[:], SC[:, 0:SC_RANK].rearrange("p (t h e) -> p t e h", h=2, e=E),
                                        AX.X, ALU.add).then_inc(S_["scores_ready"], 1)
                dve.wait_ge(S_["scores_ready"], b + 1)
                nc.vector.tensor_reduce(top[:], scores[:], AX.X, ALU.max).then_inc(S_["top_ready"], 1)
                dve.wait_ge(S_["top_ready"], b + 1)
                nc.vector.tensor_tensor(hit[:], scores[:], top[:].unsqueeze(2).to_broadcast([P, NT, E]), ALU.is_ge
                                        ).then_inc(S_["hit_ready"], 1)
                dve.wait_ge(S_["hit_ready"], b + 1)
                nc.vector.scalar_tensor_tensor(cand[:], hit[:], -float(E), e_iota[:], ALU.mult, ALU.add
                                               ).then_inc(S_["cand_ready"], 1)
                dve.wait_ge(S_["cand_ready"], b + 1)
                nc.vector.tensor_reduce(best[:], cand[:], AX.X, ALU.min).then_inc(S_["best_ready"], 1)
                dve.wait_ge(S_["best_ready"], b + 1)
                nc.vector.tensor_scalar(bounded[:], best[:], -1.0, float(E), ALU.min, ALU.add
                                        ).then_inc(S_["bounded_ready"], 1)
                dve.wait_ge(S_["bounded_ready"], b + 1)
                nc.vector.tensor_tensor(onehot[:], e_iota[:], bounded[:].unsqueeze(2).to_broadcast([P, NT, E]),
                                        ALU.is_equal).then_inc(S_["onehot_ready"], 1)

            def place(b, q, turn):
                ranks = SC[:, SC_RANK:SC_RANK + NT * E].rearrange("p (t e) -> p t e", e=E)
                dve.wait_ge(S_["rank_psum"], b + 1)
                wait(dve, S_["run_ready"], b)
                nc.vector.tensor_tensor(pos[:], ranks, run[:].unsqueeze(1).to_broadcast([P, NT, E]), ALU.add
                                        ).then_inc(S_["pos_ready"], 1)
                dve.wait_ge(S_["pos_ready"], b + 1)
                nc.vector.tensor_tensor(picked[:], pos[:], onehot[:], ALU.mult).then_inc(S_["picked_ready"], 1)
                nc.vector.tensor_tensor(run[:], SC[:, SC_COUNT:SC_COUNT + E], run[:], ALU.add
                                        ).then_inc(S_["run_ready"], 1)
                dve.wait_ge(S_["picked_ready"], b + 1)
                nc.vector.tensor_reduce(dest_f[:], picked[:], AX.X, ALU.add).then_inc(S_["destf_ready"], 1)
                dve.wait_ge(S_["destf_ready"], b + 1)
                wait(dve, rows_sent[q], 16 * NT * turn)
                nc.vector.tensor_copy(dest[q][:], dest_f[:]).then_inc(S_["dest_ready"], 1)

            def body(b, q, turn):
                tail = not (isinstance(b, int) and b == 0)
                ahead = not (isinstance(b, int) and b == LASTB)
                old, oldq, oldturn = b - 1, 1 - q, turn - (1 - q)
                for i in range(NT):
                    dve.wait_ge(S_["xT_hi"], NT * b + i + 1)
                    nc.vector.tensor_tensor(xT[1][:, :, i * P:(i + 1) * P], by_block(XT_BANKS[i]),
                                            xT[0][:, :, i * P:(i + 1) * P].bitcast(f32), ALU.subtract
                                            ).then_inc(S_["xT_lo"], 1)
                if tail:
                    gated(old)
                for m in range(KH):
                    dve.wait_ge(S_["s1_sig"], KH * b + m + 1)
                    nc.vector.scalar_tensor_tensor(silu[:, m, :], (G, TP)[m][:], b1[:, m:m + 1], silu[:, m, :],
                                                   ALU.add, ALU.mult).then_inc(S_["silu_ready"], 1)
                    if tail:
                        ln2_stats(old, oldq, 2 * m)
                    dve.wait_ge(S_["silu_hi"], KH * b + m + 1)
                    nc.vector.tensor_tensor(sT[1][:, m, :], silu[:, m, :], sT[0][:, m, :].bitcast(f32),
                                            ALU.subtract).then_inc(S_["silu_lo"], 1)
                    if tail:
                        ln2_stats(old, oldq, 2 * m + 1)
                if tail:
                    ln2_mv(old)
                    normalise2(old, oldq)
                dve.wait_ge(S_["sel_ready"], b + 1)
                dve.wait_ge(S_["bt_psum"], b + 1)
                for n in range(NB):
                    cols = slice(n * SB, (n + 1) * SB)
                    ins = nc.vector.scalar_tensor_tensor(
                        z[:, :, :, n].rearrange("p j c -> p c j"), SA[:, cols].rearrange("p (c j) -> p c j", j=J),
                        bB[:], sel[:, cols].rearrange("p (c j) -> p c j", j=J), ALU.add, ALU.mult)
                ins.then_inc(S_["scan_sum"], 1)
                split(zp[0][:], zp[1][:], z2, NSTEP * b + 1)
                inside(b, 0)
                inside(b, 1)
                if tail:
                    tail_lo(old, 0)
                over(b, 0)
                if ahead:
                    ln1_stats(b + 1, 0)
                over(b, 1)
                if tail:
                    tail_lo(old, 1)
                over(b, 2)
                if ahead:
                    ln1_stats(b + 1, 1)
                over(b, 3)
                if tail:
                    tail_lo(old, 2)
                over(b, 4)
                if ahead:
                    ln1_stats(b + 1, 2)
                    ln1_stats(b + 1, 3)
                over(b, 5)
                if tail:
                    tail_lo(old, 3)
                if ahead:
                    ln1_mv(b + 1)
                over(b, 6)
                if ahead:
                    normalise1(b + 1)
                dve.wait_ge(S_["down_psum"], b + 1)
                nc.vector.tensor_tensor(z2, SA[:], z2, ALU.add).then_inc(S_["h_sum"], 1)
                if tail:
                    choose(old)
                dve.wait_ge(S_["h_hi"], b + 1)
                nc.vector.tensor_tensor(token_order(hT[1]), z[:], token_order(hT[0]).bitcast(f32), ALU.subtract
                                        ).then_inc(S_["h_lo"], 1)
                nc.vector.tensor_copy(ends[:, 0:NB], ends[:, CH * NB:]).then_inc(S_["carry_ready"], 1)
                for h in endp:
                    ins = nc.vector.tensor_copy(h[:, 0:NB], h[:, CH * NB:].bitcast(f32))
                ins.then_inc(S_["carry_ready"], 1)
                if tail:
                    place(old, oldq, oldturn)

            dve.wait_ge(S_["cols_loaded"], 16 * (KH + 2))
            dve.wait_ge(S_["consts2_made"], 6)
            for b in range(3):
                body(b, b % 2, b // 2)
            with dve.Fori(1, NBLK // 2 - 1) as t:
                body(t * 2 + 1, 1, t)
                body(t * 2 + 2, 0, t + 1)
            body(LASTB, 1, NBLK // 2 - 1)

            def experts(first, end):
                for n in range(first, end):
                    dve.wait_ge(S_["expert_hi"], n + 1)
                    nc.vector.tensor_tensor(We[1][:, n // KD, n % KD, :], EBANKS[n % 6][:],
                                            We[0][:, n // KD, n % KD, :].bitcast(f32), ALU.subtract
                                            ).then_inc(S_["expert_lo"], 1)

            gated(LASTB)
            experts(0, E_STEPS[0])
            for i in range(NT):
                ln2_stats(LASTB, 1, i)
            ln2_mv(LASTB)
            normalise2(LASTB, 1)
            for i in range(NT):
                tail_lo(LASTB, i)
                experts(E_STEPS[i], E_STEPS[i + 1])
            choose(LASTB)
            place(LASTB, 1, NBLK // 2 - 1)
            dve.wait_ge(S_["run_ready"], NBLK)
            nc.vector.tensor_scalar(pad_idx[:], run[:], part_id[:], None, ALU.add).then_inc(S_["pad_idx_ready"], 1)

            steps = [0]

            def then(ins):
                steps[0] += 1
                ins.then_inc(S_["table_step"], 1)
                dve.wait_ge(S_["table_step"], steps[0])

            wide = [1, SLOTS, E]
            then(nc.vector.tensor_scalar(zeros[:], run[0:1, :], 0.0, None, ALU.mult))
            then(nc.vector.scalar_tensor_tensor(count[:], e_iota[0:1, 0, :], -float(REG), run[0:1, :],
                                                ALU.mult, ALU.add))
            then(nc.vector.tensor_scalar(tiles_i[:], count[:], float(P - 1), None, ALU.add))
            then(nc.vector.tensor_scalar(tiles_s[:], tiles_i[:], P.bit_length() - 1, None, ALU.arith_shift_right))
            then(nc.vector.tensor_copy(tiles_f[:], tiles_s[:]))
            then(nc.vector.tensor_tensor_scan(cum[:], tiles_f[:], zeros[:], 0.0, ALU.add, ALU.add))
            then(nc.vector.tensor_scalar(gap[:], tiles_f[:], -float(P), float(REG), ALU.mult, ALU.add))
            then(nc.vector.tensor_tensor(past[:], slot_iota[:].unsqueeze(2).to_broadcast(wide),
                                         cum[:].unsqueeze(1).to_broadcast(wide), ALU.is_ge))
            then(nc.vector.tensor_reduce(slot_e[:], past[:], AX.X, ALU.add))
            nc.vector.tensor_scalar(slot_expert[:], slot_e[:], float(E - 1), float(D * KD), ALU.min, ALU.mult
                                    ).then_inc(S_["expert_table"], 1)
            then(nc.vector.tensor_tensor(past_gap[:], past[:], gap[:].unsqueeze(1).to_broadcast(wide), ALU.mult))
            then(nc.vector.tensor_reduce(slot_r[:], past_gap[:], AX.X, ALU.add))
            then(nc.vector.scalar_tensor_tensor(slot_r2[:], slot_iota[:], float(P), slot_r[:], ALU.mult, ALU.add))
            nc.vector.tensor_scalar(slot_row[:], slot_r2[:], float(DUMMY), None, ALU.min).then_inc(S_["row_table"], 1)
            experts(E_STEPS[NT], NE)

            def slot_norm(s, m, turn):
                dve.wait_ge(row_loaded[m], 16 * (turn + 1))
                wait(dve, S_["slot_turned"], s - M + 1)
                wait(dve, S_["slot_base"], s - M + 1)
                nc.vector.tensor_scalar(rnorm[m], rows[m][:, 0:D], rows[m][:, MEAN:MEAN + 1],
                                        rows[m][:, RSTD:RSTD + 1], ALU.subtract, ALU.mult
                                        ).then_inc(S_["slot_norm"], 1)

            def slot_lo(s, q):
                dve.wait_ge(S_["slot_hi"], s + 1)
                nc.vector.tensor_tensor(x2T[q][1][:], by_block((TP, SC)[q]), x2T[q][0][:].bitcast(f32), ALU.subtract
                                        ).then_inc(S_["slot_lo"], 1)

            def slot_sum(s, m, turn):
                dve.wait_ge(S_["slot_psum"], s + 1)
                dve.wait_ge(S_["slot_base"], s + 1)
                wait(dve, out_sent[m], 16 * turn)
                nc.vector.tensor_tensor(res[m], Y[m % 2][:], rows[m][:, 0:D], ALU.add).then_inc(S_["slot_result"], 1)

            def slot(s, m, turn):
                slot_lo(s, m % 2)
                if not (isinstance(s, int) and s == SLOTS - 1):
                    slot_norm(s + 1, (m + 1) % M, turn + (m + 1) // M)
                if not (isinstance(s, int) and s == 0):
                    slot_sum(s - 1, (m - 1) % M, turn - (m == 0))

            slot_norm(0, 0, 0)
            for s in range(2 * M):
                slot(s, s % M, s // M)
            with dve.Fori(2, FULL) as u:
                for m in range(M):
                    slot(u * M + m, m, u)
            for s in range(FULL * M, SLOTS):
                slot(s, s % M, FULL)
            slot_sum(SLOTS - 1, (SLOTS - 1) % M, (SLOTS - 1) // M)

        @block.tensor
        def _(pe):
            def mm3(dst, left, right, first=True, last=True):
                nc.tensor.matmul(dst, left[0], right[0], start=first, stop=False)
                nc.tensor.matmul(dst, left[0], right[1], start=False, stop=False)
                return nc.tensor.matmul(dst, left[1], right[0], start=False, stop=last)

            pe.wait_ge(S_["ident_made"], 1)
            pe.wait_ge(S_["aux_loaded"], 48)
            copied = 0
            for what, n in PREP:
                if what == "pow":
                    wait(pe, S_["pow_copied"], copied)
                    for i, (side, k, a, m) in enumerate(ROUNDS[n]):
                        dst = SC[:, i * NS:(i + 1) * NS]
                        if a == 0:
                            ins = nc.tensor.transpose(dst, raw_A, ident[:])
                        elif side == "T":
                            ins = nc.tensor.matmul(dst, pslot(a), tslot(m), start=True, stop=True)
                        else:
                            ins = nc.tensor.matmul(dst, tslot(a), pslot(m), start=True, stop=True)
                    ins.then_inc(S_["pow_psum"], 1)
                    copied += len(ROUNDS[n])
                else:
                    r, turns, _, _ = JOBS[n]
                    if r is not None:
                        pe.wait_ge(raw_loaded[r], RAW_NEED[r])
                    if n >= len(PREP_BANKS):
                        pe.wait_ge(S_["w_lo"], n + 1 - len(PREP_BANKS))
                    for src, at, rows_in in turns:
                        ins = nc.tensor.transpose(PREP_BANKS[n % len(PREP_BANKS)][:, at:at + rows_in], src,
                                                  ident[0:rows_in, 0:rows_in])
                    ins.then_inc(S_["w_turned"], 1)
            pe.wait_ge(S_["w_lo"], len(JOBS))
            pe.wait_ge(S_["pow_copied"], copied)
            pe.wait_ge(S_["bias_done"], 2)
            pe.wait_ge(S_["consts2_made"], 6)

            def dense(dst, i, w, bias, part, closed):
                if part == 0:
                    nc.tensor.matmul(dst[:], bias_pick[:], bias[:], start=True, stop=False)
                for k in (0, 1) if part == 0 else (2, 3):
                    ins = mm3(dst[:], [h[:, k, i * P:(i + 1) * P] for h in xT], [h[:, k, :] for h in w],
                              first=False, last=closed and k == KD - 1)
                return ins

            def gates(b, i, part):
                if part == 0 and i > 0:
                    pe.wait_ge(S_["gate_ready"], NT * b + i)
                ins = dense(G, i, GwT, bias_rows[1], part, True)
                if part == 1:
                    ins.then_inc(S_["g_psum"], 1)

            def y_dense(b, i, part):
                if part == 0:
                    wait(pe, S_["yg_ready"], NT * (b - 1) + i + 1)
                dense(Y[i], i, DwT, bias_rows[0], part, False)

            def y_state(b):
                pe.wait_ge(S_["h_lo"], b + 1)
                for i in range(NT):
                    mm3(Y[i][:], [h[:, i * P:(i + 1) * P] for h in hT], [h[:] for h in CwT], first=False
                        ).then_inc(S_["y_psum"], 1)

            def tail_turn(b, i):
                pe.wait_ge(S_["xn2_ready"], NT * b + i + 1)
                if i > 0:
                    pe.wait_ge(S_["x2T_lo"], NT * b + i)
                for k in range(KD):
                    ins = nc.tensor.transpose(TP[:, k * P:(k + 1) * P], xn2[:, i, k * P:(k + 1) * P], ident[:])
                ins.then_inc(S_["x2T_psum"], 1)

            def tail_scores(b, i):
                pe.wait_ge(S_["x2T_lo"], NT * b + i + 1)
                hi, lo = x2T[i % 2]
                at = i * 2 * E
                for k in range(KD):
                    if k == KD - 1:
                        for kl in range(KD):
                            nc.tensor.matmul(SC[:, at:at + E], lo[:, kl, :], gateT[:, kl, 0, :], start=False, stop=False)
                    ins = nc.tensor.matmul(SC[:, at:at + 2 * E], hi[:, k, :],
                                           gateT[:, k].rearrange("p h e -> p (h e)"),
                                           start=(k == 0), stop=(k == KD - 1))
                if i == NT - 1:
                    ins.then_inc(S_["scores_psum"], 1)

            def tail_ranks(b):
                pe.wait_ge(S_["onehot_ready"], b + 1)
                for i in range(NT):
                    dst = SC[:, SC_RANK + i * E:SC_RANK + (i + 1) * E]
                    for before in range(i):
                        nc.tensor.matmul(dst, ones[:], onehot[:, before, :], start=(before == 0), stop=False)
                    nc.tensor.matmul(dst, tri[:], onehot[:, i, :], start=(i == 0), stop=True)
                for i in range(NT):
                    ins = nc.tensor.matmul(SC[:, SC_COUNT:SC_COUNT + E], ones[:], onehot[:, i, :],
                                           start=(i == 0), stop=(i == NT - 1))
                ins.then_inc(S_["rank_psum"], 1)

            def power(k):
                return [h[:, POWERS.index(k), :] for h in AT]

            def inside(b, k):
                o = 2 ** k
                pe.wait_ge(S_["scan_lo"], NSTEP * b + 1 + k)
                mm3(SA[:, o * CW:], power(o), [h[:, 0:(J - o) * CW] for h in zp]).then_inc(S_["scan_psum"], 1)

            def over(b, l):
                o = LEVELS[l]
                pe.wait_ge(S_["scan_lo"], NSTEP * b + 1 + KIN + l)
                if l == 0:
                    wait(pe, S_["carry_ready"], 3 * b)
                mm3(SA[:, o * NB:EC], power(J * o), [h[:, 0:(CH + 1 - o) * NB] for h in endp]
                    ).then_inc(S_["scan_psum"], 1)

            def down(b):
                pe.wait_ge(S_["scan_lo"], NSTEP * (b + 1))
                for j in range(J):
                    ins = mm3(SA[:, j * CW:(j + 1) * CW], power(j + 1), [h[:, 0:CW] for h in endp])
                ins.then_inc(S_["down_psum"], 1)

            def body(b):
                tail = not (isinstance(b, int) and b == 0)
                wait(pe, S_["h_sum"], b)
                wait(pe, S_["gate_ready"], NT * b)
                wait(pe, S_["x2T_lo"], NT * (b - 1))
                for i in range(NT):
                    pe.wait_ge(S_["xn_ready"], NT * b + i + 1)
                    if i == NT - 1:
                        wait(pe, S_["run_ready"], b - 1)
                    for k in range(KD):
                        ins = nc.tensor.transpose(XT_BANKS[i][:, k * P:(k + 1) * P],
                                                  xn[:, i, k * P:(k + 1) * P], ident[:])
                    ins.then_inc(S_["xT_psum"], 1)
                if tail:
                    y_state(b - 1)
                pe.wait_ge(S_["xT_lo"], NT * (b + 1))
                for m in range(KH):
                    for k in range(KD):
                        ins = mm3((G, TP)[m][:], [h[:, k, m * P:(m + 1) * P] for h in s1T],
                                  [h[:, k, :] for h in xT], first=(k == 0), last=(k == KD - 1))
                    ins.then_inc(S_["s1_psum"], 1)
                for k in range(KD):
                    ins = mm3(SA[:], [h[:, k, :] for h in BwT], [h[:, k, :] for h in xT],
                              first=(k == 0), last=(k == KD - 1))
                ins.then_inc(S_["bt_psum"], 1)
                y_dense(b, 0, 0)
                y_dense(b, 0, 1)
                pe.wait_ge(S_["silu_lo"], KH * (b + 1))
                for m in range(KH):
                    ins = mm3(SC[:], [h[:, m, :] for h in s2T], [h[:, m, :] for h in sT],
                              first=(m == 0), last=(m == KH - 1))
                ins.then_inc(S_["s2_psum"], 1)
                y_dense(b, 1, 0)
                y_dense(b, 1, 1)
                if isinstance(b, int) and b == 0:
                    pe.wait_ge(S_["pow_lo"], 1)
                inside(b, 0)
                gates(b, 0, 0)
                gates(b, 0, 1)
                inside(b, 1)
                if tail:
                    tail_turn(b - 1, 0)
                y_dense(b, 2, 0)
                over(b, 0)
                y_dense(b, 2, 1)
                if tail:
                    tail_scores(b - 1, 0)
                over(b, 1)
                if tail:
                    tail_turn(b - 1, 1)
                gates(b, 1, 0)
                over(b, 2)
                gates(b, 1, 1)
                if tail:
                    tail_scores(b - 1, 1)
                over(b, 3)
                if tail:
                    tail_turn(b - 1, 2)
                y_dense(b, 3, 0)
                over(b, 4)
                y_dense(b, 3, 1)
                if tail:
                    tail_scores(b - 1, 2)
                over(b, 5)
                if tail:
                    tail_turn(b - 1, 3)
                gates(b, 2, 0)
                over(b, 6)
                gates(b, 2, 1)
                if tail:
                    tail_scores(b - 1, 3)
                down(b)
                gates(b, 3, 0)
                gates(b, 3, 1)
                if tail:
                    tail_ranks(b - 1)

            body(0)
            body(1)
            with pe.Fori(2, NBLK) as b:
                body(b)

            def experts(first, end):
                for n in range(first, end):
                    e, k = n // KD, n % KD
                    pe.wait_ge(raw_loaded[e % RING], RAW_NEED[e % RING] + 16 * (e // RING + 1))
                    if n >= 6:
                        pe.wait_ge(S_["expert_lo"], n - 5)
                    for f in range(KD):
                        ins = nc.tensor.transpose(EBANKS[n % 6][:, f * P:(f + 1) * P],
                                                  raw[:, e % RING, f, k * P:(k + 1) * P], ident[:])
                    ins.then_inc(S_["expert_turned"], 1)

            y_state(LASTB)
            pe.wait_ge(S_["gate_ready"], NT * NBLK)
            pe.wait_ge(S_["h_sum"], NBLK)
            pe.wait_ge(S_["yg_ready"], NT * NBLK)
            experts(0, E_STEPS[0])
            for i in range(NT):
                tail_turn(LASTB, i)
                experts(E_STEPS[i], E_STEPS[i + 1])
                tail_scores(LASTB, i)
            tail_ranks(LASTB)
            experts(E_STEPS[NT], NE)
            pe.wait_ge(S_["expert_lo"], NE)
            pe.wait_ge(S_["run_ready"], NBLK)
            pe.wait_ge(S_["expert_table"], 1)
            flat = [h[:].rearrange("p e k f -> p (e k f)") for h in We]

            def slot_turn(s, m):
                bank = (TP, SC)[m % 2]
                pe.wait_ge(S_["slot_norm"], s + 1)
                wait(pe, S_["slot_lo"], s - 1)
                for k in range(KD):
                    ins = nc.tensor.transpose(bank[:, k * P:(k + 1) * P], rnorm[m][:, k * P:(k + 1) * P], ident[:])
                ins.then_inc(S_["slot_turned"], 1)

            def slot_product(s, m):
                first = pe.value_load(slot_expert[0:1, bass.ds(s, 1)], min_val=0, max_val=(E - 1) * KD * D)
                pe.wait_ge(S_["slot_lo"], s + 1)
                wait(pe, S_["slot_result"], s - 1)
                for k in range(KD):
                    for a, w in ((0, 0), (0, 1), (1, 0)):
                        ins = nc.tensor.matmul(Y[m % 2][:], x2T[m % 2][a][:, k, :], flat[w][:, bass.ds(first + k * D, D)],
                                               start=(k == 0 and a == 0 and w == 0), stop=(k == KD - 1 and a == 1))
                ins.then_inc(S_["slot_psum"], 1)

            def slot(s, m):
                slot_turn(s, m)
                if not (isinstance(s, int) and s == 0):
                    slot_product(s - 1, (m - 1) % M)

            for m in range(M):
                slot(m, m)
            with pe.Fori(1, FULL) as u:
                for m in range(M):
                    slot(u * M + m, m)
            for s in range(FULL * M, SLOTS):
                slot(s, s % M)
            slot_product(SLOTS - 1, (SLOTS - 1) % M)


_INS = ["x", "A", "B_w", "B_b", "C_w", "C_b", "D_w", "D_b", "s_w1", "s_b1", "s_w2", "s_b2", "g_w", "g_b"]
_NAMES = ["L0_attn_" + n for n in _INS] + ["L0_ffn_gate_w", "L0_ffn_expert_w"]


def kernel(**inputs):
    import numpy as np
    import concourse.bacc as bacc
    from concourse.bass_utils import run_bass_kernel_spmd

    nc = bacc.Bacc("TRN2", target_bir_lowering=False, num_devices=1)
    arrays, args = {}, []
    for name in _NAMES:
        a = np.ascontiguousarray(inputs[name])
        arrays[name] = a
        args.append(nc.dram_tensor(name, a.shape, mybir.dt.from_np(a.dtype), kind="ExternalInput").ap())
    shape = arrays["L0_attn_x"].shape
    args.append(nc.dram_tensor("out", shape, mybir.dt.float32, kind="ExternalOutput").ap())
    preln_ssm_moe_kernel(nc, *args)
    r = run_bass_kernel_spmd(nc, [arrays], core_ids=[0])
    return r.results[0]["out"]
```

```python
import concourse.bass as bass
from concourse import mybir
from contextlib import ExitStack


def preln_ssm_moe_kernel(nc, x, A, B_w, B_b, C_w, C_b, D_w, D_b, s_w1, s_b1, s_w2, s_b2, g_w, g_b,
                         gate_w, expert_w, out):
    f32, f32r, bf16, i32 = mybir.dt.float32, mybir.dt.float32r, mybir.dt.bfloat16, mybir.dt.int32
    ALU, ACT, AX = mybir.AluOpType, mybir.ActivationFunctionType, mybir.AxisListType

    P = 128
    NB, S, D = x.shape
    NS = A.shape[0]
    DH = s_w1.shape[0]
    E = expert_w.shape[0]
    KD, KH = D // P, DH // P
    EPS = 1e-5
    TB = 512
    SB = TB // NB
    NT = TB // P
    NBLK = NB * S // TB
    LASTB = NBLK - 1
    J = 4
    CH = SB // J
    CW = CH * NB
    EC = (CH + 1) * NB
    KIN = J.bit_length() - 1
    LEVELS = [2 ** i for i in range(CH.bit_length())]
    NSTEP = 1 + KIN + len(LEVELS)
    POWERS = list(range(1, J + 1)) + [J * o for o in LEVELS[1:]]
    RW = D + 4
    MEAN, RSTD, TID = D, D + 1, D + 2
    REG = NB * S + P
    DUMMY = E * REG
    SLOTS = NB * S // P + E - 1
    OOB = NB * S
    RING = 3
    M = 4
    FULL = SLOTS // M
    SC_RANK, SC_COUNT, SC_TURN = 2 * NT * E, 4 * NT * E, 2 * P

    x_t = [x[n].rearrange("(b t p) d -> b p t d", t=SB // P, p=P) for n in range(NB)]
    out_rows = out.rearrange("n s d -> (n s) d")
    routed = nc.dram_tensor("routed_rows", (DUMMY + P, RW), f32, kind="Internal").ap()

    def wait(eng, sem, value):
        if not isinstance(value, int) or value > 0:
            eng.wait_ge(sem, value)

    with ExitStack() as keep:
        def psum(name):
            return keep.enter_context(nc.psum_tensor(name, [P, 512], f32))

        def sem(name):
            return keep.enter_context(nc.semaphore(name))

        def kb(name, shape, dt=f32):
            return keep.enter_context(nc.sbuf_tensor(name, shape, dt))

        Y = [psum(f"y{i}") for i in range(NT)]
        G, TP, SA, SC = psum("gates"), psum("turned"), psum("scan"), psum("scores")
        XT_BANKS = [SA, TP, SC, G]

        raw = kb("raw_weights", [P, RING, KD, D])
        ident = kb("ident", [P, P])
        tri, ones = kb("strictly_before", [P, P], bf16), kb("ones", [P, P], bf16)
        run = kb("list_ends", [P, E])
        e_iota = kb("expert_iota", [P, NT, E])
        end_rows = kb("list_end_rows", [1, E], i32)
        padrow = kb("padrow", [P, RW])
        gate = kb("gate", [P, NT, D])
        xrow = [kb(f"x1_rows{q}", [P, NT, RW]) for q in range(2)]
        xn2 = kb("x1_norm", [P, NT, D])
        x2T = kb("x1T_hi", [P, KD, 2 * P], f32r), kb("x1T_lo", [P, KD, 2 * P], f32r)
        scT = kb("scoresT", [2 * E, 2 * P])
        gateT = kb("gateT", [P, KD, 2, E], f32r)
        ends = kb("chunk_ends", [P, EC])
        endp = kb("chunk_ends_hi", [P, EC], f32r), kb("chunk_ends_lo", [P, EC], f32r)
        st1, st2 = kb("ln1_stats", [P, NT, 6]), kb("ln2_stats", [P, NT, 6])
        mv1, mv2 = kb("ln1_mean_var", [P, NT, 2]), kb("ln2_mean_var", [P, NT, 2])
        ve1, ve2 = kb("ln1_var_eps", [P, NT]), kb("ln2_var_eps", [P, NT])
        rs1, mhalf = kb("ln1_rstd", [P, NT]), kb("minus_half", [P, NT])
        scores = kb("score_sums", [P, NT, E])
        top, best, bounded = kb("top_score", [P, NT]), kb("best", [P, NT]), kb("best_bounded", [P, NT])
        hit, cand = kb("is_top", [P, NT, E]), kb("candidate", [P, NT, E])
        onehot = kb("onehot", [P, NT, E], bf16)
        pos, picked = kb("list_position", [P, NT, E]), kb("picked_position", [P, NT, E])
        dest_f = kb("dest_f", [P, NT])
        dest = [kb(f"dest{q}", [P, NT], i32) for q in range(2)]
        ids = [kb(f"ids{m}", [P, 1], i32) for m in range(M)]
        count, tiles_f, cum, gap = kb("list_count", [1, E]), kb("list_tiles", [1, E]), kb("tiles_upto", [1, E]), kb("list_gap", [1, E])
        tiles_i, tiles_s, zeros = kb("list_tiles_i", [1, E], i32), kb("list_tiles_s", [1, E], i32), kb("zeros_row", [1, E])
        slot_iota = kb("slot_iota", [1, SLOTS])
        past, past_gap = kb("slot_past", [1, SLOTS, E]), kb("slot_past_gap", [1, SLOTS, E])
        slot_e, slot_r, slot_r2 = kb("slot_expert_f", [1, SLOTS]), kb("slot_row_f", [1, SLOTS]), kb("slot_row_sum", [1, SLOTS])
        slot_expert, slot_row = kb("slot_expert", [1, SLOTS], i32), kb("slot_row", [1, SLOTS], i32)
        rows = [xrow[0][:, m, :] for m in range(M)]
        rnorm = [xn2[:, m, :] for m in range(M)]
        res = [gate[:, m, :] for m in range(M)]

        with ExitStack() as main:
            def sb(name, shape, dt=f32):
                return main.enter_context(nc.sbuf_tensor(name, shape, dt))

            def pair(name, shape):
                return sb(name + "_hi", shape, f32r), sb(name + "_lo", shape, f32r)

            DwT, GwT = pair("DwT", [P, KD, D]), pair("GwT", [P, KD, D])
            s1T, s2T = pair("s1T", [P, KD, DH]), pair("s2T", [P, KH, NS])
            BwT, CwT = pair("BwT", [P, KD, NS]), pair("CwT", [P, D])
            AT = pair("A_powers", [P, len(POWERS), NS])
            bias_y, bias_g = sb("y_bias", [P, D]), sb("g_bias", [P, D])
            gbias = [sb(f"gated_bias{q}", [P, D]) for q in range(2)]
            b1, b2, bB = sb("s_b1_col", [P, KH]), sb("s_b2_col", [P, 1]), sb("B_b_col", [P, 1])
            xin, xn = sb("x_in", [P, NT, D]), sb("x_norm", [P, NT, D])
            xT = pair("xT", [P, KD, TB])
            silu = sb("silu", [P, KH, TB])
            sT = pair("siluT", [P, KH, TB])
            sel = sb("select", [P, TB])
            z = sb("z", [P, J, CH, NB])
            zp = pair("z", [P, J * CW])
            hT = pair("hT", [P, TB])
        with ExitStack() as later:
            We = [later.enter_context(nc.sbuf_tensor("expert" + h, [P, E, KD, D], f32r)) for h in ("_hi", "_lo")]
        z2 = z[:].rearrange("p j c n -> p (j c n)")
        powT, powP = xn2[:].rearrange("p t d -> p (t d)"), gate[:].rearrange("p t d -> p (t d)")
        bias_c = gbias[0]
        raw_C, raw_A, raw_gate = silu[:, 0, :], silu[:, 1, 0:NS], z2[0:E, :]

        S_ = {}
        for name in ("bias_loaded cols_loaded aux_loaded xin_loaded consts_made consts2_made pad_made ident_made "
                     "bias_sum w_turned w_hi w_lo pow_psum pow_copied pow_hi pow_lo "
                     "stats1 mv1_ready ve1_ready rstd1_ready xn_ready xT_psum xT_hi xT_lo "
                     "s1_psum s1_sig silu_ready silu_hi silu_lo bt_psum s2_psum sel_ready "
                     "scan_psum scan_sum scan_hi scan_lo down_psum h_sum h_hi h_lo carry_ready "
                     "g_psum g_sum gate_ready bias_gated biased y_psum yg_ready x1_ready "
                     "stats2 mv2_ready ve2_ready rstd2_ready mean_copied xn2_ready x2T_psum x2T_hi x2T_lo "
                     "scoresT_psum scoresT_ready scores_psum scores_ready top_ready hit_ready cand_ready best_ready bounded_ready onehot_ready "
                     "rank_psum pos_ready picked_ready run_ready destf_ready dest_ready ids_ready ends_ready pad_sent "
                     "expert_turned expert_hi expert_full expert_lo expert_lo_pool table_step slot_iota_made expert_table row_table "
                     "slot_norm slot_turned slot_hi slot_lo slot_psum slot_base slot_ids slot_result").split():
            S_[name] = sem(name)
        raw_loaded = [sem(f"raw_loaded{r}") for r in range(RING)]
        xres_loaded = [sem("xres_loaded_even"), sem("xres_loaded_odd")]
        rows_sent = [sem("rows_sent_even"), sem("rows_sent_odd")]
        row_loaded = [sem(f"row_loaded{m}") for m in range(M)]
        out_sent = [sem(f"out_sent{m}") for m in range(M)]

        def counted_waits(eng, *waits):
            waits = [(sem, v if isinstance(v, int) else eng.to_reg(v)) for sem, v in waits]
            eng.wait_ge(S_["ident_made"], 1)
            for sem, v in waits:
                wait(eng, sem, v)

        def by_block(bank):
            return bank[:].rearrange("p (k t) -> p k t", k=KD)

        def token_order(t):
            return t[:].rearrange("p (n c j) -> p j c n", n=NB, j=J)

        JOBS = []
        for k in range(KD):
            JOBS.append((0, [(raw[:, 0, f, k * P:(k + 1) * P], f * P, P) for f in range(KH)], DH,
                         [h[:, k, :] for h in s1T]))
        JOBS.append((0, [(raw[:, 0, 2, k * P:(k + 1) * P], k * NS, P) for k in range(KD)], KD * NS,
                     [h[:].rearrange("p k n -> p (k n)") for h in BwT]))
        JOBS.append((0, [(raw[:, 0, 3, k * P:(k + 1) * P], k * NS, P) for k in range(KH)], KH * NS,
                     [h[:].rearrange("p k n -> p (k n)") for h in s2T]))
        for r, w in ((1, DwT), (2, GwT)):
            for k in range(KD):
                JOBS.append((r, [(raw[:, r, f, k * P:(k + 1) * P], f * P, P) for f in range(KD)], D,
                             [h[:, k, :] for h in w]))
        JOBS.append((None, [(raw_C[:, f * P:(f + 1) * P], f * P, P) for f in range(KD)], D, [h[:] for h in CwT]))
        JOBS.append((None, [(raw_gate[:, k * P:(k + 1) * P], k * E, E) for k in range(KD)], KD * E,
                     [gateT[:, :, h, :] for h in range(2)]))
        RAW_NEED = [48, 16, 16]
        PREP_BANKS = Y + [G, TP, SA]

        def job_view(j):
            _, _, n, dst = JOBS[j]
            bank = PREP_BANKS[j % len(PREP_BANKS)][:, 0:n]
            return bank.rearrange("p (k e) -> p k e", e=E) if len(dst[0].shape) == 3 else bank

        PK = [1] + [2 ** i for i in range(1, POWERS[-1].bit_length() - 1)]

        def tslot(k):
            i = POWERS.index(k)
            return powT[:, i * NS:(i + 1) * NS]

        def pslot(k):
            i = PK.index(k)
            return raw_A if k == 1 else powP[:, i * NS:(i + 1) * NS]

        ROUNDS = [[("T", 1, 0, 0)], [("T", 2, 1, 1), ("P", 2, 1, 1)],
                  [("T", 3, 1, 2), ("T", 4, 2, 2), ("P", 4, 2, 2)]]
        for k in PK[2:]:
            ROUNDS.append([("T", 2 * k, k, k)] + ([("P", 2 * k, k, k)] if 2 * k in PK else []))

        PREP = []
        for n in range(max(len(JOBS), len(ROUNDS))):
            PREP += [("job", n)] * (n < len(JOBS)) + [("pow", n)] * (n < len(ROUNDS))

        EBANKS = [G] + Y
        NE = E * KD
        NEB = len(EBANKS)
        E_STEPS = [8, 11, 15, 20]

        def by_pool(n):
            return n < KD or n % 3 == 0

        def pool_count(n):
            return sum(map(by_pool, range(n)))

        def dve_count(n):
            return n - pool_count(n)

        def turn_bank(b, i):
            return SA if isinstance(b, int) and b == LASTB and i % 2 else TP

        block = keep.enter_context(nc.Block())

        def send_padding(eng, lists):
            eng.wait_ge(S_["ends_ready"], 1)
            for e in lists:
                end = eng.value_load(end_rows[0:1, e:e + 1], min_val=0, max_val=DUMMY - P)
                eng.dma_start(routed[bass.ds(end, P), :], padrow[:]).then_inc(S_["pad_sent"], 16)

        @block.sync
        def _(sp):
            def load_x(b):
                wait(sp, S_["xn_ready"], NT * b)
                for n in range(NB):
                    sp.dma_start(xin[:, 2 * n:2 * n + 2, :], x_t[n][b] if isinstance(b, int)
                                 else x_t[n][bass.ds(b, 1)].rearrange("o p t d -> p (o t) d")
                                 ).then_inc(S_["xin_loaded"], 16)

            def load_residual(b, q, turn):
                wait(sp, rows_sent[q], 16 * NT * turn)
                for n in range(NB):
                    sp.dma_start(xrow[q][:, 2 * n:2 * n + 2, 0:D], x_t[n][b] if isinstance(b, int)
                                 else x_t[n][bass.ds(b, 1)].rearrange("o p t d -> p (o t) d")
                                 ).then_inc(xres_loaded[q], 16)

            def load_expert(e):
                sp.dma_start(raw[:, e % RING], expert_w[e].rearrange("(f p) d -> p f d", p=P)
                             ).then_inc(raw_loaded[e % RING], 16)

            sp.dma_start(raw[:, 0, 0:KH], s_w1.rearrange("(f p) d -> p f d", p=P)).then_inc(raw_loaded[0], 16)
            sp.dma_start(raw[:, 0, 2], B_w).then_inc(raw_loaded[0], 16)
            sp.dma_start(raw[:, 0, 3, 0:DH], s_w2).then_inc(raw_loaded[0], 16)
            load_x(0)
            sp.dma_start(raw[:, 1], D_w.rearrange("(f p) d -> p f d", p=P)).then_inc(raw_loaded[1], 16)
            sp.dma_start(raw[:, 2], g_w.rearrange("(f p) d -> p f d", p=P)).then_inc(raw_loaded[2], 16)
            load_residual(0, 0, 0)
            load_x(1)
            load_residual(1, 1, 0)
            load_x(2)
            sp.wait_ge(S_["pad_made"], 1)
            sp.dma_start(routed[DUMMY:DUMMY + P, :], padrow[:]).then_inc(S_["pad_sent"], 16)
            sp.wait_ge(S_["w_turned"], len(JOBS))
            for e in range(RING):
                load_expert(e)
            with sp.Fori(1, NBLK // 2 - 1) as t:
                load_x(t * 2 + 1)
                load_residual(t * 2, 0, t)
                load_x(t * 2 + 2)
                load_residual(t * 2 + 1, 1, t)
            load_x(LASTB)
            load_residual(LASTB - 1, 0, NBLK // 2 - 1)
            load_residual(LASTB, 1, NBLK // 2 - 1)
            for e in range(RING, E):
                sp.wait_ge(S_["expert_turned"], KD * (e - RING + 1))
                load_expert(e)
            send_padding(sp, range(0, E, 2))
            for q in range(2):
                sp.wait_ge(rows_sent[q], 16 * NT * NBLK // 2)
            sp.wait_ge(S_["pad_sent"], 16 * (E + 1))
            sp.wait_ge(S_["row_table"], 1)

            def load_slot(s, m):
                row = sp.value_load(slot_row[0:1, bass.ds(s, 1)], min_val=0, max_val=DUMMY)
                wait(sp, S_["slot_result"], s - M + 1)
                wait(sp, S_["slot_ids"], s - M + 1)
                sp.dma_start(rows[m], routed[bass.ds(row, P), :]).then_inc(row_loaded[m], 16)

            for m in range(M):
                load_slot(m, m)
            with sp.Fori(1, FULL) as u:
                for m in range(M):
                    load_slot(u * M + m, m)
            for s in range(FULL * M, SLOTS):
                load_slot(s, s % M)

        @block.gpsimd
        def _(pool):
            made = [nc.gpsimd.memset(ident[:], 0.0), nc.gpsimd.memset(tri[:], 1.0),
                    nc.gpsimd.memset(ones[:], 1.0), nc.gpsimd.memset(mhalf[:], -0.5),
                    nc.gpsimd.memset(padrow[:], 0.0),
                    nc.gpsimd.memset(xrow[0][:, :, D:RW], 0.0), nc.gpsimd.memset(xrow[1][:, :, D:RW], 0.0),
                    nc.gpsimd.memset(ends[:, 0:NB], 0.0)]
            made += [nc.gpsimd.memset(h[:, 0:NB].bitcast(f32), 0.0) for h in endp]
            for ins in made:
                ins.then_inc(S_["consts_made"], 1)
            pool.wait_ge(S_["consts_made"], len(made))
            nc.gpsimd.affine_select(out=ident[:], in_=ident[:], compare_op=ALU.not_equal, fill=1.0, base=0,
                                    pattern=[[-1, P]], channel_multiplier=1).then_inc(S_["ident_made"], 1)
            nc.gpsimd.affine_select(out=tri[:], in_=tri[:], compare_op=ALU.is_gt, fill=0.0, base=0,
                                    pattern=[[1, P]], channel_multiplier=-1).then_inc(S_["consts2_made"], 1)
            for tile, pattern, mult in ((run[:], [[REG, E]], 0), (e_iota[:], [[0, NT], [1, E]], 0),
                                        (slot_iota[:], [[1, SLOTS]], 0)):
                nc.gpsimd.iota(tile, pattern=pattern, base=0, channel_multiplier=mult,
                               allow_small_or_imprecise_dtypes=True).then_inc(S_["consts2_made"], 1)
            nc.gpsimd.memset(padrow[:].bitcast(i32)[:, TID:TID + 1], OOB).then_inc(S_["pad_made"], 1)
            for q in range(2):
                nc.gpsimd.iota(xrow[q][:].bitcast(i32)[:, :, TID].rearrange("p (n t) -> p n t", n=NB),
                               pattern=[[S, NB], [P, SB // P]], base=(q - 2) * SB,
                               channel_multiplier=1).then_inc(S_["ids_ready"], 1)

            def rstd1(b):
                counted_waits(pool, (S_["mv1_ready"], b + 1))
                nc.gpsimd.tensor_scalar(ve1[:], mv1[:, :, 1], EPS, None, ALU.add).then_inc(S_["ve1_ready"], 1)
                pool.wait_ge(S_["ve1_ready"], b + 1)
                wait(pool, S_["xn_ready"], NT * b)
                nc.gpsimd.tensor_tensor(rs1[:], ve1[:], mhalf[:], ALU.pow).then_inc(S_["rstd1_ready"], 1)

            def residual(b, q):
                for i in range(NT):
                    pool.wait_ge(S_["biased"], NT * b + i + 1)
                    pool.wait_ge(S_["yg_ready"], NT * b + i + 1)
                    nc.gpsimd.tensor_tensor(xrow[q][:, i, 0:D], xrow[q][:, i, 0:D], gate[:, i, :],
                                            ALU.add).then_inc(S_["x1_ready"], 1)

            def rstd2(b, q):
                row_i = xrow[q][:].bitcast(i32)[:, :, TID]
                counted_waits(pool, (S_["mv2_ready"], b + 1))
                nc.gpsimd.tensor_scalar(ve2[:], mv2[:, :, 1], EPS, None, ALU.add).then_inc(S_["ve2_ready"], 1)
                nc.gpsimd.tensor_copy(xrow[q][:, :, MEAN], mv2[:, :, 0]).then_inc(S_["mean_copied"], 1)
                pool.wait_ge(S_["ve2_ready"], b + 1)
                nc.gpsimd.tensor_tensor(xrow[q][:, :, RSTD], ve2[:], mhalf[:], ALU.pow).then_inc(S_["rstd2_ready"], 1)
                counted_waits(pool, (S_["ids_ready"], b + 2))
                nc.gpsimd.tensor_scalar(row_i, row_i, float(2 * SB), None, ALU.add).then_inc(S_["ids_ready"], 1)

            def scatter(b, q):
                counted_waits(pool, (S_["dest_ready"], b + 1), (S_["rstd2_ready"], b + 1),
                              (S_["mean_copied"], b + 1), (S_["ids_ready"], b + 3))
                for i in range(NT):
                    nc.gpsimd.indirect_dma_start(
                        out=routed, out_offset=bass.IndirectOffsetOnAxis(ap=dest[q][:, i:i + 1], axis=0),
                        in_=xrow[q][:, i, :], in_offset=None).then_inc(rows_sent[q], 16)

            def bias(b, q, turn, i):
                if i == 0:
                    pool.wait_ge(xres_loaded[q], 16 * NB * (turn + 1))
                pool.wait_ge(S_["gate_ready"], NT * b + i + 1)
                wait(pool, S_["biased"], NT * b + i - 1)
                nc.gpsimd.tensor_tensor(gbias[i % 2][:], gate[:, i, :], bias_y[:], ALU.mult
                                        ).then_inc(S_["bias_gated"], 1)
                pool.wait_ge(S_["bias_gated"], NT * b + i + 1)
                nc.gpsimd.tensor_tensor(xrow[q][:, i, 0:D], xrow[q][:, i, 0:D], gbias[i % 2][:], ALU.add
                                        ).then_inc(S_["biased"], 1)

            def body(b, q, turn):
                if not (isinstance(b, int) and b == 0):
                    residual(b - 1, 1 - q)
                    rstd2(b - 1, 1 - q)
                if not (isinstance(b, int) and b == LASTB):
                    rstd1(b + 1)
                if not (isinstance(b, int) and b < 2):
                    scatter(b - 2, q)
                for i in range(NT):
                    bias(b, q, turn, i)

            pool.wait_ge(S_["bias_sum"], 1)
            rstd1(0)
            for b in range(3):
                body(b, b % 2, b // 2)
            with pool.Fori(1, NBLK // 2 - 1) as t:
                body(t * 2 + 1, 1, t)
                body(t * 2 + 2, 0, t + 1)
            body(LASTB, 1, NBLK // 2 - 1)
            scatter(LASTB - 1, 0)

            def experts(first, end):
                for n in filter(by_pool, range(first, end)):
                    pool.wait_ge(S_["expert_hi"], n + 1)
                    pool.wait_ge(S_["expert_full"], pool_count(n) + 1)
                    hi, lo = We[0][:, n // KD, n % KD, :], We[1][:, n // KD, n % KD, :]
                    nc.gpsimd.tensor_tensor(lo, lo.bitcast(f32), hi.bitcast(f32), ALU.subtract
                                            ).then_inc(S_["expert_lo_pool"], 1)

            rstd2(LASTB, 1)
            experts(0, E_STEPS[-1])
            scatter(LASTB, 1)
            experts(E_STEPS[-1], NE)

            def slot_base(s, m, turn):
                counted_waits(pool, (row_loaded[m], 16 * (turn + 1)), (out_sent[m], 16 * turn))
                nc.gpsimd.tensor_copy(ids[m][:], rows[m].bitcast(i32)[:, TID:TID + 1]).then_inc(S_["slot_ids"], 1)
                pool.wait_ge(S_["slot_norm"], s + 1)
                nc.gpsimd.tensor_tensor(rows[m][:, 0:D], rows[m][:, 0:D], rnorm[m], ALU.add
                                        ).then_inc(S_["slot_base"], 1)

            def slot_store(s, m):
                counted_waits(pool, (S_["slot_result"], s + 1), (S_["slot_ids"], s + 1))
                nc.gpsimd.indirect_dma_start(
                    out=out_rows, out_offset=bass.IndirectOffsetOnAxis(ap=ids[m][:, 0:1], axis=0),
                    in_=res[m], in_offset=None, bounds_check=OOB - 1, oob_is_err=False
                ).then_inc(out_sent[m], 16)

            def slot(s, m, turn):
                slot_base(s, m, turn)
                if not (isinstance(s, int) and s == 0):
                    slot_store(s - 1, (m - 1) % M)

            for m in range(M):
                slot(m, m, 0)
            with pool.Fori(1, FULL) as u:
                for m in range(M):
                    slot(u * M + m, m, u)
            for s in range(FULL * M, SLOTS):
                slot(s, s % M, FULL)
            slot_store(SLOTS - 1, (SLOTS - 1) % M)
            for m in range(M):
                pool.wait_ge(out_sent[m], 16 * len(range(m, SLOTS, M)))

        @block.scalar
        def _(act):
            act.dma_start(raw_A, A).then_inc(S_["aux_loaded"], 16)
            act.dma_start(bias_y[:], D_b.partition_broadcast(P)).then_inc(S_["bias_loaded"], 16)
            act.dma_start(bias_g[:], g_b.partition_broadcast(P)).then_inc(S_["bias_loaded"], 16)
            act.dma_start(bias_c[:], C_b.partition_broadcast(P)).then_inc(S_["bias_loaded"], 16)
            act.dma_start(raw_C.rearrange("p (f s) -> p f s", f=KD), C_w.rearrange("(f p) s -> p f s", p=P)
                          ).then_inc(S_["aux_loaded"], 16)
            act.dma_start(raw_gate, gate_w).then_inc(S_["aux_loaded"], 16)
            for m in range(KH):
                act.dma_start(b1[:, m:m + 1], s_b1[m * P:(m + 1) * P].unsqueeze(1)).then_inc(S_["cols_loaded"], 16)
            act.dma_start(b2[:], s_b2.unsqueeze(1)).then_inc(S_["cols_loaded"], 16)
            act.dma_start(bB[:], B_b.unsqueeze(1)).then_inc(S_["cols_loaded"], 16)
            copied = 0
            for what, n in PREP:
                if what == "pow":
                    act.wait_ge(S_["pow_psum"], n + 1)
                    for i, (side, k, _, _) in enumerate(ROUNDS[n]):
                        nc.scalar.activation(tslot(k) if side == "T" else pslot(k), SC[:, i * NS:(i + 1) * NS],
                                             ACT.Copy).then_inc(S_["pow_copied"], 1)
                    copied += len(ROUNDS[n])
                else:
                    act.wait_ge(S_["w_turned"], n + 1)
                    nc.scalar.activation(JOBS[n][3][0], job_view(n), ACT.Copy).then_inc(S_["w_hi"], 1)
            act.wait_ge(S_["pow_copied"], copied)
            nc.scalar.activation(AT[0][:].rearrange("p k s -> p (k s)"), powT[:, 0:len(POWERS) * NS],
                                 ACT.Copy).then_inc(S_["pow_hi"], 1)
            act.wait_ge(S_["cols_loaded"], 16 * (KH + 2))

            def tail_hi(b, i):
                act.wait_ge(S_["x2T_psum"], NT * b + i + 1)
                nc.scalar.activation(x2T[0][:, :, i % 2 * P:(i % 2 + 1) * P], by_block(turn_bank(b, i)), ACT.Copy
                                     ).then_inc(S_["x2T_hi"], 1)

            def scoresT(b, pair):
                act.wait_ge(S_["scoresT_psum"], 2 * b + pair + 1)
                nc.scalar.activation(scT[:], SC[0:2 * E, SC_TURN:], ACT.Copy).then_inc(S_["scoresT_ready"], 1)

            def gates(b, i):
                act.wait_ge(S_["g_sum"], NT * b + i + 1)
                nc.scalar.activation(gate[:, i, :], gate[:, i, :], ACT.Sigmoid).then_inc(S_["gate_ready"], 1)

            def body(b):
                tail = not (isinstance(b, int) and b == 0)
                for i in range(NT):
                    act.wait_ge(S_["xT_psum"], NT * b + i + 1)
                    nc.scalar.activation(xT[0][:, :, i * P:(i + 1) * P], by_block(XT_BANKS[i]), ACT.Copy
                                         ).then_inc(S_["xT_hi"], 1)
                for m in range(KH):
                    act.wait_ge(S_["s1_psum"], KH * b + m + 1)
                    wait(act, S_["silu_lo"], KH * (b - 1) + m + 1)
                    nc.scalar.activation(silu[:, m, :], (TP, G)[m][:], ACT.Sigmoid, bias=b1[:, m:m + 1]
                                         ).then_inc(S_["s1_sig"], 1)
                    act.wait_ge(S_["silu_ready"], KH * b + m + 1)
                    nc.scalar.activation(sT[0][:, m, :], silu[:, m, :], ACT.Copy).then_inc(S_["silu_hi"], 1)
                act.wait_ge(S_["s2_psum"], b + 1)
                nc.scalar.activation(sel[:], SC[:], ACT.Sigmoid, bias=b2[:]).then_inc(S_["sel_ready"], 1)
                if tail:
                    tail_hi(b - 1, 0)
                    tail_hi(b - 1, 1)
                    scoresT(b - 1, 0)
                    tail_hi(b - 1, 2)
                gates(b, 0)
                if tail:
                    tail_hi(b - 1, 3)
                    scoresT(b - 1, 1)
                gates(b, 1)
                act.wait_ge(S_["h_sum"], b + 1)
                nc.scalar.activation(token_order(hT[0]), z[:], ACT.Copy).then_inc(S_["h_hi"], 1)
                gates(b, 2)
                gates(b, 3)

            body(0)
            body(1)
            with act.Fori(2, NBLK) as b:
                body(b)

            def experts(first, end):
                for n in range(first, end):
                    act.wait_ge(S_["expert_turned"], n + 1)
                    nc.scalar.activation(We[0][:, n // KD, n % KD, :], EBANKS[n % NEB][:], ACT.Copy
                                         ).then_inc(S_["expert_hi"], 1)
                    if by_pool(n):
                        nc.scalar.activation(We[1][:, n // KD, n % KD, :].bitcast(f32), EBANKS[n % NEB][:], ACT.Copy
                                             ).then_inc(S_["expert_full"], 1)

            experts(0, E_STEPS[0])
            for pair in range(2):
                tail_hi(LASTB, 2 * pair)
                tail_hi(LASTB, 2 * pair + 1)
                experts(E_STEPS[pair], E_STEPS[pair + 1])
                scoresT(LASTB, pair)
            experts(E_STEPS[2], E_STEPS[3] + KD)
            send_padding(act, range(1, E, 2))
            experts(E_STEPS[3] + KD, NE)

            def slot_hi(s, q):
                act.wait_ge(S_["slot_turned"], s + 1)
                wait(act, S_["slot_psum"], s - 1)
                nc.scalar.activation(x2T[0][:, :, q * P:(q + 1) * P], by_block((TP, SC)[q]), ACT.Copy).then_inc(S_["slot_hi"], 1)

            for s in range(M):
                slot_hi(s, s % 2)
            with act.Fori(1, FULL) as u:
                for m in range(M):
                    slot_hi(u * M + m, m % 2)
            for s in range(FULL * M, SLOTS):
                slot_hi(s, s % 2)

        @block.vector
        def _(dve):
            def ln1_stats(b, i):
                if i == 0:
                    dve.wait_ge(S_["xin_loaded"], 16 * NB * (b + 1))
                nc.vector.bn_stats(st1[:, i, :], xin[:, i, :]).then_inc(S_["stats1"], 1)

            def ln1_mv(b):
                counted_waits(dve, (S_["stats1"], NT * (b + 1)), (S_["rstd1_ready"], b))
                for i in range(NT):
                    ins = nc.vector.bn_aggr(mv1[:, i, :], st1[:, i, :])
                ins.then_inc(S_["mv1_ready"], 1)

            def normalise1(b, first=0, end=NT):
                dve.wait_ge(S_["rstd1_ready"], b + 1)
                dve.wait_ge(S_["mv1_ready"], b + 1)
                wait(dve, S_["xT_psum"], NT * b)
                for i in range(first, end):
                    nc.vector.tensor_scalar(xn[:, i, :], xin[:, i, :], mv1[:, i, 0:1], rs1[:, i:i + 1],
                                            ALU.subtract, ALU.mult).then_inc(S_["xn_ready"], 1)

            dve.wait_ge(S_["bias_loaded"], 48)
            nc.vector.tensor_tensor(bias_y[:], bias_y[:], bias_c[:], ALU.add).then_inc(S_["bias_sum"], 1)
            for i in range(NT):
                ln1_stats(0, i)
            ln1_mv(0)
            for j, (_, _, _, dst) in enumerate(JOBS):
                dve.wait_ge(S_["w_hi"], j + 1)
                nc.vector.tensor_tensor(dst[1], job_view(j), dst[0].bitcast(f32), ALU.subtract).then_inc(S_["w_lo"], 1)
                if j == len(JOBS) // 2:
                    normalise1(0)
            dve.wait_ge(S_["pow_hi"], 1)
            nc.vector.tensor_tensor(AT[1][:].rearrange("p k s -> p (k s)"), powT[:, 0:len(POWERS) * NS],
                                    AT[0][:].rearrange("p k s -> p (k s)").bitcast(f32),
                                    ALU.subtract).then_inc(S_["pow_lo"], 1)

            def split(hi, lo, src, n):
                dve.wait_ge(S_["scan_sum"], n)
                nc.vector.tensor_copy(hi, src).then_inc(S_["scan_hi"], 1)
                dve.wait_ge(S_["scan_hi"], n)
                nc.vector.tensor_tensor(lo, src, hi.bitcast(f32), ALU.subtract).then_inc(S_["scan_lo"], 1)

            def inside(b, k):
                n = NSTEP * b + 2 + k
                o = 2 ** k * CW
                dve.wait_ge(S_["scan_psum"], (NSTEP - 1) * b + k + 1)
                nc.vector.tensor_tensor(z2[:, o:], SA[:, o:], z2[:, o:], ALU.add).then_inc(S_["scan_sum"], 1)
                if k < KIN - 1:
                    split(zp[0][:, o:], zp[1][:, o:], z2[:, o:], n)
                else:
                    split(endp[0][:, NB:], endp[1][:, NB:], z2[:, (J - 1) * CW:], n)
                    nc.vector.tensor_copy(ends[:, NB:], z2[:, (J - 1) * CW:]).then_inc(S_["carry_ready"], 1)

            def over(b, l):
                n = NSTEP * b + 2 + KIN + l
                o = LEVELS[l] * NB
                dve.wait_ge(S_["scan_psum"], (NSTEP - 1) * b + KIN + l + 1)
                if l == 0:
                    dve.wait_ge(S_["carry_ready"], 3 * b + 1)
                nc.vector.tensor_tensor(ends[:, o:], SA[:, o:EC], ends[:, o:], ALU.add).then_inc(S_["scan_sum"], 1)
                split(endp[0][:, o:], endp[1][:, o:], ends[:, o:], n)

            def gate_sum(b, i):
                dve.wait_ge(S_["g_psum"], NT * b + i + 1)
                wait(dve, S_["x1_ready"], NT * (b - 1) + i + 1)
                nc.vector.tensor_tensor(gate[:, i, :], G[:], bias_g[:], ALU.add).then_inc(S_["g_sum"], 1)

            def gated(b):
                for i in range(NT):
                    dve.wait_ge(S_["y_psum"], NT * b + i + 1)
                    dve.wait_ge(S_["bias_gated"], NT * b + i + 1)
                    nc.vector.tensor_tensor(gate[:, i, :], Y[i][:], gate[:, i, :], ALU.mult
                                            ).then_inc(S_["yg_ready"], 1)

            def ln2_stats(b, q, i):
                dve.wait_ge(S_["x1_ready"], NT * b + i + 1)
                nc.vector.bn_stats(st2[:, i, :], xrow[q][:, i, 0:D]).then_inc(S_["stats2"], 1)

            def ln2_mv(b):
                counted_waits(dve, (S_["stats2"], NT * (b + 1)), (S_["rstd2_ready"], b), (S_["mean_copied"], b))
                for i in range(NT):
                    ins = nc.vector.bn_aggr(mv2[:, i, :], st2[:, i, :])
                ins.then_inc(S_["mv2_ready"], 1)

            def normalise2(b, q, first=0, end=NT):
                dve.wait_ge(S_["rstd2_ready"], b + 1)
                dve.wait_ge(S_["mean_copied"], b + 1)
                wait(dve, S_["x2T_psum"], NT * b)
                for i in range(first, end):
                    nc.vector.tensor_scalar(xn2[:, i, :], xrow[q][:, i, 0:D], xrow[q][:, i, MEAN:MEAN + 1],
                                            xrow[q][:, i, RSTD:RSTD + 1], ALU.subtract, ALU.mult
                                            ).then_inc(S_["xn2_ready"], 1)

            def tail_lo(b, i):
                dve.wait_ge(S_["x2T_hi"], NT * b + i + 1)
                hi, lo = [h[:, :, i % 2 * P:(i % 2 + 1) * P] for h in x2T]
                nc.vector.tensor_tensor(lo, by_block(turn_bank(b, i)), hi.bitcast(f32), ALU.subtract
                                        ).then_inc(S_["x2T_lo"], 1)

            def choose(b):
                dve.wait_ge(S_["scores_psum"], 2 * b + 2)
                nc.vector.tensor_reduce(scores[:], SC[:, 0:SC_RANK].rearrange("p (t h e) -> p t e h", h=2, e=E),
                                        AX.X, ALU.add).then_inc(S_["scores_ready"], 1)
                dve.wait_ge(S_["scores_ready"], b + 1)
                nc.vector.tensor_reduce(top[:], scores[:], AX.X, ALU.max).then_inc(S_["top_ready"], 1)
                dve.wait_ge(S_["top_ready"], b + 1)
                nc.vector.tensor_tensor(hit[:], scores[:], top[:].unsqueeze(2).to_broadcast([P, NT, E]), ALU.is_ge
                                        ).then_inc(S_["hit_ready"], 1)
                dve.wait_ge(S_["hit_ready"], b + 1)
                nc.vector.scalar_tensor_tensor(cand[:], hit[:], -float(E), e_iota[:], ALU.mult, ALU.add
                                               ).then_inc(S_["cand_ready"], 1)
                dve.wait_ge(S_["cand_ready"], b + 1)
                nc.vector.tensor_reduce(best[:], cand[:], AX.X, ALU.min).then_inc(S_["best_ready"], 1)
                dve.wait_ge(S_["best_ready"], b + 1)
                nc.vector.tensor_scalar(bounded[:], best[:], -1.0, float(E), ALU.min, ALU.add
                                        ).then_inc(S_["bounded_ready"], 1)
                dve.wait_ge(S_["bounded_ready"], b + 1)
                nc.vector.tensor_tensor(onehot[:], e_iota[:], bounded[:].unsqueeze(2).to_broadcast([P, NT, E]),
                                        ALU.is_equal).then_inc(S_["onehot_ready"], 1)

            def place(b, q, turn):
                ranks = SC[:, SC_RANK:SC_RANK + NT * E].rearrange("p (t e) -> p t e", e=E)
                dve.wait_ge(S_["rank_psum"], b + 1)
                wait(dve, S_["run_ready"], b)
                nc.vector.tensor_tensor(pos[:], ranks, run[:].unsqueeze(1).to_broadcast([P, NT, E]), ALU.add
                                        ).then_inc(S_["pos_ready"], 1)
                dve.wait_ge(S_["pos_ready"], b + 1)
                nc.vector.tensor_tensor(picked[:], pos[:], onehot[:], ALU.mult).then_inc(S_["picked_ready"], 1)
                nc.vector.tensor_tensor(run[:], SC[:, SC_COUNT:SC_COUNT + E], run[:], ALU.add
                                        ).then_inc(S_["run_ready"], 1)
                dve.wait_ge(S_["picked_ready"], b + 1)
                nc.vector.tensor_reduce(dest_f[:], picked[:], AX.X, ALU.add).then_inc(S_["destf_ready"], 1)
                dve.wait_ge(S_["destf_ready"], b + 1)
                wait(dve, rows_sent[q], 16 * NT * turn)
                nc.vector.tensor_copy(dest[q][:], dest_f[:]).then_inc(S_["dest_ready"], 1)

            def body(b, q, turn):
                tail = not (isinstance(b, int) and b == 0)
                ahead = not (isinstance(b, int) and b == LASTB)
                old, oldq, oldturn = b - 1, 1 - q, turn - (1 - q)
                for i in range(NT):
                    dve.wait_ge(S_["xT_hi"], NT * b + i + 1)
                    nc.vector.tensor_tensor(xT[1][:, :, i * P:(i + 1) * P], by_block(XT_BANKS[i]),
                                            xT[0][:, :, i * P:(i + 1) * P].bitcast(f32), ALU.subtract
                                            ).then_inc(S_["xT_lo"], 1)
                if tail:
                    gated(old)
                if ahead:
                    ln1_stats(b + 1, 0)
                    ln1_stats(b + 1, 1)
                for m in range(KH):
                    dve.wait_ge(S_["s1_sig"], KH * b + m + 1)
                    nc.vector.scalar_tensor_tensor(silu[:, m, :], (TP, G)[m][:], b1[:, m:m + 1], silu[:, m, :],
                                                   ALU.add, ALU.mult).then_inc(S_["silu_ready"], 1)
                    if tail:
                        ln2_stats(old, oldq, 2 * m)
                    dve.wait_ge(S_["silu_hi"], KH * b + m + 1)
                    nc.vector.tensor_tensor(sT[1][:, m, :], silu[:, m, :], sT[0][:, m, :].bitcast(f32),
                                            ALU.subtract).then_inc(S_["silu_lo"], 1)
                    if tail:
                        ln2_stats(old, oldq, 2 * m + 1)
                if tail:
                    ln2_mv(old)
                if ahead:
                    ln1_stats(b + 1, 2)
                    ln1_stats(b + 1, 3)
                    ln1_mv(b + 1)
                if tail:
                    normalise2(old, oldq, 0, 2)
                dve.wait_ge(S_["sel_ready"], b + 1)
                dve.wait_ge(S_["bt_psum"], b + 1)
                for n in range(NB):
                    cols = slice(n * SB, (n + 1) * SB)
                    ins = nc.vector.scalar_tensor_tensor(
                        z[:, :, :, n].rearrange("p j c -> p c j"), SA[:, cols].rearrange("p (c j) -> p c j", j=J),
                        bB[:], sel[:, cols].rearrange("p (c j) -> p c j", j=J), ALU.add, ALU.mult)
                ins.then_inc(S_["scan_sum"], 1)
                split(zp[0][:], zp[1][:], z2, NSTEP * b + 1)
                if tail:
                    tail_lo(old, 0)
                inside(b, 0)
                if tail:
                    normalise2(old, oldq, 2, 3)
                inside(b, 1)
                if tail:
                    tail_lo(old, 1)
                over(b, 0)
                gate_sum(b, 0)
                if tail:
                    normalise2(old, oldq, 3, 4)
                over(b, 1)
                if tail:
                    tail_lo(old, 2)
                over(b, 2)
                if ahead:
                    normalise1(b + 1, 0, 1)
                over(b, 3)
                if tail:
                    tail_lo(old, 3)
                over(b, 4)
                gate_sum(b, 1)
                over(b, 5)
                if ahead:
                    normalise1(b + 1, 1, NT)
                over(b, 6)
                gate_sum(b, 2)
                if tail:
                    choose(old)
                dve.wait_ge(S_["down_psum"], b + 1)
                nc.vector.tensor_tensor(z2, SA[:], z2, ALU.add).then_inc(S_["h_sum"], 1)
                dve.wait_ge(S_["h_hi"], b + 1)
                nc.vector.tensor_tensor(token_order(hT[1]), z[:], token_order(hT[0]).bitcast(f32), ALU.subtract
                                        ).then_inc(S_["h_lo"], 1)
                nc.vector.tensor_copy(ends[:, 0:NB], ends[:, CH * NB:]).then_inc(S_["carry_ready"], 1)
                for h in endp:
                    ins = nc.vector.tensor_copy(h[:, 0:NB], h[:, CH * NB:].bitcast(f32))
                ins.then_inc(S_["carry_ready"], 1)
                if tail:
                    place(old, oldq, oldturn)
                gate_sum(b, 3)

            dve.wait_ge(S_["cols_loaded"], 16 * (KH + 2))
            dve.wait_ge(S_["consts2_made"], 4)
            for b in range(3):
                body(b, b % 2, b // 2)
            with dve.Fori(1, NBLK // 2 - 1) as t:
                body(t * 2 + 1, 1, t)
                body(t * 2 + 2, 0, t + 1)
            body(LASTB, 1, NBLK // 2 - 1)

            def experts(first, end):
                for n in filter(lambda n: not by_pool(n), range(first, end)):
                    dve.wait_ge(S_["expert_hi"], n + 1)
                    nc.vector.tensor_tensor(We[1][:, n // KD, n % KD, :], EBANKS[n % NEB][:],
                                            We[0][:, n // KD, n % KD, :].bitcast(f32), ALU.subtract
                                            ).then_inc(S_["expert_lo"], 1)

            gated(LASTB)
            for i in range(NT):
                dve.wait_ge(S_["biased"], NT * LASTB + i + 1)
                dve.wait_ge(S_["yg_ready"], NT * LASTB + i + 1)
                nc.vector.tensor_tensor(xrow[1][:, i, 0:D], xrow[1][:, i, 0:D], gate[:, i, :], ALU.add
                                        ).then_inc(S_["x1_ready"], 1)
            for i in range(NT):
                ln2_stats(LASTB, 1, i)
            ln2_mv(LASTB)
            experts(0, E_STEPS[0])
            normalise2(LASTB, 1)
            for pair in range(2):
                tail_lo(LASTB, 2 * pair)
                tail_lo(LASTB, 2 * pair + 1)
                experts(E_STEPS[pair], E_STEPS[pair + 1])
            choose(LASTB)
            place(LASTB, 1, NBLK // 2 - 1)
            dve.wait_ge(S_["run_ready"], NBLK)
            nc.vector.tensor_copy(end_rows[:], run[0:1, :]).then_inc(S_["ends_ready"], 1)

            steps = [0]

            def then(ins):
                ins.then_inc(S_["table_step"], 1)
                experts(E_STEPS[2] + steps[0], E_STEPS[2] + steps[0] + 1)
                steps[0] += 1
                dve.wait_ge(S_["table_step"], steps[0])

            wide = [1, SLOTS, E]
            then(nc.vector.tensor_scalar(zeros[:], run[0:1, :], 0.0, None, ALU.mult))
            then(nc.vector.scalar_tensor_tensor(count[:], e_iota[0:1, 0, :], -float(REG), run[0:1, :],
                                                ALU.mult, ALU.add))
            then(nc.vector.tensor_scalar(tiles_i[:], count[:], float(P - 1), None, ALU.add))
            then(nc.vector.tensor_scalar(tiles_s[:], tiles_i[:], P.bit_length() - 1, None, ALU.arith_shift_right))
            then(nc.vector.tensor_copy(tiles_f[:], tiles_s[:]))
            then(nc.vector.tensor_tensor_scan(cum[:], tiles_f[:], zeros[:], 0.0, ALU.add, ALU.add))
            then(nc.vector.tensor_scalar(gap[:], tiles_f[:], -float(P), float(REG), ALU.mult, ALU.add))
            then(nc.vector.tensor_tensor(past[:], slot_iota[:].unsqueeze(2).to_broadcast(wide),
                                         cum[:].unsqueeze(1).to_broadcast(wide), ALU.is_ge))
            then(nc.vector.tensor_reduce(slot_e[:], past[:], AX.X, ALU.add))
            nc.vector.tensor_scalar(slot_expert[:], slot_e[:], float(E - 1), float(D * KD), ALU.min, ALU.mult
                                    ).then_inc(S_["expert_table"], 1)
            then(nc.vector.tensor_tensor(past_gap[:], past[:], gap[:].unsqueeze(1).to_broadcast(wide), ALU.mult))
            then(nc.vector.tensor_reduce(slot_r[:], past_gap[:], AX.X, ALU.add))
            then(nc.vector.scalar_tensor_tensor(slot_r2[:], slot_iota[:], float(P), slot_r[:], ALU.mult, ALU.add))
            nc.vector.tensor_scalar(slot_row[:], slot_r2[:], float(DUMMY), None, ALU.min).then_inc(S_["row_table"], 1)
            experts(E_STEPS[2] + steps[0], NE)

            def slot_norm(s, m, turn):
                dve.wait_ge(row_loaded[m], 16 * (turn + 1))
                wait(dve, S_["slot_turned"], s - M + 1)
                wait(dve, S_["slot_base"], s - M + 1)
                nc.vector.tensor_scalar(rnorm[m], rows[m][:, 0:D], rows[m][:, MEAN:MEAN + 1],
                                        rows[m][:, RSTD:RSTD + 1], ALU.subtract, ALU.mult
                                        ).then_inc(S_["slot_norm"], 1)

            def slot_lo(s, q):
                dve.wait_ge(S_["slot_hi"], s + 1)
                hi, lo = [h[:, :, q * P:(q + 1) * P] for h in x2T]
                nc.vector.tensor_tensor(lo, by_block((TP, SC)[q]), hi.bitcast(f32), ALU.subtract).then_inc(S_["slot_lo"], 1)

            def slot_sum(s, m, turn):
                dve.wait_ge(S_["slot_psum"], s + 1)
                dve.wait_ge(S_["slot_base"], s + 1)
                wait(dve, out_sent[m], 16 * turn)
                nc.vector.tensor_tensor(res[m], Y[m % 2][:], rows[m][:, 0:D], ALU.add).then_inc(S_["slot_result"], 1)

            def slot(s, m, turn):
                slot_lo(s, m % 2)
                if not (isinstance(s, int) and s == SLOTS - 1):
                    slot_norm(s + 1, (m + 1) % M, turn + (m + 1) // M)
                if not (isinstance(s, int) and s == 0):
                    slot_sum(s - 1, (m - 1) % M, turn - (m == 0))

            slot_norm(0, 0, 0)
            for s in range(2 * M):
                slot(s, s % M, s // M)
            with dve.Fori(2, FULL) as u:
                for m in range(M):
                    slot(u * M + m, m, u)
            for s in range(FULL * M, SLOTS):
                slot(s, s % M, FULL)
            slot_sum(SLOTS - 1, (SLOTS - 1) % M, (SLOTS - 1) // M)

        @block.tensor
        def _(pe):
            def mm3(dst, left, right, first=True, last=True):
                nc.tensor.matmul(dst, left[0], right[0], start=first, stop=False)
                nc.tensor.matmul(dst, left[0], right[1], start=False, stop=False)
                return nc.tensor.matmul(dst, left[1], right[0], start=False, stop=last)

            pe.wait_ge(S_["ident_made"], 1)
            pe.wait_ge(S_["aux_loaded"], 48)
            copied = 0
            for what, n in PREP:
                if what == "pow":
                    wait(pe, S_["pow_copied"], copied)
                    for i, (side, k, a, m) in enumerate(ROUNDS[n]):
                        dst = SC[:, i * NS:(i + 1) * NS]
                        if a == 0:
                            ins = nc.tensor.transpose(dst, raw_A, ident[:])
                        elif side == "T":
                            ins = nc.tensor.matmul(dst, pslot(a), tslot(m), start=True, stop=True)
                        else:
                            ins = nc.tensor.matmul(dst, tslot(a), pslot(m), start=True, stop=True)
                    ins.then_inc(S_["pow_psum"], 1)
                    copied += len(ROUNDS[n])
                else:
                    r, turns, _, _ = JOBS[n]
                    if r is not None:
                        pe.wait_ge(raw_loaded[r], RAW_NEED[r])
                    if n >= len(PREP_BANKS):
                        pe.wait_ge(S_["w_lo"], n + 1 - len(PREP_BANKS))
                    for src, at, rows_in in turns:
                        ins = nc.tensor.transpose(PREP_BANKS[n % len(PREP_BANKS)][:, at:at + rows_in], src,
                                                  ident[0:rows_in, 0:rows_in])
                    ins.then_inc(S_["w_turned"], 1)
            pe.wait_ge(S_["w_lo"], len(JOBS))
            pe.wait_ge(S_["pow_copied"], copied)
            pe.wait_ge(S_["consts2_made"], 4)

            def dense(dst, i, w, part, closed):
                for k in (0, 1) if part == 0 else (2, 3):
                    ins = mm3(dst[:], [h[:, k, i * P:(i + 1) * P] for h in xT], [h[:, k, :] for h in w],
                              first=(k == 0), last=closed and k == KD - 1)
                return ins

            def gates(b, i, part):
                if part == 0 and i > 0:
                    pe.wait_ge(S_["g_sum"], NT * b + i)
                ins = dense(G, i, GwT, part, True)
                if part == 1:
                    ins.then_inc(S_["g_psum"], 1)

            def y_dense(b, i, part):
                if part == 0:
                    wait(pe, S_["yg_ready"], NT * (b - 1) + i + 1)
                dense(Y[i], i, DwT, part, False)

            def y_state(b):
                pe.wait_ge(S_["h_lo"], b + 1)
                for i in range(NT):
                    mm3(Y[i][:], [h[:, i * P:(i + 1) * P] for h in hT], [h[:] for h in CwT], first=False
                        ).then_inc(S_["y_psum"], 1)

            def tail_turn(b, i):
                pe.wait_ge(S_["xn2_ready"], NT * b + i + 1)
                bank = turn_bank(b, i)
                if i > 0 and turn_bank(b, i - 1) is bank:
                    pe.wait_ge(S_["x2T_lo"], NT * b + i)
                elif i > 1:
                    pe.wait_ge(S_["x2T_lo"], NT * b + i - 1)
                for k in range(KD):
                    ins = nc.tensor.transpose(bank[:, k * P:(k + 1) * P], xn2[:, i, k * P:(k + 1) * P], ident[:])
                ins.then_inc(S_["x2T_psum"], 1)

            def tail_scores(b, pair):
                pe.wait_ge(S_["x2T_lo"], NT * b + 2 * pair + 2)
                hi, lo = x2T
                for k in range(KD):
                    if k == KD - 1:
                        for kl in range(KD):
                            nc.tensor.matmul(SC[0:E, SC_TURN:], gateT[:, kl, 0, :], lo[:, kl, :], start=False, stop=False)
                    ins = nc.tensor.matmul(SC[0:2 * E, SC_TURN:], gateT[:, k].rearrange("p h e -> p (h e)"), hi[:, k, :],
                                           start=(k == 0), stop=(k == KD - 1))
                ins.then_inc(S_["scoresT_psum"], 1)

            def tail_back(b, pair):
                counted_waits(pe, (S_["scoresT_ready"], 2 * b + pair + 1))
                for i in range(2):
                    at = (2 * pair + i) * 2 * E
                    ins = nc.tensor.transpose(SC[:, at:at + 2 * E], scT[:, i * P:(i + 1) * P], ident[0:2 * E, 0:2 * E])
                ins.then_inc(S_["scores_psum"], 1)

            def tail_ranks(b):
                pe.wait_ge(S_["onehot_ready"], b + 1)
                for i in range(NT):
                    dst = SC[:, SC_RANK + i * E:SC_RANK + (i + 1) * E]
                    for before in range(i):
                        nc.tensor.matmul(dst, ones[:], onehot[:, before, :], start=(before == 0), stop=False)
                    nc.tensor.matmul(dst, tri[:], onehot[:, i, :], start=(i == 0), stop=True)
                for i in range(NT):
                    ins = nc.tensor.matmul(SC[:, SC_COUNT:SC_COUNT + E], ones[:], onehot[:, i, :],
                                           start=(i == 0), stop=(i == NT - 1))
                ins.then_inc(S_["rank_psum"], 1)

            def power(k):
                return [h[:, POWERS.index(k), :] for h in AT]

            def inside(b, k):
                o = 2 ** k
                pe.wait_ge(S_["scan_lo"], NSTEP * b + 1 + k)
                mm3(SA[:, o * CW:], power(o), [h[:, 0:(J - o) * CW] for h in zp]).then_inc(S_["scan_psum"], 1)

            def over(b, l):
                o = LEVELS[l]
                pe.wait_ge(S_["scan_lo"], NSTEP * b + 1 + KIN + l)
                if l == 0:
                    wait(pe, S_["carry_ready"], 3 * b)
                mm3(SA[:, o * NB:EC], power(J * o), [h[:, 0:(CH + 1 - o) * NB] for h in endp]
                    ).then_inc(S_["scan_psum"], 1)

            def down(b):
                pe.wait_ge(S_["scan_lo"], NSTEP * (b + 1))
                for j in range(J):
                    ins = mm3(SA[:, j * CW:(j + 1) * CW], power(j + 1), [h[:, 0:CW] for h in endp])
                ins.then_inc(S_["down_psum"], 1)

            def body(b):
                tail = not (isinstance(b, int) and b == 0)
                free = ((S_["h_sum"], b), (S_["x2T_lo"], NT * (b - 1)), (S_["run_ready"], b - 1), (S_["g_sum"], NT * b))
                for i in range(NT):
                    pe.wait_ge(S_["xn_ready"], NT * b + i + 1)
                    wait(pe, *free[i])
                    for k in range(KD):
                        ins = nc.tensor.transpose(XT_BANKS[i][:, k * P:(k + 1) * P],
                                                  xn[:, i, k * P:(k + 1) * P], ident[:])
                    ins.then_inc(S_["xT_psum"], 1)
                if tail:
                    y_state(b - 1)
                pe.wait_ge(S_["xT_lo"], NT * b + 2)
                for m in range(KH):
                    pe.wait_ge(S_["xT_hi"], NT * (b + 1))
                    for k in range(KD):
                        for h in s1T:
                            nc.tensor.matmul((TP, G)[m][:], h[:, k, m * P:(m + 1) * P], xT[0][:, k, :],
                                             start=(k == 0 and h is s1T[0]), stop=False)
                    pe.wait_ge(S_["xT_lo"], NT * (b + 1))
                    for k in range(KD):
                        ins = nc.tensor.matmul((TP, G)[m][:], s1T[0][:, k, m * P:(m + 1) * P], xT[1][:, k, :],
                                               start=False, stop=(k == KD - 1))
                    ins.then_inc(S_["s1_psum"], 1)
                for k in range(KD):
                    ins = mm3(SA[:], [h[:, k, :] for h in BwT], [h[:, k, :] for h in xT],
                              first=(k == 0), last=(k == KD - 1))
                ins.then_inc(S_["bt_psum"], 1)
                y_dense(b, 0, 0)
                y_dense(b, 0, 1)
                pe.wait_ge(S_["silu_lo"], KH * (b + 1))
                for m in range(KH):
                    ins = mm3(SC[:], [h[:, m, :] for h in s2T], [h[:, m, :] for h in sT],
                              first=(m == 0), last=(m == KH - 1))
                ins.then_inc(S_["s2_psum"], 1)
                y_dense(b, 1, 0)
                if tail:
                    tail_turn(b - 1, 0)
                y_dense(b, 1, 1)
                if isinstance(b, int) and b == 0:
                    pe.wait_ge(S_["pow_lo"], 1)
                inside(b, 0)
                gates(b, 0, 0)
                if tail:
                    tail_turn(b - 1, 1)
                inside(b, 1)
                gates(b, 0, 1)
                over(b, 0)
                y_dense(b, 2, 0)
                if tail:
                    tail_scores(b - 1, 0)
                    tail_turn(b - 1, 2)
                over(b, 1)
                y_dense(b, 2, 1)
                over(b, 2)
                gates(b, 1, 0)
                if tail:
                    tail_turn(b - 1, 3)
                    tail_back(b - 1, 0)
                over(b, 3)
                gates(b, 1, 1)
                over(b, 4)
                y_dense(b, 3, 0)
                if tail:
                    tail_scores(b - 1, 1)
                over(b, 5)
                gates(b, 2, 0)
                if tail:
                    tail_back(b - 1, 1)
                over(b, 6)
                gates(b, 2, 1)
                down(b)
                y_dense(b, 3, 1)
                gates(b, 3, 0)
                if tail:
                    tail_ranks(b - 1)
                gates(b, 3, 1)

            body(0)
            body(1)
            with pe.Fori(2, NBLK) as b:
                body(b)

            def experts(first, end):
                for n in range(first, end):
                    e, k = n // KD, n % KD
                    pe.wait_ge(raw_loaded[e % RING], RAW_NEED[e % RING] + 16 * (e // RING + 1))
                    if n >= NEB and by_pool(n - NEB):
                        pe.wait_ge(S_["expert_full"], pool_count(n - NEB) + 1)
                    elif n >= NEB:
                        pe.wait_ge(S_["expert_lo"], dve_count(n - NEB) + 1)
                    for f in range(KD):
                        ins = nc.tensor.transpose(EBANKS[n % NEB][:, f * P:(f + 1) * P],
                                                  raw[:, e % RING, f, k * P:(k + 1) * P], ident[:])
                    ins.then_inc(S_["expert_turned"], 1)

            y_state(LASTB)
            pe.wait_ge(S_["g_sum"], NT * NBLK)
            pe.wait_ge(S_["h_sum"], NBLK)
            pe.wait_ge(S_["yg_ready"], NT * NBLK)
            pe.wait_ge(S_["biased"], NT * NBLK)
            experts(0, E_STEPS[0])
            for pair in range(2):
                tail_turn(LASTB, 2 * pair)
                tail_turn(LASTB, 2 * pair + 1)
                experts(E_STEPS[pair], E_STEPS[pair + 1])
                tail_scores(LASTB, pair)
                if pair == 1:
                    experts(E_STEPS[2], E_STEPS[3])
                tail_back(LASTB, pair)
            tail_ranks(LASTB)
            experts(E_STEPS[3], NE)
            pe.wait_ge(S_["expert_lo"], dve_count(NE))
            pe.wait_ge(S_["expert_lo_pool"], pool_count(NE))
            pe.wait_ge(S_["run_ready"], NBLK)
            pe.wait_ge(S_["expert_table"], 1)
            flat = [h[:].rearrange("p e k f -> p (e k f)") for h in We]

            def slot_turn(s, m):
                bank = (TP, SC)[m % 2]
                pe.wait_ge(S_["slot_norm"], s + 1)
                wait(pe, S_["slot_lo"], s - 1)
                for k in range(KD):
                    ins = nc.tensor.transpose(bank[:, k * P:(k + 1) * P], rnorm[m][:, k * P:(k + 1) * P], ident[:])
                ins.then_inc(S_["slot_turned"], 1)

            def slot_product(s, m):
                first = pe.value_load(slot_expert[0:1, bass.ds(s, 1)], min_val=0, max_val=(E - 1) * KD * D)
                pe.wait_ge(S_["slot_lo"], s + 1)
                wait(pe, S_["slot_result"], s - 1)
                for k in range(KD):
                    for a, w in ((0, 0), (0, 1), (1, 0)):
                        ins = nc.tensor.matmul(Y[m % 2][:], x2T[a][:, k, m % 2 * P:(m % 2 + 1) * P], flat[w][:, bass.ds(first + k * D, D)],
                                               start=(k == 0 and a == 0 and w == 0), stop=(k == KD - 1 and a == 1))
                ins.then_inc(S_["slot_psum"], 1)

            def slot(s, m):
                slot_turn(s, m)
                if not (isinstance(s, int) and s == 0):
                    slot_product(s - 1, (m - 1) % M)

            for m in range(M):
                slot(m, m)
            with pe.Fori(1, FULL) as u:
                for m in range(M):
                    slot(u * M + m, m)
            for s in range(FULL * M, SLOTS):
                slot(s, s % M)
            slot_product(SLOTS - 1, (SLOTS - 1) % M)


_INS = ["x", "A", "B_w", "B_b", "C_w", "C_b", "D_w", "D_b", "s_w1", "s_b1", "s_w2", "s_b2", "g_w", "g_b"]
_NAMES = ["L0_attn_" + n for n in _INS] + ["L0_ffn_gate_w", "L0_ffn_expert_w"]


def kernel(**inputs):
    import numpy as np
    import concourse.bacc as bacc
    from concourse.bass_utils import run_bass_kernel_spmd

    nc = bacc.Bacc("TRN2", target_bir_lowering=False, num_devices=1)
    arrays, args = {}, []
    for name in _NAMES:
        a = np.ascontiguousarray(inputs[name])
        arrays[name] = a
        args.append(nc.dram_tensor(name, a.shape, mybir.dt.from_np(a.dtype), kind="ExternalInput").ap())
    shape = arrays["L0_attn_x"].shape
    args.append(nc.dram_tensor("out", shape, mybir.dt.float32, kind="ExternalOutput").ap())
    preln_ssm_moe_kernel(nc, *args)
    r = run_bass_kernel_spmd(nc, [arrays], core_ids=[0])
    return r.results[0]["out"]
```

```python
import concourse.bass as bass
from concourse import mybir
from contextlib import ExitStack


def preln_ssm_moe_kernel(nc, x, A, B_w, B_b, C_w, C_b, D_w, D_b, s_w1, s_b1, s_w2, s_b2, g_w, g_b,
                         gate_w, expert_w, out):
    f32, f32r, bf16, i32 = mybir.dt.float32, mybir.dt.float32r, mybir.dt.bfloat16, mybir.dt.int32
    ALU, ACT, AX = mybir.AluOpType, mybir.ActivationFunctionType, mybir.AxisListType

    P = 128
    NB, S, D = x.shape
    NS = A.shape[0]
    DH = s_w1.shape[0]
    E = expert_w.shape[0]
    KD, KH = D // P, DH // P
    EPS = 1e-5
    TB = 512
    SB = TB // NB
    NT = TB // P
    NBLK = NB * S // TB
    LASTB = NBLK - 1
    J = 2
    PAIRS = SB // J
    CW = PAIRS * NB
    CH = PAIRS // 2
    CHUNK = 2 * J
    LEVELS = [2 ** i for i in range((CH - 1).bit_length())]
    NSTEP = 3 + len(LEVELS) + 1
    POWERS = [1, J] + [CHUNK * o for o in LEVELS]
    RW = D + 4
    MEAN, RSTD, TID = D, D + 1, D + 2
    REG = NB * S + P
    DUMMY = E * REG
    SLOTS = NB * S // P + E - 1
    OOB = NB * S
    RING = 3
    M = 4
    FULL = SLOTS // M
    EARLY = ((NBLK - 2) * TB // P - (E - 1)) // M
    FIRST = EARLY * M
    TABLE = max(FIRST, SLOTS - FIRST)
    SC_RANK, SC_COUNT, SC_TURN = 2 * NT * E, 3 * NT * E, 2 * P

    x_t = [x[n].rearrange("(b t p) d -> b p t d", t=SB // P, p=P) for n in range(NB)]
    out_rows = out.rearrange("n s d -> (n s) d")
    routed = nc.dram_tensor("routed_rows", (DUMMY + P, RW), f32, kind="Internal").ap()

    def wait(eng, sem, value):
        if not isinstance(value, int) or value > 0:
            eng.wait_ge(sem, value)

    with ExitStack() as keep:
        def psum(name):
            return keep.enter_context(nc.psum_tensor(name, [P, 512], f32))

        def sem(name):
            return keep.enter_context(nc.semaphore(name))

        def kb(name, shape, dt=f32):
            return keep.enter_context(nc.sbuf_tensor(name, shape, dt))

        Y = [psum(f"y{i}") for i in range(NT)]
        G, TP, SA, SC = psum("gates"), psum("turned"), psum("scan"), psum("scores")
        XT_BANKS = [SA, TP, SC, G]

        raw = kb("raw_weights", [P, RING, KD, D])
        ident = kb("ident", [P, P])
        tri, ones = kb("strictly_before", [P, P], bf16), kb("ones", [P, P], bf16)
        run = kb("list_ends", [P, E])
        e_iota = kb("expert_iota", [P, NT, E])
        end_rows = kb("list_end_rows", [1, E], i32)
        padrow = kb("padrow", [P, RW])
        gate = kb("gate", [P, NT, D])
        xrow = [kb(f"x1_rows{q}", [P, NT, RW]) for q in range(2)]
        xn2 = kb("x1_norm", [P, NT, D])
        x2T = kb("x1T_hi", [P, KD, 2 * P], f32r), kb("x1T_lo", [P, KD, 2 * P], f32r)
        scT = kb("scoresT", [2 * E, 2 * P])
        gateT = kb("gateT", [P, KD, 2, E], f32r)
        endp = kb("chunk_ends", [P, CH, 2, NB], f32r)
        carried = kb("carried_state", [P, NB])
        st1, st2 = kb("ln1_stats", [P, NT, 6]), kb("ln2_stats", [P, NT, 6])
        mv1, mv2 = kb("ln1_mean_var", [P, NT, 2]), kb("ln2_mean_var", [P, NT, 2])
        ve1, ve2 = kb("ln1_var_eps", [P, NT]), kb("ln2_var_eps", [P, NT])
        rs1, mhalf = kb("ln1_rstd", [P, NT]), kb("minus_half", [P, NT])
        scores = kb("score_sums", [P, NT, E])
        top, best, bounded = kb("top_score", [P, NT]), kb("best", [P, NT]), kb("best_bounded", [P, NT])
        hit, cand = kb("is_top", [P, NT, E]), kb("candidate", [P, NT, E])
        onehot = kb("onehot", [P, NT + 1, E], bf16)
        pos, picked = kb("list_position", [P, NT, E]), kb("picked_position", [P, NT, E])
        dest_f = kb("dest_f", [P, NT])
        dest = [kb(f"dest{q}", [P, NT], i32) for q in range(2)]
        ids = [kb(f"ids{m}", [P, 1], i32) for m in range(M)]
        count, tiles_f, cum, gap = kb("list_count", [1, E]), kb("list_tiles", [1, E]), kb("tiles_upto", [1, E]), kb("list_gap", [1, E])
        tiles_i, tiles_s, zeros = kb("list_tiles_i", [1, E], i32), kb("list_tiles_s", [1, E], i32), kb("zeros_row", [1, E])
        taken = kb("tiles_taken", [1, E + 1])
        upto, before, shift = kb("taken_upto", [1, E]), kb("taken_before", [1, E]), kb("taken_shift", [1, E])
        slot_iota = kb("slot_iota", [1, TABLE])
        past, past_gap = kb("slot_past", [1, TABLE, E]), kb("slot_past_gap", [1, TABLE, E])
        slot_e, slot_r, slot_r2 = kb("slot_expert_f", [1, TABLE]), kb("slot_row_f", [1, TABLE]), kb("slot_row_sum", [1, TABLE])
        slot_at = kb("slot_place", [1, TABLE])
        slot_expert, slot_row = kb("slot_expert", [1, SLOTS], i32), kb("slot_row", [1, SLOTS], i32)
        rows = [xrow[0][:, m, :] for m in range(M)]
        rnorm = [xn2[:, m, :] for m in range(M)]
        res = [gate[:, m, :] for m in range(M)]

        with ExitStack() as main:
            def sb(name, shape, dt=f32):
                return main.enter_context(nc.sbuf_tensor(name, shape, dt))

            def pair(name, shape):
                return sb(name + "_hi", shape, f32r), sb(name + "_lo", shape, f32r)

            DwT, GwT = pair("DwT", [P, KD, D]), pair("GwT", [P, KD, D])
            s1T, s2T = pair("s1T", [P, KD, DH]), pair("s2T", [P, KH, NS])
            BwT, CwT = pair("BwT", [P, KD, NS]), pair("CwT", [P, D])
            AT = pair("A_powers", [P, len(POWERS), NS])
            xin, xn = sb("x_in", [P, NT, D]), sb("x_norm", [P, NT, D])
            xT = pair("xT", [P, KD, TB])
            bias_y, bias_g = sb("y_bias", [P, D]), sb("g_bias", [P, D])
            gbias = [sb(f"gated_bias{q}", [P, D]) for q in range(2)]
            b1, b2, bB = sb("s_b1_col", [P, KH]), sb("s_b2_col", [P, 1]), sb("B_b_col", [P, 1])
            silu = sb("silu", [P, KH, TB])
            sT = pair("siluT", [P, KH, TB])
            sel = sb("select", [P, TB])
            z = sb("z", [P, J, PAIRS, NB])
            zp = pair("z_half", [P, CW])
            hT = pair("hT", [P, TB])
        with ExitStack() as later:
            We = [later.enter_context(nc.sbuf_tensor("expert" + h, [P, E, KD, D], f32r)) for h in ("_hi", "_lo")]
        first_of, last_of = (z[:, j].rearrange("p c n -> p (c n)") for j in range(J))
        middle, end = (z[:, J - 1].rearrange("p (c a) n -> p a c n", a=2)[:, a] for a in range(2))
        powT, powP = xn2[:].rearrange("p t d -> p (t d)"), gate[:].rearrange("p t d -> p (t d)")
        bias_c = gbias[0]
        raw_C, raw_A, raw_gate = powT[:, 10 * NS:14 * NS], powT[:, 14 * NS:15 * NS], powP[0:E, 8 * NS:8 * NS + D]

        S_ = {}
        for name in ("bias_loaded cols_loaded A_loaded s1_loaded aux_loaded xin_loaded consts_made consts2_made pad_made ident_made "
                     "bias_sum w_turned w_hi w_lo pow_psum pow_copied pow_hi pow_lo "
                     "stats1 mv1_ready ve1_ready rstd1_ready xn_ready xT_psum xT_hi xT_lo "
                     "s1_psum s1_sig silu_ready silu_hi silu_lo bt_psum s2_psum sel_ready "
                     "scan_psum scan_part scan_sum scan_hi scan_lo down_psum h_sum h_hi h_lo u_ready carry_ready "
                     "g_psum g_sum gate_ready bias_gated biased y_psum yg_ready x1_ready "
                     "stats2 mv2_ready ve2_ready rstd2_ready mean_copied xn2_ready x2T_psum x2T_hi x2T_lo "
                     "scoresT_psum scoresT_ready scores_psum scores_ready top_ready sig_warm hit_ready cand_ready best_ready bounded_ready onehot_ready "
                     "rank_psum pos_ready picked_ready run_ready destf_ready dest_ready ids_ready ends_ready pad_sent "
                     "expert_turned expert_hi expert_full expert_lo expert_lo_pool table_step slot_iota_made expert_table row_table "
                     "slot_norm slot_turned slot_hi slot_lo slot_psum slot_base slot_ids slot_result").split():
            S_[name] = sem(name)
        raw_loaded = [sem(f"raw_loaded{r}") for r in range(RING)]
        xres_loaded = [sem("xres_loaded_even"), sem("xres_loaded_odd")]
        rows_sent = [sem("rows_sent_even"), sem("rows_sent_odd")]
        row_loaded = [sem(f"row_loaded{m}") for m in range(M)]
        out_sent = [sem(f"out_sent{m}") for m in range(M)]

        def counted_waits(eng, *waits):
            waits = [(sem, v if isinstance(v, int) else eng.to_reg(v)) for sem, v in waits]
            eng.wait_ge(S_["ident_made"], 1)
            for sem, v in waits:
                wait(eng, sem, v)

        def by_block(bank):
            return bank[:].rearrange("p (k t) -> p k t", k=KD)

        def token_order(t):
            return t[:].rearrange("p (n c j) -> p j c n", n=NB, j=J)

        JOBS = []
        for k in range(KD):
            JOBS.append(([(raw[:, 0, f, k * P:(k + 1) * P], f * P, P) for f in range(KH)], DH,
                         [h[:, k, :] for h in s1T]))
        JOBS.append(([(raw[:, 0, 2, k * P:(k + 1) * P], k * NS, P) for k in range(KD)], KD * NS,
                     [h[:].rearrange("p k n -> p (k n)") for h in BwT]))
        JOBS.append(([(raw[:, 0, 3, k * P:(k + 1) * P], k * NS, P) for k in range(KH)], KH * NS,
                     [h[:].rearrange("p k n -> p (k n)") for h in s2T]))
        for r, w in ((1, DwT), (2, GwT)):
            for k in range(KD):
                JOBS.append(([(raw[:, r, f, k * P:(k + 1) * P], f * P, P) for f in range(KD)], D,
                             [h[:, k, :] for h in w]))
        JOBS.append(([(raw_C[:, f * P:(f + 1) * P], f * P, P) for f in range(KD)], D, [h[:] for h in CwT]))
        JOBS.append(([(raw_gate[:, k * P:(k + 1) * P], k * E, E) for k in range(KD)], KD * E,
                     [gateT[:, :, h, :] for h in range(2)]))
        RAW_NEED = [32, 16, 16]
        PREP_BANKS, POW_BANK = Y[:NT - 1], Y[NT - 1]
        JOB_LOAD = ([(S_["s1_loaded"], 16)] * KD + [(raw_loaded[0], RAW_NEED[0])] * 2
                    + [(raw_loaded[r], RAW_NEED[r]) for r in (1, 2) for _ in range(KD)] + [(S_["aux_loaded"], 32)] * 2)

        def job_view(j):
            _, n, dst = JOBS[j]
            bank = PREP_BANKS[j % len(PREP_BANKS)][:, 0:n]
            return bank.rearrange("p (k e) -> p k e", e=E) if len(dst[0].shape) == 3 else bank

        PK = [1] + [2 ** i for i in range(1, POWERS[-1].bit_length() - 1)]

        def tslot(k):
            i = POWERS.index(k)
            return powT[:, i * NS:(i + 1) * NS]

        def pslot(k):
            i = PK.index(k)
            return raw_A if k == 1 else powP[:, i * NS:(i + 1) * NS]

        ROUNDS = [[("T", 1, 0, 0)], [("T", 2, 1, 1), ("P", 2, 1, 1)],
                  [("T", 4, 2, 2), ("P", 4, 2, 2)]]
        for k in PK[2:]:
            ROUNDS.append([("T", 2 * k, k, k)] + ([("P", 2 * k, k, k)] if 2 * k in PK else []))

        COPIED = [sum(len(done) for done in ROUNDS[:n]) for n in range(len(ROUNDS) + 1)]

        STAGES = [[("pow", 0), ("pow", 1), ("pow", 2), ("job", 0), ("pow", 3), ("job", 1), ("job", 2), ("pow", 4)]
                  + [("job", j) for j in range(3, 6)]]
        for j in range(6, len(JOBS), 3):
            STAGES.append([("job", n) for n in range(j, min(j + 3, len(JOBS)))]
                          + [("pow", n) for n in (len(STAGES) + 4,) if n < len(ROUNDS)])

        EBANKS = [G] + Y
        NE = E * KD
        NEB = len(EBANKS)
        E_STEPS = [9, 12, 16, 18, 21, 28]
        POOL_PIECES = [0, 1, 2, 3, 4, 8, 9, 12, 15, 16, 17, 18, 22, 26]

        def by_pool(n):
            return n in POOL_PIECES

        def pool_count(n):
            return sum(map(by_pool, range(n)))

        def dve_count(n):
            return n - pool_count(n)

        def turn_bank(b, i):
            return SA if isinstance(b, int) and b == LASTB and i % 2 else TP

        block = keep.enter_context(nc.Block())

        def load_expert(eng, e):
            eng.dma_start(raw[:, e % RING], expert_w[e].rearrange("(f p) d -> p f d", p=P)
                          ).then_inc(raw_loaded[e % RING], 16)

        @block.sync
        def _(sp):
            def load_x(b):
                wait(sp, S_["xn_ready"], NT * b)
                for n in range(NB):
                    sp.dma_start(xin[:, 2 * n:2 * n + 2, :], x_t[n][b] if isinstance(b, int)
                                 else x_t[n][bass.ds(b, 1)].rearrange("o p t d -> p (o t) d")
                                 ).then_inc(S_["xin_loaded"], 16)

            def load_residual(b, q, turn):
                wait(sp, rows_sent[q], 16 * NT * turn)
                for n in range(NB):
                    sp.dma_start(xrow[q][:, 2 * n:2 * n + 2, 0:D], x_t[n][b] if isinstance(b, int)
                                 else x_t[n][bass.ds(b, 1)].rearrange("o p t d -> p (o t) d")
                                 ).then_inc(xres_loaded[q], 16)

            load_x(0)
            sp.dma_start(raw[:, 0, 0:KH], s_w1.rearrange("(f p) d -> p f d", p=P)).then_inc(S_["s1_loaded"], 16)
            sp.dma_start(raw[:, 0, 2], B_w).then_inc(raw_loaded[0], 16)
            sp.dma_start(raw[:, 0, 3, 0:DH], s_w2).then_inc(raw_loaded[0], 16)
            for m in range(KH):
                sp.dma_start(b1[:, m:m + 1], s_b1[m * P:(m + 1) * P].unsqueeze(1)).then_inc(S_["cols_loaded"], 16)
            sp.dma_start(b2[:], s_b2.unsqueeze(1)).then_inc(S_["cols_loaded"], 16)
            sp.dma_start(bB[:], B_b.unsqueeze(1)).then_inc(S_["cols_loaded"], 16)
            sp.dma_start(raw[:, 1], D_w.rearrange("(f p) d -> p f d", p=P)).then_inc(raw_loaded[1], 16)
            sp.dma_start(raw[:, 2], g_w.rearrange("(f p) d -> p f d", p=P)).then_inc(raw_loaded[2], 16)
            sp.dma_start(raw_C.rearrange("p (f s) -> p f s", f=KD), C_w.rearrange("(f p) s -> p f s", p=P)
                         ).then_inc(S_["aux_loaded"], 16)
            sp.dma_start(raw_gate, gate_w).then_inc(S_["aux_loaded"], 16)
            for row, b in ((bias_y, D_b), (bias_c, C_b), (bias_g, g_b)):
                sp.dma_start(row[:], b.partition_broadcast(P)).then_inc(S_["bias_loaded"], 16)
            load_residual(0, 0, 0)
            load_x(1)
            load_residual(1, 1, 0)
            load_x(2)
            sp.wait_ge(S_["pad_made"], 1)
            sp.dma_start(routed[DUMMY:DUMMY + P, :], padrow[:]).then_inc(S_["pad_sent"], 16)
            sp.wait_ge(S_["w_turned"], len(JOBS))
            for e in range(RING):
                load_expert(sp, e)
            with sp.Fori(1, NBLK // 2 - 1) as t:
                load_x(t * 2 + 1)
                load_residual(t * 2, 0, t)
                load_x(t * 2 + 2)
                load_residual(t * 2 + 1, 1, t)
            load_x(LASTB)
            load_residual(LASTB - 1, 0, NBLK // 2 - 1)
            load_residual(LASTB, 1, NBLK // 2 - 1)
            sp.wait_ge(rows_sent[0], 16 * NT * (NBLK // 2))
            sp.wait_ge(rows_sent[1], 16 * NT * (NBLK // 2 - 1))
            sp.wait_ge(S_["row_table"], 1)

            def load_slot(s, m):
                row = sp.value_load(slot_row[0:1, bass.ds(s, 1)], min_val=0, max_val=DUMMY)
                wait(sp, S_["slot_result"], s - M + 1)
                wait(sp, S_["slot_ids"], s - M + 1)
                sp.dma_start(rows[m], routed[bass.ds(row, P), :]).then_inc(row_loaded[m], 16)

            for m in range(M):
                load_slot(m, m)
            sp.wait_ge(S_["ends_ready"], 1)
            for e in range(E):
                end = sp.value_load(end_rows[0:1, e:e + 1], min_val=0, max_val=DUMMY - P)
                sp.dma_start(routed[bass.ds(end, P), :], padrow[:]).then_inc(S_["pad_sent"], 16)
            with sp.Fori(1, EARLY) as u:
                for m in range(M):
                    load_slot(u * M + m, m)
            sp.wait_ge(rows_sent[1], 16 * NT * (NBLK // 2))
            sp.wait_ge(S_["pad_sent"], 16 * (E + 1))
            sp.wait_ge(S_["row_table"], 2)
            with sp.Fori(EARLY, FULL) as u:
                for m in range(M):
                    load_slot(u * M + m, m)
            for s in range(FULL * M, SLOTS):
                load_slot(s, s % M)

        @block.gpsimd
        def _(pool):
            made = [nc.gpsimd.memset(mhalf[:], -0.5), nc.gpsimd.memset(ident[:], 0.0),
                    nc.gpsimd.memset(tri[:], 1.0), nc.gpsimd.memset(ones[:], 1.0),
                    nc.gpsimd.memset(padrow[:], 0.0),
                    nc.gpsimd.memset(xrow[0][:, :, D:RW], 0.0), nc.gpsimd.memset(xrow[1][:, :, D:RW], 0.0),
                    nc.gpsimd.memset(zeros[:], 0.0), nc.gpsimd.memset(onehot[:, NT, :], 0.0), nc.gpsimd.memset(taken[:], 0.0)]
            for ins in made:
                ins.then_inc(S_["consts_made"], 1)
            pool.wait_ge(S_["consts_made"], len(made))
            nc.gpsimd.affine_select(out=ident[:], in_=ident[:], compare_op=ALU.not_equal, fill=1.0, base=0,
                                    pattern=[[-1, P]], channel_multiplier=1).then_inc(S_["ident_made"], 1)
            nc.gpsimd.affine_select(out=tri[:], in_=tri[:], compare_op=ALU.is_gt, fill=0.0, base=0,
                                    pattern=[[1, P]], channel_multiplier=-1).then_inc(S_["consts2_made"], 1)
            for tile, pattern, mult in ((run[:], [[REG, E]], 0), (e_iota[:], [[0, NT], [1, E]], 0),
                                        (slot_iota[:], [[1, TABLE]], 0)):
                nc.gpsimd.iota(tile, pattern=pattern, base=0, channel_multiplier=mult,
                               allow_small_or_imprecise_dtypes=True).then_inc(S_["consts2_made"], 1)
            nc.gpsimd.memset(padrow[:].bitcast(i32)[:, TID:TID + 1], OOB).then_inc(S_["pad_made"], 1)
            for q in range(2):
                nc.gpsimd.iota(xrow[q][:].bitcast(i32)[:, :, TID].rearrange("p (n t) -> p n t", n=NB),
                               pattern=[[S, NB], [P, SB // P]], base=(q - 2) * SB,
                               channel_multiplier=1).then_inc(S_["ids_ready"], 1)

            def rstd1(b):
                counted_waits(pool, (S_["mv1_ready"], b + 1))
                nc.gpsimd.tensor_scalar(ve1[:], mv1[:, :, 1], EPS, None, ALU.add).then_inc(S_["ve1_ready"], 1)
                pool.wait_ge(S_["ve1_ready"], b + 1)
                wait(pool, S_["xn_ready"], NT * b)
                nc.gpsimd.tensor_tensor(rs1[:], ve1[:], mhalf[:], ALU.pow).then_inc(S_["rstd1_ready"], 1)

            def residual(b, q):
                for i in range(NT):
                    pool.wait_ge(S_["biased"], NT * b + i + 1)
                    pool.wait_ge(S_["yg_ready"], NT * b + i + 1)
                    nc.gpsimd.tensor_tensor(xrow[q][:, i, 0:D], xrow[q][:, i, 0:D], gate[:, i, :],
                                            ALU.add).then_inc(S_["x1_ready"], 1)

            def rstd2(b, q):
                row_i = xrow[q][:].bitcast(i32)[:, :, TID]
                counted_waits(pool, (S_["mv2_ready"], b + 1))
                nc.gpsimd.tensor_scalar(ve2[:], mv2[:, :, 1], EPS, None, ALU.add).then_inc(S_["ve2_ready"], 1)
                nc.gpsimd.tensor_copy(xrow[q][:, :, MEAN], mv2[:, :, 0]).then_inc(S_["mean_copied"], 1)
                pool.wait_ge(S_["ve2_ready"], b + 1)
                nc.gpsimd.tensor_tensor(xrow[q][:, :, RSTD], ve2[:], mhalf[:], ALU.pow).then_inc(S_["rstd2_ready"], 1)
                counted_waits(pool, (S_["ids_ready"], b + 2))
                nc.gpsimd.tensor_scalar(row_i, row_i, float(2 * SB), None, ALU.add).then_inc(S_["ids_ready"], 1)

            def scatter(b, q):
                counted_waits(pool, (S_["dest_ready"], b + 1), (S_["rstd2_ready"], b + 1),
                              (S_["mean_copied"], b + 1), (S_["ids_ready"], b + 3))
                for i in range(NT):
                    nc.gpsimd.indirect_dma_start(
                        out=routed, out_offset=bass.IndirectOffsetOnAxis(ap=dest[q][:, i:i + 1], axis=0),
                        in_=xrow[q][:, i, :], in_offset=None).then_inc(rows_sent[q], 16)

            def bias(b, q, turn, i):
                if i == 0:
                    pool.wait_ge(xres_loaded[q], 16 * NB * (turn + 1))
                if i == 0 and isinstance(b, int) and b == 0:
                    pool.wait_ge(S_["bias_sum"], 1)
                pool.wait_ge(S_["gate_ready"], NT * b + i + 1)
                wait(pool, S_["biased"], NT * b + i - 1)
                nc.gpsimd.tensor_tensor(gbias[i % 2][:], gate[:, i, :], bias_y[:], ALU.mult
                                        ).then_inc(S_["bias_gated"], 1)
                pool.wait_ge(S_["bias_gated"], NT * b + i + 1)
                nc.gpsimd.tensor_tensor(xrow[q][:, i, 0:D], xrow[q][:, i, 0:D], gbias[i % 2][:], ALU.add
                                        ).then_inc(S_["biased"], 1)

            def body(b, q, turn):
                if not (isinstance(b, int) and b == 0):
                    residual(b - 1, 1 - q)
                    rstd2(b - 1, 1 - q)
                if not (isinstance(b, int) and b < 2):
                    scatter(b - 2, q)
                if not (isinstance(b, int) and b == LASTB):
                    rstd1(b + 1)
                for i in range(NT):
                    bias(b, q, turn, i)

            rstd1(0)
            for b in range(3):
                body(b, b % 2, b // 2)
            with pool.Fori(1, NBLK // 2 - 1) as t:
                body(t * 2 + 1, 1, t)
                body(t * 2 + 2, 0, t + 1)
            body(LASTB, 1, NBLK // 2 - 1)

            def experts(first, end):
                for n in filter(by_pool, range(first, end)):
                    pool.wait_ge(S_["expert_hi"], n + 1)
                    pool.wait_ge(S_["expert_full"], pool_count(n) + 1)
                    hi, lo = We[0][:, n // KD, n % KD, :], We[1][:, n // KD, n % KD, :]
                    nc.gpsimd.tensor_tensor(lo, lo.bitcast(f32), hi.bitcast(f32), ALU.subtract
                                            ).then_inc(S_["expert_lo_pool"], 1)

            experts(0, 3)
            rstd2(LASTB, 1)
            scatter(LASTB - 1, 0)
            experts(3, E_STEPS[4])
            scatter(LASTB, 1)
            experts(E_STEPS[4], NE)

            def slot_base(s, m, turn):
                counted_waits(pool, (row_loaded[m], 16 * (turn + 1)), (out_sent[m], 16 * turn))
                nc.gpsimd.tensor_copy(ids[m][:], rows[m].bitcast(i32)[:, TID:TID + 1]).then_inc(S_["slot_ids"], 1)
                pool.wait_ge(S_["slot_norm"], s + 1)
                nc.gpsimd.tensor_tensor(rows[m][:, 0:D], rows[m][:, 0:D], rnorm[m], ALU.add
                                        ).then_inc(S_["slot_base"], 1)

            def slot_store(s, m):
                counted_waits(pool, (S_["slot_result"], s + 1), (S_["slot_ids"], s + 1))
                nc.gpsimd.indirect_dma_start(
                    out=out_rows, out_offset=bass.IndirectOffsetOnAxis(ap=ids[m][:, 0:1], axis=0),
                    in_=res[m], in_offset=None, bounds_check=OOB - 1, oob_is_err=False
                ).then_inc(out_sent[m], 16)

            def slot(s, m, turn):
                slot_base(s, m, turn)
                if not (isinstance(s, int) and s == 0):
                    slot_store(s - 1, (m - 1) % M)

            for m in range(M):
                slot(m, m, 0)
            with pool.Fori(1, FULL) as u:
                for m in range(M):
                    slot(u * M + m, m, u)
            for s in range(FULL * M, SLOTS):
                slot(s, s % M, FULL)
            slot_store(SLOTS - 1, (SLOTS - 1) % M)
            for m in range(M):
                pool.wait_ge(out_sent[m], 16 * len(range(m, SLOTS, M)))

        @block.scalar
        def _(act):
            act.dma_start(raw_A, A).then_inc(S_["A_loaded"], 16)
            act.wait_ge(S_["consts_made"], 1)
            nc.scalar.activation(sel[:, 0:1], mhalf[:, 0:1], ACT.Sigmoid).then_inc(S_["sig_warm"], 1)

            def prep(stage):
                for what, n in STAGES[stage]:
                    if what == "pow":
                        act.wait_ge(S_["pow_psum"], n + 1)
                        for i, (side, k, _, _) in enumerate(ROUNDS[n]):
                            nc.scalar.activation(tslot(k) if side == "T" else pslot(k),
                                                 POW_BANK[:, i * NS:(i + 1) * NS], ACT.Copy
                                                 ).then_inc(S_["pow_copied"], 1)
                    else:
                        act.wait_ge(S_["w_turned"], n + 1)
                        nc.scalar.activation(JOBS[n][2][0], job_view(n), ACT.Copy).then_inc(S_["w_hi"], 1)

            def powers_hi():
                act.wait_ge(S_["pow_copied"], COPIED[-1])
                nc.scalar.activation(AT[0][:].rearrange("p k s -> p (k s)"), powT[:, 0:len(POWERS) * NS],
                                     ACT.Copy).then_inc(S_["pow_hi"], 1)

            prep(0)
            act.wait_ge(S_["cols_loaded"], 16 * (KH + 2))

            def tail_hi(b, i):
                act.wait_ge(S_["x2T_psum"], NT * b + i + 1)
                nc.scalar.activation(x2T[0][:, :, i % 2 * P:(i % 2 + 1) * P], by_block(turn_bank(b, i)), ACT.Copy
                                     ).then_inc(S_["x2T_hi"], 1)

            def scoresT(b, pair):
                act.wait_ge(S_["scoresT_psum"], 2 * b + pair + 1)
                nc.scalar.activation(scT[:], SC[0:2 * E, SC_TURN:], ACT.Copy).then_inc(S_["scoresT_ready"], 1)

            def gates(b, i):
                act.wait_ge(S_["g_sum"], NT * b + i + 1)
                nc.scalar.activation(gate[:, i, :], gate[:, i, :], ACT.Sigmoid).then_inc(S_["gate_ready"], 1)

            def body(b):
                tail = not (isinstance(b, int) and b == 0)
                for i in range(NT):
                    act.wait_ge(S_["xT_psum"], NT * b + i + 1)
                    nc.scalar.activation(xT[0][:, :, i * P:(i + 1) * P], by_block(XT_BANKS[i]), ACT.Copy
                                         ).then_inc(S_["xT_hi"], 1)
                if not tail:
                    prep(1)
                for m in range(KH):
                    act.wait_ge(S_["s1_psum"], KH * b + m + 1)
                    wait(act, S_["silu_lo"], KH * (b - 1) + m + 1)
                    nc.scalar.activation(silu[:, m, :], (TP, G)[m][:], ACT.Sigmoid, bias=b1[:, m:m + 1]
                                         ).then_inc(S_["s1_sig"], 1)
                    if not tail:
                        prep(2 + m)
                    act.wait_ge(S_["silu_ready"], KH * b + m + 1)
                    nc.scalar.activation(sT[0][:, m, :], silu[:, m, :], ACT.Copy).then_inc(S_["silu_hi"], 1)
                if not tail:
                    prep(2 + KH)
                    powers_hi()
                act.wait_ge(S_["s2_psum"], b + 1)
                nc.scalar.activation(sel[:], SC[:], ACT.Sigmoid, bias=b2[:]).then_inc(S_["sel_ready"], 1)
                if tail:
                    tail_hi(b - 1, 0)
                    tail_hi(b - 1, 1)
                    scoresT(b - 1, 0)
                    tail_hi(b - 1, 2)
                gates(b, 0)
                if tail:
                    tail_hi(b - 1, 3)
                    scoresT(b - 1, 1)
                gates(b, 1)
                act.wait_ge(S_["h_sum"], b + 1)
                nc.scalar.activation(token_order(hT[0]), z[:], ACT.Copy).then_inc(S_["h_hi"], 1)
                gates(b, 2)
                gates(b, 3)

            body(0)
            body(1)
            with act.Fori(2, NBLK) as b:
                body(b)

            def experts(first, end):
                for n in range(first, end):
                    act.wait_ge(S_["expert_turned"], n + 1)
                    nc.scalar.activation(We[0][:, n // KD, n % KD, :], EBANKS[n % NEB][:], ACT.Copy
                                         ).then_inc(S_["expert_hi"], 1)
                    if by_pool(n):
                        nc.scalar.activation(We[1][:, n // KD, n % KD, :].bitcast(f32), EBANKS[n % NEB][:], ACT.Copy
                                             ).then_inc(S_["expert_full"], 1)
                    if n % KD == KD - 1 and n // KD + RING < E:
                        load_expert(act, n // KD + RING)

            experts(0, E_STEPS[0])
            for pair in range(2):
                tail_hi(LASTB, 2 * pair)
                tail_hi(LASTB, 2 * pair + 1)
                experts(E_STEPS[pair], E_STEPS[pair + 1])
                scoresT(LASTB, pair)
            experts(E_STEPS[2], E_STEPS[5])

            def slot_hi(s, q):
                act.wait_ge(S_["slot_turned"], s + 1)
                wait(act, S_["slot_psum"], s - 1)
                nc.scalar.activation(x2T[0][:, :, q * P:(q + 1) * P], by_block((TP, SC)[q]), ACT.Copy).then_inc(S_["slot_hi"], 1)

            slot_hi(0, 0)
            experts(E_STEPS[5], NE)
            for s in range(1, M):
                slot_hi(s, s % 2)
            with act.Fori(1, FULL) as u:
                for m in range(M):
                    slot_hi(u * M + m, m % 2)
            for s in range(FULL * M, SLOTS):
                slot_hi(s, s % 2)

        @block.vector
        def _(dve):
            def ln1_stats(b, i):
                if i == 0:
                    dve.wait_ge(S_["xin_loaded"], 16 * NB * (b + 1))
                nc.vector.bn_stats(st1[:, i, :], xin[:, i, :]).then_inc(S_["stats1"], 1)

            def ln1_mv(b):
                counted_waits(dve, (S_["stats1"], NT * (b + 1)), (S_["rstd1_ready"], b))
                for i in range(NT):
                    ins = nc.vector.bn_aggr(mv1[:, i, :], st1[:, i, :])
                ins.then_inc(S_["mv1_ready"], 1)

            def normalise1(b, first=0, end=NT):
                dve.wait_ge(S_["rstd1_ready"], b + 1)
                dve.wait_ge(S_["mv1_ready"], b + 1)
                wait(dve, S_["xT_psum"], NT * b)
                for i in range(first, end):
                    nc.vector.tensor_scalar(xn[:, i, :], xin[:, i, :], mv1[:, i, 0:1], rs1[:, i:i + 1],
                                            ALU.subtract, ALU.mult).then_inc(S_["xn_ready"], 1)

            def prep(stage):
                for n in [n for what, n in STAGES[stage] if what == "job"]:
                    if n == 0:
                        for i in range(NT):
                            ln1_stats(0, i)
                        ln1_mv(0)
                    if n == 3:
                        normalise1(0)
                    dve.wait_ge(S_["w_hi"], n + 1)
                    hi, lo = JOBS[n][2]
                    nc.vector.tensor_tensor(lo, job_view(n), hi.bitcast(f32), ALU.subtract).then_inc(S_["w_lo"], 1)

            def powers_lo():
                dve.wait_ge(S_["pow_hi"], 1)
                nc.vector.tensor_tensor(AT[1][:].rearrange("p k s -> p (k s)"), powT[:, 0:len(POWERS) * NS],
                                        AT[0][:].rearrange("p k s -> p (k s)").bitcast(f32),
                                        ALU.subtract).then_inc(S_["pow_lo"], 1)

            prep(0)

            def split(hi, lo, src, n):
                dve.wait_ge(S_["scan_sum"], n)
                nc.vector.tensor_copy(hi, src).then_inc(S_["scan_hi"], 1)
                dve.wait_ge(S_["scan_hi"], n)
                nc.vector.tensor_tensor(lo, src, hi.bitcast(f32), ALU.subtract).then_inc(S_["scan_lo"], 1)

            def add_both(states, b, step, o):
                both = SA[:, 0:2 * (CH - o) * NB].rearrange("p (c h n) -> p h c n", h=2, n=NB)
                dve.wait_ge(S_["scan_psum"], (NSTEP - 1) * b + step)
                nc.vector.tensor_tensor(states, both[:, 0], states, ALU.add).then_inc(S_["scan_part"], 1)
                dve.wait_ge(S_["scan_part"], (NSTEP - 2) * b + step - 1)
                nc.vector.tensor_tensor(states, both[:, 1], states, ALU.add).then_inc(S_["scan_sum"], 1)

            def to_pairs(b):
                n = NSTEP * b + 2
                dve.wait_ge(S_["scan_psum"], (NSTEP - 1) * b + 1)
                nc.vector.tensor_tensor(last_of, SA[:, 0:CW], last_of, ALU.add).then_inc(S_["scan_sum"], 1)
                split(endp[:, :, 0, :], endp[:, :, 1, :], middle, n)

            def to_chunks(b):
                add_both(end, b, 2, 0)
                split(endp[:, :, 0, :], endp[:, :, 1, :], end, NSTEP * b + 3)

            def over(b, l):
                o = LEVELS[l]
                add_both(end[:, o:], b, 3 + l, o)
                split(endp[:, o:, 0, :], endp[:, o:, 1, :], end[:, o:], NSTEP * b + 4 + l)

            def to_middles(b):
                add_both(middle[:, 1:], b, NSTEP - 1, 1)
                split(zp[0][:], zp[1][:], last_of, NSTEP * (b + 1))

            def gate_sum(b, i):
                dve.wait_ge(S_["g_psum"], NT * b + i + 1)
                wait(dve, S_["x1_ready"], NT * (b - 1) + i + 1)
                nc.vector.tensor_tensor(gate[:, i, :], G[:], bias_g[:], ALU.add).then_inc(S_["g_sum"], 1)

            def gated(b):
                for i in range(NT):
                    dve.wait_ge(S_["y_psum"], NT * b + i + 1)
                    dve.wait_ge(S_["bias_gated"], NT * b + i + 1)
                    nc.vector.tensor_tensor(gate[:, i, :], Y[i][:], gate[:, i, :], ALU.mult
                                            ).then_inc(S_["yg_ready"], 1)

            def ln2_stats(b, q, i):
                dve.wait_ge(S_["x1_ready"], NT * b + i + 1)
                nc.vector.bn_stats(st2[:, i, :], xrow[q][:, i, 0:D]).then_inc(S_["stats2"], 1)

            def ln2_mv(b):
                counted_waits(dve, (S_["stats2"], NT * (b + 1)), (S_["rstd2_ready"], b), (S_["mean_copied"], b))
                for i in range(NT):
                    ins = nc.vector.bn_aggr(mv2[:, i, :], st2[:, i, :])
                ins.then_inc(S_["mv2_ready"], 1)

            def normalise2(b, q, first=0, end=NT):
                dve.wait_ge(S_["rstd2_ready"], b + 1)
                dve.wait_ge(S_["mean_copied"], b + 1)
                wait(dve, S_["x2T_psum"], NT * b)
                for i in range(first, end):
                    nc.vector.tensor_scalar(xn2[:, i, :], xrow[q][:, i, 0:D], xrow[q][:, i, MEAN:MEAN + 1],
                                            xrow[q][:, i, RSTD:RSTD + 1], ALU.subtract, ALU.mult
                                            ).then_inc(S_["xn2_ready"], 1)

            def tail_lo(b, i):
                dve.wait_ge(S_["x2T_hi"], NT * b + i + 1)
                hi, lo = [h[:, :, i % 2 * P:(i % 2 + 1) * P] for h in x2T]
                nc.vector.tensor_tensor(lo, by_block(turn_bank(b, i)), hi.bitcast(f32), ALU.subtract
                                        ).then_inc(S_["x2T_lo"], 1)

            def choose(b):
                dve.wait_ge(S_["scores_psum"], 2 * b + 2)
                nc.vector.tensor_reduce(scores[:], SC[:, 0:SC_RANK].rearrange("p (t h e) -> p t e h", h=2, e=E),
                                        AX.X, ALU.add).then_inc(S_["scores_ready"], 1)
                dve.wait_ge(S_["scores_ready"], b + 1)
                nc.vector.tensor_reduce(top[:], scores[:], AX.X, ALU.max).then_inc(S_["top_ready"], 1)
                dve.wait_ge(S_["top_ready"], b + 1)
                nc.vector.tensor_tensor(hit[:], scores[:], top[:].unsqueeze(2).to_broadcast([P, NT, E]), ALU.is_ge
                                        ).then_inc(S_["hit_ready"], 1)
                dve.wait_ge(S_["hit_ready"], b + 1)
                nc.vector.scalar_tensor_tensor(cand[:], hit[:], -float(E), e_iota[:], ALU.mult, ALU.add
                                               ).then_inc(S_["cand_ready"], 1)
                dve.wait_ge(S_["cand_ready"], b + 1)
                nc.vector.tensor_reduce(best[:], cand[:], AX.X, ALU.min).then_inc(S_["best_ready"], 1)
                dve.wait_ge(S_["best_ready"], b + 1)
                nc.vector.tensor_scalar(bounded[:], best[:], -1.0, float(E), ALU.min, ALU.add
                                        ).then_inc(S_["bounded_ready"], 1)
                dve.wait_ge(S_["bounded_ready"], b + 1)
                nc.vector.tensor_tensor(onehot[:, 0:NT, :], e_iota[:], bounded[:].unsqueeze(2).to_broadcast([P, NT, E]),
                                        ALU.is_equal).then_inc(S_["onehot_ready"], 1)

            def place(b, q, turn):
                ranks = SC[:, SC_RANK:SC_RANK + NT * E].rearrange("p (t e) -> p t e", e=E)
                dve.wait_ge(S_["rank_psum"], b + 1)
                wait(dve, S_["run_ready"], b)
                nc.vector.tensor_tensor(pos[:], ranks, run[:].unsqueeze(1).to_broadcast([P, NT, E]), ALU.add
                                        ).then_inc(S_["pos_ready"], 1)
                dve.wait_ge(S_["pos_ready"], b + 1)
                nc.vector.tensor_tensor(picked[:], pos[:], onehot[:, 0:NT, :], ALU.mult).then_inc(S_["picked_ready"], 1)
                nc.vector.tensor_tensor(run[:], SC[:, SC_COUNT:SC_COUNT + E], run[:], ALU.add
                                        ).then_inc(S_["run_ready"], 1)
                dve.wait_ge(S_["picked_ready"], b + 1)
                nc.vector.tensor_reduce(dest_f[:], picked[:], AX.X, ALU.add).then_inc(S_["destf_ready"], 1)
                dve.wait_ge(S_["destf_ready"], b + 1)
                wait(dve, rows_sent[q], 16 * NT * turn)
                nc.vector.tensor_copy(dest[q][:], dest_f[:]).then_inc(S_["dest_ready"], 1)

            steps = [0]

            def then(ins):
                steps[0] += 1
                ins.then_inc(S_["table_step"], 1)
                dve.wait_ge(S_["table_step"], steps[0])

            def list_tiles(round_up):
                then(nc.vector.scalar_tensor_tensor(count[:], e_iota[0:1, 0, :], -float(REG), run[0:1, :],
                                                    ALU.mult, ALU.add))
                then(nc.vector.tensor_scalar(tiles_i[:], count[:], float(round_up), None, ALU.add))
                then(nc.vector.tensor_scalar(tiles_s[:], tiles_i[:], P.bit_length() - 1, None, ALU.arith_shift_right))
                then(nc.vector.tensor_copy(tiles_f[:], tiles_s[:]))
                then(nc.vector.tensor_tensor(tiles_f[:], tiles_f[:], taken[:, 0:E], ALU.subtract))
                then(nc.vector.tensor_tensor_scan(cum[:], tiles_f[:], zeros[:], 0.0, ALU.add, ALU.add))

            def list_gaps():
                then(nc.vector.tensor_tensor(shift[:], taken[:, 1:], taken[:, 0:E], ALU.subtract))
                then(nc.vector.tensor_tensor(shift[:], shift[:], tiles_f[:], ALU.subtract))
                then(nc.vector.tensor_scalar(gap[:], shift[:], float(P), float(REG), ALU.mult, ALU.add))

            def slot_experts(first, n):
                wide = [1, n, E]
                then(nc.vector.tensor_tensor(past[:, 0:n], slot_iota[:, 0:n].unsqueeze(2).to_broadcast(wide),
                                             cum[:].unsqueeze(1).to_broadcast(wide), ALU.is_ge))
                then(nc.vector.tensor_reduce(slot_e[:, 0:n], past[:, 0:n], AX.X, ALU.add))
                nc.vector.tensor_scalar(slot_expert[:, first:first + n], slot_e[:, 0:n], float(E - 1), float(D * KD),
                                        ALU.min, ALU.mult).then_inc(S_["expert_table"], 1)

            def slot_rows(first, n):
                wide = [1, n, E]
                then(nc.vector.tensor_tensor(past_gap[:, 0:n], past[:, 0:n],
                                             gap[:].unsqueeze(1).to_broadcast(wide), ALU.mult))
                then(nc.vector.tensor_reduce(slot_r[:, 0:n], past_gap[:, 0:n], AX.X, ALU.add))
                then(nc.vector.tensor_scalar(slot_at[:, 0:n], slot_iota[:, 0:n], taken[:, 0:1], None, ALU.add))
                then(nc.vector.scalar_tensor_tensor(slot_r2[:, 0:n], slot_at[:, 0:n], float(P), slot_r[:, 0:n],
                                                    ALU.mult, ALU.add))
                nc.vector.tensor_scalar(slot_row[:, first:first + n], slot_r2[:, 0:n], float(DUMMY), None, ALU.min
                                        ).then_inc(S_["row_table"], 1)

            def take_first():
                then(nc.vector.tensor_scalar(upto[:], cum[:], float(FIRST), None, ALU.min))
                then(nc.vector.tensor_tensor(before[:], cum[:], tiles_f[:], ALU.subtract))
                then(nc.vector.tensor_scalar(before[:], before[:], float(FIRST), None, ALU.min))
                then(nc.vector.tensor_tensor(taken[:, 0:E], upto[:], before[:], ALU.subtract))

            def body(b, q, turn):
                tail = not (isinstance(b, int) and b == 0)
                ahead = not (isinstance(b, int) and b == LASTB)
                old, oldq, oldturn = b - 1, 1 - q, turn - (1 - q)
                for i in range(NT):
                    dve.wait_ge(S_["xT_hi"], NT * b + i + 1)
                    nc.vector.tensor_tensor(xT[1][:, :, i * P:(i + 1) * P], by_block(XT_BANKS[i]),
                                            xT[0][:, :, i * P:(i + 1) * P].bitcast(f32), ALU.subtract
                                            ).then_inc(S_["xT_lo"], 1)
                if tail:
                    gated(old)
                else:
                    prep(1)
                    dve.wait_ge(S_["bias_loaded"], 48)
                    nc.vector.tensor_tensor(bias_y[:], bias_y[:], bias_c[:], ALU.add).then_inc(S_["bias_sum"], 1)
                if ahead and tail:
                    ln1_stats(b + 1, 0)
                    ln1_stats(b + 1, 1)
                for m in range(KH):
                    dve.wait_ge(S_["s1_sig"], KH * b + m + 1)
                    nc.vector.scalar_tensor_tensor(silu[:, m, :], (TP, G)[m][:], b1[:, m:m + 1], silu[:, m, :],
                                                   ALU.add, ALU.mult).then_inc(S_["silu_ready"], 1)
                    if tail:
                        ln2_stats(old, oldq, 2 * m)
                    else:
                        prep(2 + m)
                    dve.wait_ge(S_["silu_hi"], KH * b + m + 1)
                    nc.vector.tensor_tensor(sT[1][:, m, :], silu[:, m, :], sT[0][:, m, :].bitcast(f32),
                                            ALU.subtract).then_inc(S_["silu_lo"], 1)
                    if tail:
                        ln2_stats(old, oldq, 2 * m + 1)
                if tail:
                    ln2_mv(old)
                else:
                    prep(2 + KH)
                    powers_lo()
                if ahead and tail:
                    ln1_stats(b + 1, 2)
                    ln1_stats(b + 1, 3)
                if tail:
                    normalise2(old, oldq, 0, 1)
                dve.wait_ge(S_["sel_ready"], b + 1)
                dve.wait_ge(S_["bt_psum"], b + 1)
                for n in range(NB):
                    cols = slice(n * SB, (n + 1) * SB)
                    ins = nc.vector.scalar_tensor_tensor(
                        z[:, :, :, n].rearrange("p j c -> p c j"), SA[:, cols].rearrange("p (c j) -> p c j", j=J),
                        bB[:], sel[:, cols].rearrange("p (c j) -> p c j", j=J), ALU.add, ALU.mult)
                if tail:
                    ins.then_inc(S_["u_ready"], 1)
                    dve.wait_ge(S_["u_ready"], b)
                    dve.wait_ge(S_["carry_ready"], b)
                    ins = nc.vector.tensor_tensor(z[:, 0, 0, :], z[:, 0, 0, :], carried[:], ALU.add)
                ins.then_inc(S_["scan_sum"], 1)
                split(zp[0][:], zp[1][:], first_of, NSTEP * b + 1)
                if tail:
                    normalise2(old, oldq, 1, 2)
                    tail_lo(old, 0)
                else:
                    ln1_stats(b + 1, 0)
                    ln1_stats(b + 1, 1)
                to_pairs(b)
                if tail:
                    normalise2(old, oldq, 2, 3)
                else:
                    ln1_stats(b + 1, 2)
                    ln1_stats(b + 1, 3)
                to_chunks(b)
                if tail:
                    tail_lo(old, 1)
                over(b, 0)
                gate_sum(b, 0)
                over(b, 1)
                if tail:
                    tail_lo(old, 2)
                    normalise2(old, oldq, 3, 4)
                over(b, 2)
                if ahead:
                    ln1_mv(b + 1)
                else:
                    list_tiles(0)
                over(b, 3)
                if tail:
                    tail_lo(old, 3)
                over(b, 4)
                gate_sum(b, 1)
                if ahead:
                    normalise1(b + 1, 0, 1)
                else:
                    list_gaps()
                over(b, 5)
                if ahead:
                    normalise1(b + 1, 1, 2)
                else:
                    slot_experts(0, FIRST)
                to_middles(b)
                gate_sum(b, 2)
                dve.wait_ge(S_["down_psum"], b + 1)
                nc.vector.tensor_copy(carried[:], SA[:, CW - NB:CW]).then_inc(S_["carry_ready"], 1)
                nc.vector.tensor_tensor(first_of[:, NB:], SA[:, 0:CW - NB], first_of[:, NB:], ALU.add
                                        ).then_inc(S_["h_sum"], 1)
                if tail:
                    choose(old)
                if ahead:
                    normalise1(b + 1, 2, NT)
                    if tail:
                        place(old, oldq, oldturn)
                    gate_sum(b, 3)
                dve.wait_ge(S_["h_hi"], b + 1)
                nc.vector.tensor_tensor(token_order(hT[1]), z[:], token_order(hT[0]).bitcast(f32), ALU.subtract
                                        ).then_inc(S_["h_lo"], 1)
                if not ahead:
                    gate_sum(b, 3)
                    place(old, oldq, oldturn)

            dve.wait_ge(S_["cols_loaded"], 16 * (KH + 2))
            dve.wait_ge(S_["consts2_made"], 4)
            for b in range(3):
                body(b, b % 2, b // 2)
            with dve.Fori(1, NBLK // 2 - 1) as t:
                body(t * 2 + 1, 1, t)
                body(t * 2 + 2, 0, t + 1)
            body(LASTB, 1, NBLK // 2 - 1)

            def experts(first, end):
                for n in filter(lambda n: not by_pool(n), range(first, end)):
                    dve.wait_ge(S_["expert_hi"], n + 1)
                    nc.vector.tensor_tensor(We[1][:, n // KD, n % KD, :], EBANKS[n % NEB][:],
                                            We[0][:, n // KD, n % KD, :].bitcast(f32), ALU.subtract
                                            ).then_inc(S_["expert_lo"], 1)

            gated(LASTB)
            for i in range(NT):
                dve.wait_ge(S_["biased"], NT * LASTB + i + 1)
                dve.wait_ge(S_["yg_ready"], NT * LASTB + i + 1)
                nc.vector.tensor_tensor(xrow[1][:, i, 0:D], xrow[1][:, i, 0:D], gate[:, i, :], ALU.add
                                        ).then_inc(S_["x1_ready"], 1)
            for i in range(NT):
                ln2_stats(LASTB, 1, i)
            ln2_mv(LASTB)
            experts(0, E_STEPS[0])
            normalise2(LASTB, 1)
            for pair in range(2):
                tail_lo(LASTB, 2 * pair)
                tail_lo(LASTB, 2 * pair + 1)
                if pair == 0:
                    slot_rows(0, FIRST)
                experts(E_STEPS[pair], E_STEPS[pair + 1])
            choose(LASTB)
            place(LASTB, 1, NBLK // 2 - 1)
            dve.wait_ge(S_["run_ready"], NBLK)
            nc.vector.tensor_copy(end_rows[:], run[0:1, :]).then_inc(S_["ends_ready"], 1)
            def slot_norm(s, m, turn):
                dve.wait_ge(row_loaded[m], 16 * (turn + 1))
                wait(dve, S_["slot_turned"], s - M + 1)
                wait(dve, S_["slot_base"], s - M + 1)
                nc.vector.tensor_scalar(rnorm[m], rows[m][:, 0:D], rows[m][:, MEAN:MEAN + 1],
                                        rows[m][:, RSTD:RSTD + 1], ALU.subtract, ALU.mult
                                        ).then_inc(S_["slot_norm"], 1)

            def slot_lo(s, q):
                dve.wait_ge(S_["slot_hi"], s + 1)
                hi, lo = [h[:, :, q * P:(q + 1) * P] for h in x2T]
                nc.vector.tensor_tensor(lo, by_block((TP, SC)[q]), hi.bitcast(f32), ALU.subtract).then_inc(S_["slot_lo"], 1)

            def slot_sum(s, m, turn):
                dve.wait_ge(S_["slot_psum"], s + 1)
                dve.wait_ge(S_["slot_base"], s + 1)
                wait(dve, out_sent[m], 16 * turn)
                nc.vector.tensor_tensor(res[m], Y[m % 2][:], rows[m][:, 0:D], ALU.add).then_inc(S_["slot_result"], 1)

            def slot(s, m, turn):
                slot_lo(s, m % 2)
                if not (isinstance(s, int) and s == SLOTS - 1):
                    slot_norm(s + 1, (m + 1) % M, turn + (m + 1) // M)
                if not (isinstance(s, int) and s == 0):
                    slot_sum(s - 1, (m - 1) % M, turn - (m == 0))

            slot_norm(0, 0, 0)
            experts(E_STEPS[2], E_STEPS[5])
            slot(0, 0, 0)
            experts(E_STEPS[5], NE)
            for s in range(1, 2 * M):
                slot(s, s % M, s // M)
                if s == 1:
                    take_first()
                elif s == 2:
                    list_tiles(P - 1)
                elif s == 3:
                    list_gaps()
                elif s == 4:
                    slot_experts(FIRST, SLOTS - FIRST)
                elif s == 6:
                    slot_rows(FIRST, SLOTS - FIRST)
            with dve.Fori(2, FULL) as u:
                for m in range(M):
                    slot(u * M + m, m, u)
            for s in range(FULL * M, SLOTS):
                slot(s, s % M, FULL)
            slot_sum(SLOTS - 1, (SLOTS - 1) % M, (SLOTS - 1) // M)

        @block.tensor
        def _(pe):
            def mm3(dst, left, right, first=True, last=True):
                nc.tensor.matmul(dst, left[0], right[0], start=first, stop=False)
                nc.tensor.matmul(dst, left[0], right[1], start=False, stop=False)
                return nc.tensor.matmul(dst, left[1], right[0], start=False, stop=last)

            pe.wait_ge(S_["ident_made"], 1)
            pe.wait_ge(S_["A_loaded"], 16)

            def prep(stage):
                for what, n in STAGES[stage]:
                    if what == "pow":
                        wait(pe, S_["pow_copied"], COPIED[n])
                        for i, (side, k, a, m) in enumerate(ROUNDS[n]):
                            dst = POW_BANK[:, i * NS:(i + 1) * NS]
                            if a == 0:
                                ins = nc.tensor.transpose(dst, raw_A, ident[:])
                            elif side == "T":
                                ins = nc.tensor.matmul(dst, pslot(a), tslot(m), start=True, stop=True)
                            else:
                                ins = nc.tensor.matmul(dst, tslot(a), pslot(m), start=True, stop=True)
                        ins.then_inc(S_["pow_psum"], 1)
                    else:
                        pe.wait_ge(*JOB_LOAD[n])
                        if n >= len(PREP_BANKS):
                            pe.wait_ge(S_["w_lo"], n + 1 - len(PREP_BANKS))
                        for src, at, rows_in in JOBS[n][0]:
                            ins = nc.tensor.transpose(PREP_BANKS[n % len(PREP_BANKS)][:, at:at + rows_in], src,
                                                      ident[0:rows_in, 0:rows_in])
                        ins.then_inc(S_["w_turned"], 1)

            prep(0)
            pe.wait_ge(S_["consts2_made"], 4)

            def dense(dst, i, w, ks, closed):
                for k in ks:
                    ins = mm3(dst[:], [h[:, k, i * P:(i + 1) * P] for h in xT], [h[:, k, :] for h in w],
                              first=(k == 0), last=closed and k == KD - 1)
                return ins

            def gates(b, i, *ks):
                if 0 in ks and i > 0:
                    pe.wait_ge(S_["g_sum"], NT * b + i)
                ins = dense(G, i, GwT, ks, True)
                if KD - 1 in ks:
                    ins.then_inc(S_["g_psum"], 1)

            def y_dense(b, i, *ks):
                if 0 in ks:
                    wait(pe, S_["yg_ready"], NT * (b - 1) + i + 1)
                dense(Y[i], i, DwT, ks, False)

            def y_state(b):
                pe.wait_ge(S_["h_lo"], b + 1)
                for i in range(NT):
                    mm3(Y[i][:], [h[:, i * P:(i + 1) * P] for h in hT], [h[:] for h in CwT], first=False
                        ).then_inc(S_["y_psum"], 1)

            def tail_turn(b, i):
                pe.wait_ge(S_["xn2_ready"], NT * b + i + 1)
                bank = turn_bank(b, i)
                if i > 0 and turn_bank(b, i - 1) is bank:
                    pe.wait_ge(S_["x2T_lo"], NT * b + i)
                elif i > 1:
                    pe.wait_ge(S_["x2T_lo"], NT * b + i - 1)
                for k in range(KD):
                    ins = nc.tensor.transpose(bank[:, k * P:(k + 1) * P], xn2[:, i, k * P:(k + 1) * P], ident[:])
                ins.then_inc(S_["x2T_psum"], 1)

            def tail_scores(b, pair):
                pe.wait_ge(S_["x2T_lo"], NT * b + 2 * pair + 2)
                hi, lo = x2T
                for k in range(KD):
                    if k == KD - 1:
                        for kl in range(KD):
                            nc.tensor.matmul(SC[0:E, SC_TURN:], gateT[:, kl, 0, :], lo[:, kl, :], start=False, stop=False)
                    ins = nc.tensor.matmul(SC[0:2 * E, SC_TURN:], gateT[:, k].rearrange("p h e -> p (h e)"), hi[:, k, :],
                                           start=(k == 0), stop=(k == KD - 1))
                ins.then_inc(S_["scoresT_psum"], 1)

            def tail_back(b, pair):
                counted_waits(pe, (S_["scoresT_ready"], 2 * b + pair + 1))
                for i in range(2):
                    at = (2 * pair + i) * 2 * E
                    ins = nc.tensor.transpose(SC[:, at:at + 2 * E], scT[:, i * P:(i + 1) * P], ident[0:2 * E, 0:2 * E])
                ins.then_inc(S_["scores_psum"], 1)

            def tail_ranks(b):
                pe.wait_ge(S_["onehot_ready"], b + 1)
                nc.tensor.matmul(SC[:, SC_RANK:SC_COUNT + E], tri[:], onehot[:].rearrange("p t e -> p (t e)"),
                                 start=True, stop=False)
                for i in range(1, NT + 1):
                    ins = nc.tensor.matmul(SC[:, SC_RANK + i * E:SC_COUNT + E], ones[:],
                                           onehot[:, 0:NT + 1 - i, :].rearrange("p t e -> p (t e)"),
                                           start=False, stop=(i == NT))
                ins.then_inc(S_["rank_psum"], 1)

            def power(k):
                return [h[:, POWERS.index(k), :] for h in AT]

            def pairs(b, step, counted):
                pe.wait_ge(S_["scan_lo"], NSTEP * b + step)
                mm3(SA[:, 0:CW], power(1), [h[:] for h in zp]).then_inc(counted, 1)

            def chunks(b, step, k, o):
                pe.wait_ge(S_["scan_lo"], NSTEP * b + step)
                before = endp[:, 0:CH - o].rearrange("p c h n -> p (c h n)")
                for h, a in enumerate(power(k)):
                    ins = nc.tensor.matmul(SA[:, 0:2 * (CH - o) * NB], a, before, start=(h == 0), stop=(h == 1))
                ins.then_inc(S_["scan_psum"], 1)

            def to_pairs(b):
                pairs(b, 1, S_["scan_psum"])

            def to_chunks(b):
                chunks(b, 2, J, 0)

            def over(b, l):
                chunks(b, 3 + l, CHUNK * LEVELS[l], LEVELS[l])

            def to_middles(b):
                chunks(b, NSTEP - 1, J, 1)

            def down(b):
                pairs(b, NSTEP, S_["down_psum"])

            def body(b):
                tail = not (isinstance(b, int) and b == 0)
                free = ((S_["h_sum"], b), (S_["x2T_lo"], NT * (b - 1)), (S_["run_ready"], b - 1), (S_["g_sum"], NT * b))
                for i in range(NT):
                    pe.wait_ge(S_["xn_ready"], NT * b + i + 1)
                    wait(pe, *free[i])
                    for k in range(KD):
                        ins = nc.tensor.transpose(XT_BANKS[i][:, k * P:(k + 1) * P],
                                                  xn[:, i, k * P:(k + 1) * P], ident[:])
                    ins.then_inc(S_["xT_psum"], 1)
                if tail:
                    y_state(b - 1)
                else:
                    prep(1)
                    pe.wait_ge(S_["w_lo"], KD + 2)
                pe.wait_ge(S_["xT_lo"], NT * b + 2)
                for m in range(KH):
                    pe.wait_ge(S_["xT_hi"], NT * (b + 1))
                    for k in range(KD):
                        for h in s1T:
                            nc.tensor.matmul((TP, G)[m][:], h[:, k, m * P:(m + 1) * P], xT[0][:, k, :],
                                             start=(k == 0 and h is s1T[0]), stop=False)
                    pe.wait_ge(S_["xT_lo"], NT * (b + 1))
                    for k in range(KD):
                        ins = nc.tensor.matmul((TP, G)[m][:], s1T[0][:, k, m * P:(m + 1) * P], xT[1][:, k, :],
                                               start=False, stop=(k == KD - 1))
                    ins.then_inc(S_["s1_psum"], 1)
                    if not tail:
                        prep(2 + m)
                for k in range(KD):
                    ins = mm3(SA[:], [h[:, k, :] for h in BwT], [h[:, k, :] for h in xT],
                              first=(k == 0), last=(k == KD - 1))
                ins.then_inc(S_["bt_psum"], 1)
                if not tail:
                    prep(2 + KH)
                    pe.wait_ge(S_["w_lo"], len(JOBS))
                    pe.wait_ge(S_["pow_copied"], COPIED[-1])
                y_dense(b, 0, 0, 1)
                pe.wait_ge(S_["silu_lo"], KH * (b + 1))
                for m in range(KH):
                    ins = mm3(SC[:], [h[:, m, :] for h in s2T], [h[:, m, :] for h in sT],
                              first=(m == 0), last=(m == KH - 1))
                ins.then_inc(S_["s2_psum"], 1)
                y_dense(b, 0, 2, 3)
                y_dense(b, 1, 0, 1)
                if tail:
                    tail_turn(b - 1, 0)
                y_dense(b, 1, 2)
                if isinstance(b, int) and b == 0:
                    pe.wait_ge(S_["pow_lo"], 1)
                to_pairs(b)
                y_dense(b, 1, 3)
                gates(b, 0, 0)
                if tail:
                    tail_turn(b - 1, 1)
                to_chunks(b)
                gates(b, 0, 1, 2, 3)
                over(b, 0)
                y_dense(b, 2, 0)
                if tail:
                    tail_scores(b - 1, 0)
                over(b, 1)
                if tail:
                    tail_turn(b - 1, 2)
                y_dense(b, 2, 1, 2)
                over(b, 2)
                y_dense(b, 2, 3)
                if tail:
                    tail_back(b - 1, 0)
                gates(b, 1, 0, 1)
                over(b, 3)
                if tail:
                    tail_turn(b - 1, 3)
                gates(b, 1, 2, 3)
                over(b, 4)
                y_dense(b, 3, 0)
                if tail:
                    tail_scores(b - 1, 1)
                over(b, 5)
                y_dense(b, 3, 1, 2)
                if tail:
                    tail_back(b - 1, 1)
                gates(b, 2, 0)
                to_middles(b)
                gates(b, 2, 1, 2, 3)
                down(b)
                y_dense(b, 3, 3)
                gates(b, 3, 0, 1, 2)
                if tail:
                    tail_ranks(b - 1)
                gates(b, 3, 3)

            body(0)
            body(1)
            with pe.Fori(2, NBLK) as b:
                body(b)

            def experts(first, end):
                for n in range(first, end):
                    e, k = n // KD, n % KD
                    pe.wait_ge(raw_loaded[e % RING], RAW_NEED[e % RING] + 16 * (e // RING + 1))
                    if n < NEB:
                        pe.wait_ge(*((S_["g_sum"], NT * NBLK), (S_["yg_ready"], NT * LASTB + n))[min(n, 1)])
                    elif n == NEB:
                        pe.wait_ge(S_["biased"], NT * NBLK)
                    if n >= NEB and by_pool(n - NEB):
                        pe.wait_ge(S_["expert_full"], pool_count(n - NEB) + 1)
                    elif n >= NEB:
                        pe.wait_ge(S_["expert_lo"], dve_count(n - NEB) + 1)
                    for f in range(KD):
                        ins = nc.tensor.transpose(EBANKS[n % NEB][:, f * P:(f + 1) * P],
                                                  raw[:, e % RING, f, k * P:(k + 1) * P], ident[:])
                    ins.then_inc(S_["expert_turned"], 1)

            y_state(LASTB)
            experts(0, E_STEPS[0])
            tail_turn(LASTB, 0)
            tail_turn(LASTB, 1)
            experts(E_STEPS[0], E_STEPS[1])
            tail_scores(LASTB, 0)
            tail_turn(LASTB, 2)
            tail_turn(LASTB, 3)
            tail_back(LASTB, 0)
            experts(E_STEPS[1], E_STEPS[2])
            tail_scores(LASTB, 1)
            experts(E_STEPS[2], E_STEPS[3])
            tail_back(LASTB, 1)
            experts(E_STEPS[3], E_STEPS[4])
            tail_ranks(LASTB)
            experts(E_STEPS[4], E_STEPS[5])
            flat = [h[:].rearrange("p e k f -> p (e k f)") for h in We]

            def slot_turn(s, m):
                bank = (TP, SC)[m % 2]
                pe.wait_ge(S_["slot_norm"], s + 1)
                wait(pe, S_["slot_lo"], s - 1)
                for k in range(KD):
                    ins = nc.tensor.transpose(bank[:, k * P:(k + 1) * P], rnorm[m][:, k * P:(k + 1) * P], ident[:])
                ins.then_inc(S_["slot_turned"], 1)

            def slot_product(s, m):
                first = pe.value_load(slot_expert[0:1, bass.ds(s, 1)], min_val=0, max_val=(E - 1) * KD * D)
                pe.wait_ge(S_["slot_lo"], s + 1)
                wait(pe, S_["slot_result"], s - 1)
                for k in range(KD):
                    for a, w in ((0, 0), (0, 1), (1, 0)):
                        ins = nc.tensor.matmul(Y[m % 2][:], x2T[a][:, k, m % 2 * P:(m % 2 + 1) * P], flat[w][:, bass.ds(first + k * D, D)],
                                               start=(k == 0 and a == 0 and w == 0), stop=(k == KD - 1 and a == 1))
                ins.then_inc(S_["slot_psum"], 1)

            def slot(s, m):
                slot_turn(s, m)
                if not (isinstance(s, int) and s == 0):
                    slot_product(s - 1, (m - 1) % M)

            pe.wait_ge(S_["run_ready"], NBLK)
            slot(0, 0)
            experts(E_STEPS[5], NE)
            slot_turn(1, 1)
            pe.wait_ge(S_["expert_lo"], dve_count(NE))
            pe.wait_ge(S_["expert_lo_pool"], pool_count(NE))
            pe.wait_ge(S_["expert_table"], 1)
            slot_product(0, 0)
            for m in range(2, M):
                slot(m, m)
            with pe.Fori(1, EARLY) as u:
                for m in range(M):
                    slot(u * M + m, m)
            pe.wait_ge(S_["expert_table"], 2)
            with pe.Fori(EARLY, FULL) as u:
                for m in range(M):
                    slot(u * M + m, m)
            for s in range(FULL * M, SLOTS):
                slot(s, s % M)
            slot_product(SLOTS - 1, (SLOTS - 1) % M)


_INS = ["x", "A", "B_w", "B_b", "C_w", "C_b", "D_w", "D_b", "s_w1", "s_b1", "s_w2", "s_b2", "g_w", "g_b"]
_NAMES = ["L0_attn_" + n for n in _INS] + ["L0_ffn_gate_w", "L0_ffn_expert_w"]


def kernel(**inputs):
    import numpy as np
    import concourse.bacc as bacc
    from concourse.bass_utils import run_bass_kernel_spmd

    nc = bacc.Bacc("TRN2", target_bir_lowering=False, num_devices=1)
    arrays, args = {}, []
    for name in _NAMES:
        a = np.ascontiguousarray(inputs[name])
        arrays[name] = a
        args.append(nc.dram_tensor(name, a.shape, mybir.dt.from_np(a.dtype), kind="ExternalInput").ap())
    shape = arrays["L0_attn_x"].shape
    args.append(nc.dram_tensor("out", shape, mybir.dt.float32, kind="ExternalOutput").ap())
    preln_ssm_moe_kernel(nc, *args)
    r = run_bass_kernel_spmd(nc, [arrays], core_ids=[0])
    return r.results[0]["out"]
```
